# Optimizing a Trainium2 kernel written in Bass

```python
import numpy as np
import jax
import jax.numpy as jnp

def _softmax(x, axis=-1):
    return jax.nn.softmax(x, axis=axis)

def _gelu(x):
    return jax.nn.gelu(x, approximate=True)

def _silu(x):
    return jax.nn.silu(x)

def _sigmoid(x):
    return jax.nn.sigmoid(x)

def _layernorm(x, axis=-1, eps=1e-05):
    m = jnp.mean(x, axis=axis, keepdims=True)
    v = jnp.var(x, axis=axis, keepdims=True)
    return (x - m) / jnp.sqrt(v + eps)

def _scatter_add(tgt, idx, src, axis=0):
    return tgt.at[idx].add(src)

def _segment_sum(src, seg, n):
    return jax.ops.segment_sum(src, seg, n)
kernel_name = 'mk_lm_tower_d1_tok_ids1024_r4_ae537c'

def setup_inputs(seed: int=0):
    np.random.seed(seed)
    _w = jnp.asarray

    def _rec_inputs():
        import jax
        import jax.numpy as jnp
        _rk = jax.random.key(seed)
        x = jax.random.randint(jax.random.fold_in(_rk, 1), (2, 2048), 0, 64, jnp.int32)
        return x
    x = _rec_inputs()

    def _L0_tok_setup():
        import jax, jax.numpy as jnp
        import numpy as np
        N_FFT = 64
        HOP = 64
        NUM_FREQ = N_FFT // 2 + 1

        def _stft_mag(sig, window):
            L = sig.shape[1]
            pad = N_FFT // 2
            x = jnp.pad(sig, ((0, 0), (pad, pad)), mode='reflect')
            n_frames = 1 + L // HOP
            idx = jnp.arange(n_frames)[:, None] * HOP + jnp.arange(N_FFT)[None, :]
            frames = x[:, idx] * window
            spec = jnp.fft.rfft(frames, axis=-1)
            r, im = (spec.real, spec.imag)
            m2 = r * r + im * im
            mag = jnp.where(m2 == 0, 0.0, jnp.sqrt(jnp.where(m2 == 0, 1.0, m2)))
            return (mag, n_frames)

        def _linear_interp_last(feat, out_len):
            in_len = feat.shape[-1]
            coord = jnp.clip((jnp.arange(out_len) + 0.5) * (in_len / out_len) - 0.5, 0.0, in_len - 1.0)
            i0 = jnp.floor(coord).astype(jnp.int32)
            i1 = jnp.minimum(i0 + 1, in_len - 1)
            w = (coord - i0).astype(feat.dtype)
            return feat[..., i0] * (1.0 - w) + feat[..., i1] * w
        key = jax.random.key(seed)
        k0, k1, k2 = jax.random.split(key, 3)
        B, L, V, d_model = (2, 256, 64, 256)
        d_emb = int(d_model * 0.7)
        d_stft = d_model - d_emb
        input_ids = jax.random.randint(k0, (B, L), 0, V)
        emb_table = jax.random.normal(k1, (V, d_emb), jnp.float32) * 0.02
        proj_w = jax.random.normal(k2, (d_stft, V * NUM_FREQ), jnp.float32) * 0.02
        proj_b = jnp.zeros((d_stft,), jnp.float32)
        n = jnp.arange(N_FFT, dtype=jnp.float32)
        window = 0.5 * (1.0 - jnp.cos(2.0 * jnp.pi * n / N_FFT))
        return {'input_ids': input_ids, 'emb_table': emb_table, 'proj_w': proj_w, 'proj_b': proj_b, 'window': window}
    _L0_tok_all = _L0_tok_setup()
    _L0_tok_in = {k: v for k, v in _L0_tok_all.items() if k in ('emb_table', 'proj_w', 'proj_b', 'window')}
    del _L0_tok_all

    def _L0_attn_setup():
        import jax, jax.numpy as jnp
        import numpy as np
        H = 256
        W_CTX = 2

        def _local_attention(x, Wq, bq, Wk, bk, Wv, bv):
            B, S, Hd = x.shape
            Q = x @ Wq + bq
            K = x @ Wk + bk
            V = x @ Wv + bv
            w = W_CTX
            win = 2 * w + 1
            idx = jnp.arange(S)[:, None] + jnp.arange(-w, w + 1)[None, :]
            valid = (idx >= 0) & (idx < S)
            idx_c = jnp.clip(idx, 0, S - 1)
            Kw = K[:, idx_c]
            Vw = V[:, idx_c]
            scores = jnp.einsum('bsh,bswh->bsw', Q, Kw) / jnp.sqrt(jnp.float32(Hd))
            scores = jnp.where(valid[None], scores, -jnp.inf)
            probs = jax.nn.softmax(scores, axis=-1)
            return jnp.einsum('bsw,bswh->bsh', probs, Vw)
        key = jax.random.key(seed)
        ks = jax.random.split(key, 7)
        B, S = (4, 512)
        sd = 1.0 / np.sqrt(H)
        inp = {'sequence_output': jax.random.normal(ks[0], (B, S, H), dtype=jnp.float32), 'Wq': jax.random.uniform(ks[1], (H, H), jnp.float32, -sd, sd), 'bq': jax.random.uniform(ks[2], (H,), jnp.float32, -sd, sd), 'Wk': jax.random.uniform(ks[3], (H, H), jnp.float32, -sd, sd), 'bk': jax.random.uniform(ks[4], (H,), jnp.float32, -sd, sd), 'Wv': jax.random.uniform(ks[5], (H, H), jnp.float32, -sd, sd), 'bv': jax.random.uniform(ks[6], (H,), jnp.float32, -sd, sd)}
        return inp
    _L0_attn_all = _L0_attn_setup()
    _L0_attn_in = {k: v for k, v in _L0_attn_all.items() if k in ('Wq', 'bq', 'Wk', 'bk', 'Wv', 'bv')}
    del _L0_attn_all

    def _L0_ffn_setup():
        import math
        import jax, jax.numpy as jnp
        import numpy as np
        E = 8
        K = 2
        CF = 1.25
        D = 256
        F = 512
        B, S = (4, 512)
        key = jax.random.key(seed)
        ks = jax.random.split(key, 8)
        sd = 1.0 / math.sqrt(D)
        sf = 1.0 / math.sqrt(F)
        return {'x': jax.random.normal(ks[0], (B, S, D), jnp.float32), 'router_w': jax.random.normal(ks[1], (D, E), jnp.float32) * sd, 'router_b': jnp.zeros((E,), jnp.float32), 'w1': jax.random.normal(ks[2], (E, D, F), jnp.float32) * sd, 'b1': jax.random.normal(ks[3], (E, F), jnp.float32) * 0.01, 'w2': jax.random.normal(ks[4], (E, F, D), jnp.float32) * sf, 'b2': jax.random.normal(ks[5], (E, D), jnp.float32) * 0.01}
    _L0_ffn_all = _L0_ffn_setup()
    _L0_ffn_in = {k: v for k, v in _L0_ffn_all.items() if k in ('router_w', 'router_b', 'w1', 'b1', 'w2', 'b2')}
    del _L0_ffn_all
    return {'x': x, 'L0_tok_emb_table': _L0_tok_in['emb_table'], 'L0_tok_proj_w': _L0_tok_in['proj_w'], 'L0_tok_proj_b': _L0_tok_in['proj_b'], 'L0_tok_window': _L0_tok_in['window'], 'L0_attn_Wq': _L0_attn_in['Wq'], 'L0_attn_bq': _L0_attn_in['bq'], 'L0_attn_Wk': _L0_attn_in['Wk'], 'L0_attn_bk': _L0_attn_in['bk'], 'L0_attn_Wv': _L0_attn_in['Wv'], 'L0_attn_bv': _L0_attn_in['bv'], 'L0_ffn_router_w': _L0_ffn_in['router_w'], 'L0_ffn_router_b': _L0_ffn_in['router_b'], 'L0_ffn_w1': _L0_ffn_in['w1'], 'L0_ffn_b1': _L0_ffn_in['b1'], 'L0_ffn_w2': _L0_ffn_in['w2'], 'L0_ffn_b2': _L0_ffn_in['b2']}

def reference(x, L0_tok_emb_table, L0_tok_proj_w, L0_tok_proj_b, L0_tok_window, L0_attn_Wq, L0_attn_bq, L0_attn_Wk, L0_attn_bk, L0_attn_Wv, L0_attn_bv, L0_ffn_router_w, L0_ffn_router_b, L0_ffn_w1, L0_ffn_b1, L0_ffn_w2, L0_ffn_b2):
    import jax
    import jax.numpy as jnp

    def _L0_tok_ref(input_ids, emb_table, proj_w, proj_b, window):
        import jax, jax.numpy as jnp
        import numpy as np
        N_FFT = 64
        HOP = 64
        NUM_FREQ = N_FFT // 2 + 1

        def _stft_mag(sig, window):
            L = sig.shape[1]
            pad = N_FFT // 2
            x = jnp.pad(sig, ((0, 0), (pad, pad)), mode='reflect')
            n_frames = 1 + L // HOP
            idx = jnp.arange(n_frames)[:, None] * HOP + jnp.arange(N_FFT)[None, :]
            frames = x[:, idx] * window
            spec = jnp.fft.rfft(frames, axis=-1)
            r, im = (spec.real, spec.imag)
            m2 = r * r + im * im
            mag = jnp.where(m2 == 0, 0.0, jnp.sqrt(jnp.where(m2 == 0, 1.0, m2)))
            return (mag, n_frames)

        def _linear_interp_last(feat, out_len):
            in_len = feat.shape[-1]
            coord = jnp.clip((jnp.arange(out_len) + 0.5) * (in_len / out_len) - 0.5, 0.0, in_len - 1.0)
            i0 = jnp.floor(coord).astype(jnp.int32)
            i1 = jnp.minimum(i0 + 1, in_len - 1)
            w = (coord - i0).astype(feat.dtype)
            return feat[..., i0] * (1.0 - w) + feat[..., i1] * w
        B, L = input_ids.shape
        V = emb_table.shape[0]
        word_embeds = emb_table[input_ids]
        sig = jax.nn.one_hot(input_ids, V, dtype=jnp.float32)
        sig = jnp.transpose(sig, (0, 2, 1)).reshape(B * V, L)
        mag, T = _stft_mag(sig, window)
        feat = mag.reshape(B, V, T, NUM_FREQ).transpose(0, 3, 1, 2)
        feat = feat.reshape(B, NUM_FREQ * V, T)
        up = _linear_interp_last(feat, L)
        stft_feat = jnp.transpose(up, (0, 2, 1))
        stft_enc = stft_feat @ proj_w.T + proj_b
        return jnp.concatenate([word_embeds, stft_enc], axis=-1)

    def _L0_attn_ref(sequence_output, Wq, bq, Wk, bk, Wv, bv):
        import jax, jax.numpy as jnp
        import numpy as np
        H = 256
        W_CTX = 2

        def _local_attention(x, Wq, bq, Wk, bk, Wv, bv):
            B, S, Hd = x.shape
            Q = x @ Wq + bq
            K = x @ Wk + bk
            V = x @ Wv + bv
            w = W_CTX
            win = 2 * w + 1
            idx = jnp.arange(S)[:, None] + jnp.arange(-w, w + 1)[None, :]
            valid = (idx >= 0) & (idx < S)
            idx_c = jnp.clip(idx, 0, S - 1)
            Kw = K[:, idx_c]
            Vw = V[:, idx_c]
            scores = jnp.einsum('bsh,bswh->bsw', Q, Kw) / jnp.sqrt(jnp.float32(Hd))
            scores = jnp.where(valid[None], scores, -jnp.inf)
            probs = jax.nn.softmax(scores, axis=-1)
            return jnp.einsum('bsw,bswh->bsh', probs, Vw)
        return _local_attention(sequence_output, Wq, bq, Wk, bk, Wv, bv)

    def _L0_ffn_ref(x, router_w, router_b, w1, b1, w2, b2):
        import math
        import jax, jax.numpy as jnp
        import numpy as np
        E = 8
        K = 2
        CF = 1.25
        D = 256
        F = 512
        B, S = (4, 512)
        b, s, d = x.shape
        xf = x.reshape(-1, d)
        T = b * s
        A = T * K
        cap = max(1, int(math.ceil(CF * A / E)))
        logits = xf @ router_w + router_b
        probs = jax.nn.softmax(logits, axis=-1)
        topk_p, topk_i = jax.lax.top_k(probs, K)
        topk_p = topk_p / jnp.clip(topk_p.sum(-1, keepdims=True), 1e-09)
        a_tok = jnp.repeat(jnp.arange(T), K)
        a_exp = topk_i.reshape(-1)
        a_w = topk_p.reshape(-1)
        order = jnp.argsort(a_exp)
        se, st, sw = (a_exp[order], a_tok[order], a_w[order])
        counts = jnp.bincount(se, length=E)
        starts = jnp.cumsum(counts) - counts
        rank = jnp.arange(A) - starts[se]
        keep = rank < cap
        slot = jnp.where(keep, se * cap + rank, E * cap)
        buf = jnp.zeros((E * cap + 1, d), x.dtype).at[slot].set(xf[st])
        buf = buf[:-1].reshape(E, cap, d)
        h = jax.nn.gelu(jnp.einsum('ecd,edf->ecf', buf, w1) + b1[:, None, :], approximate=False)
        eo = jnp.einsum('ecf,efd->ecd', h, w2) + b2[:, None, :]
        eo_flat = jnp.concatenate([eo.reshape(E * cap, d), jnp.zeros((1, d), x.dtype)], axis=0)
        w = jnp.where(keep, sw, 0.0)[:, None]
        out = jnp.zeros_like(xf).at[st].add(eo_flat[slot] * w)
        return out.reshape(b, s, d)
    h = _L0_tok_ref(x, L0_tok_emb_table, L0_tok_proj_w, L0_tok_proj_b, L0_tok_window)
    h = h + _L0_attn_ref(_layernorm(h, axis=-1), L0_attn_Wq, L0_attn_bq, L0_attn_Wk, L0_attn_bk, L0_attn_Wv, L0_attn_bv)
    h = h + _L0_ffn_ref(_layernorm(h, axis=-1), L0_ffn_router_w, L0_ffn_router_b, L0_ffn_w1, L0_ffn_b1, L0_ffn_w2, L0_ffn_b2)
    return h

_drawn_inputs = setup_inputs


def setup_inputs(seed=0):
    import zlib

    import numpy as np

    out = dict(_drawn_inputs(seed))
    spreads = {'L0_tok_proj_b': (0.0, 0.1), 'L0_ffn_router_b': (0.0, 0.1)}
    factors = {'L0_attn_Wq': 8.0,
     'L0_attn_bq': 38.272,
     'L0_attn_Wk': 8.0,
     'L0_attn_bk': 64.0,
     'L0_ffn_b1': 8.0,
     'L0_ffn_b2': 7.482}
    for name, (base, spread) in spreads.items():
        noise = np.random.default_rng([zlib.crc32(name.encode()), seed]).standard_normal(out[name].shape)
        drawn = base * np.exp(spread * noise) if base else spread * noise
        out[name] = jnp.asarray(drawn.astype(out[name].dtype))
    for name, factor in factors.items():
        out[name] = (out[name] * factor).astype(out[name].dtype)
    return out
```

```python
from contextlib import ExitStack

import numpy as np
import concourse.bass as bass
from concourse import mybir

ALU = mybir.AluOpType
ACT = mybir.ActivationFunctionType
AX = mybir.AxisListType
F32 = mybir.dt.float32
F16 = mybir.dt.float16
BF16 = mybir.dt.bfloat16
I32 = mybir.dt.int32

P = 128
B, L = 2, 2048
TOK = B * L
V, NF, FR = 64, 33, 33
H, DE = 256, 179
DS = H - DE
NFP = 17
KZ = V + FR + 1
GRP, NG = 512, TOK // 512
NT = TOK // P
TPG = GRP // P
WCTX = 2
WIN = GRP + 2 * WCTX
KEYS = P + 2 * WCTX
HW = WIN // 2
OW = H + 8 + 1
E, FF = 8, 512
CAP = 1280
ST = CAP // P
HS = ST // 2
HALF = HS * P
CH = HALF // 2
NHALF = 2 * E
FT = FF // P
NV = 5
EPS = 1e-5
DFT_SCALE = 256.0
X_SCALE = 16.0
W_SCALE = 256.0
FRAMES_PER_BANK = 512 // (2 * NFP)

C_DFT = 0
C_IOTA = C_DFT + 4 * NFP
C_PART = C_IOTA + P
C_ID = C_PART + 1
C_TRI = C_ID + P
C_EPS = C_TRI + P
C_SUM = C_EPS + 1
C_ROW97 = C_SUM + KZ
C_TILE = C_ROW97 + KZ
C_TOK = C_TILE + NT
C_RESET = C_TOK + NT
C_PREF = C_RESET + NT
NCONST = C_PREF + E


def wait(eng, sem, value):
    if isinstance(value, int) and value <= 0:
        return
    eng.wait_ge(sem, value)


def wait_apart(eng, sem, value):
    if isinstance(value, int) and value <= 0:
        return
    eng.wait_ge(sem, value)
    if not isinstance(value, int):
        eng.nop(nofuse=True)


def build(nc, ids_frames, ids_win, window, emb, proj_w, proj_b, wq, wk, wv, bqk, bv, wr, br,
          w1, b1, w2, b2, consts, frames_of, masks, out):
    with ExitStack() as ctx:
        def sb(name, shape, dt=F32):
            return ctx.enter_context(nc.sbuf_tensor(name, shape, dt))

        def sem(name):
            return ctx.enter_context(nc.semaphore(name))

        w1s = sb("w1s", [P, 2, E, 2, FF], F16)
        w2s = sb("w2s", [P, 2, E, FT, H], F16)
        b1s = sb("b1s", [P, E, FT])
        b2s = sb("b2s", [2, E, H], F16)
        con = sb("con", [P, NCONST])
        tok_idx = sb("tok_idx", [P, E, ST], I32)
        tok_w = sb("tok_w", [P, E, ST])
        vals = sb("vals", [P, E, NT, NV], BF16)
        pos_lo = sb("pos_lo", [P, E, NT])
        pos_hi = sb("pos_hi", [P, E, NT])
        iota_b = sb("iota_b", [P, P], BF16)
        ident16 = sb("ident16", [P, P], F16)
        notp = sb("notp", [2, 1])
        ones16 = sb("ones16", [2, P], F16)

        reg_h = sb("reg_h", [P, NT * OW])
        reg_z = sb("reg_z", [P, 2 * NG * WIN])
        reg_w = sb("reg_w", [P, 2048])
        reg_a = sb("reg_a", [P, 8192])
        reg_p = sb("reg_p", [P, 2 * TPG * H])

        def carve(region, at, parts, dims, dt=F32, first=0):
            size = {F32: 4, I32: 4, F16: 2, BF16: 2}[dt]
            n = int(np.prod(dims))
            words = (n * size + 3) // 4
            ap = region[first:first + parts, at:at + words]
            if dt != F32:
                ap = ap.bitcast(dt)
            if len(dims) > 1:
                names = [f"d{i}" for i in range(len(dims))]
                ap = ap.rearrange(f"p ({' '.join(names)}) -> p {' '.join(names)}",
                                  **{m: d for m, d in zip(names[1:], dims[1:])})
            return ap

        onehot = carve(reg_h, 0, P, [B * FR, V], F16)
        sq = carve(reg_h, 2112, P, [B * FR, 2, NFP])
        sq_floor = carve(reg_h, 2112, P, [B * FR * NFP])
        m2 = carve(reg_h, 4356, P, [B * FR, NFP])
        root = carve(reg_h, 5478, P, [B * FR, NFP])
        mag = carve(reg_h, 6600, P, [NFP, B * FR])
        pw = carve(reg_a, 0, P, [NFP, DS])
        hc = reg_h[:, :].rearrange("p (t c) -> p t c", c=OW)
        hT = carve(reg_h, 0, P, [2, 2, FT, HALF], F16)
        y = carve(reg_h, 5120, P, [2, HS, H])
        gel = carve(reg_h, 7680, P, [2, CH])
        assert 7680 + 2 * CH <= NT * OW and 6600 + NFP * B * FR <= NT * OW
        zall = carve(reg_z, 0, KZ, [NG, WIN])
        ids = carve(reg_z, NG * WIN, V, [NG, WIN], I32)
        rinv = carve(reg_z, NG * WIN, KZ, [NG, WIN])
        x2 = carve(reg_z, 0, P, [NT, 2 * H], F16)
        xg = carve(reg_z, 0, P, [2, HS, 2 * H], F16)
        xT = carve(reg_z, 2560, P, [2, 4, HALF], F16)
        stage1 = carve(reg_w, 0, P, [2, FF])
        stage2 = carve(reg_w, 1024, P, [FT, H])
        oh_lo = carve(reg_w, 0, P, [NT, P], BF16)
        mask = carve(reg_a, 0, P, [4, TPG, KEYS])
        at = 4 * TPG * KEYS

        def work(parts, dims, dt=F32):
            nonlocal at
            ap = carve(reg_a, at, parts, dims, dt)
            at += (int(np.prod(dims)) * (2 if dt in (F16, BF16) else 4) + 3) // 4
            return ap

        u = work(KZ, [WIN])
        zq = work(KZ, [GRP])
        gT = work(KZ, [GRP])
        sm = work(P, [TPG, KEYS])
        pr = work(P, [TPG, KEYS])
        prT = work(P, [GRP])
        prE = work(2 * WCTX, [GRP])
        ut = work(P, [TPG + 1, KZ])
        yT = work(KZ, [GRP])
        zm = work(KZ, [2, HW])
        sd = work(KZ, [2, HW])
        bcur = work(KZ, [KZ])
        mx = work(P, [TPG])
        nmx = work(P, [TPG])
        psum_row = work(P, [TPG])
        prec = work(P, [TPG])
        stats = sb("stats", [P, NT, 6])
        half_gap = work(P, [NT])
        assert at <= 8192
        rt = [carve(reg_a, E * NT * i, P, [E, NT]) for i in range(16)]
        rv = [carve(reg_a, E * NT * 16 + NT * i, P, [NT]) for i in range(12)]
        count_b = carve(reg_a, E * NT * 17 + NT * 12, P, [E, NT], BF16)
        tri_b = carve(reg_a, E * NT * 18 + NT * 12, P, [P], BF16)
        ones_b = carve(reg_a, E * NT * 19 + NT * 12, P, [P], BF16)
        eqs = carve(reg_a, E * NT * 20 + NT * 12, P, [NT, ST], BF16)
        rhs_t = carve(reg_a, E * NT * 22 + NT * 12, P, [NT, NV, ST], BF16)
        tab = carve(reg_a, E * NT * 26 + NT * 12, P, [NV, ST])
        posi = carve(reg_a, E * NT * 28 + NT * 12, P, [E, NT], I32)
        wq_s = carve(reg_p, 0, P, [2, H])
        wk_s = carve(reg_p, 512, P, [2, H])
        wv_s = carve(reg_p, 1024, P, [2, H])
        wr_s = sb("wr_s", [P, 2, E])
        ta = sb("ta", [KZ, B, OW])
        tb = sb("tb", [KZ, B, OW])
        tcT = sb("tcT", [P, 2, B, KZ])
        tvT = sb("tvT", [P, 2, B, KZ])
        qT = sb("qT", [P, 2, B, KZ])
        kT = sb("kT", [P, 2, B, KZ])
        ball = sb("ball", [KZ, B, KZ])
        mall = sb("mall", [KZ, B, KZ])
        tmean = sb("tmean", [KZ, 4, B])
        pbs = sb("pbs", [P, DS])
        bqk_s = sb("bqk_s", [P, 2, 2])
        bv_s = sb("bv_s", [1, H])
        br_s = sb("br_s", [P, E])
        ids_f = sb("ids_f", [P, B * FR], I32)
        win_s = sb("win_s", [P, 1])
        wd = sb("wd", [P, 2, 2 * NFP])
        wd_hi = sb("wd_hi", [P, 2, 2 * NFP], F16)
        wd16 = sb("wd16", [P, 2, 2 * NFP], F16)
        ss = sb("ss", [P, NT])
        epsr = sb("epsr", [P, 1])
        sd2 = sb("sd2", [P, NT])
        r2 = sb("r2", [P, NT])
        r16 = sb("r16", [P, NT])
        hout = carve(reg_p, 0, P, [2, TPG, H])
        b2f = carve(reg_p, 0, 2, [E, H])

        bank = [ctx.enter_context(nc.psum_tensor(f"bank{i}", [P, 512], F32)) for i in range(8)]
        bank_s = [bank[0], bank[1]]

        x2_dram = nc.dram_tensor("x2_rows", [TOK, 2 * H], F16, kind="Internal").ap()

        ld_con, ld_ids, ld_emb, ld_pw = sem("ld_con"), sem("ld_ids"), sem("ld_emb"), sem("ld_pw")
        ld_proj, ld_zc, ld_mask = sem("ld_proj"), sem("ld_zc"), sem("ld_mask")
        ld_win, ld_w1, ld_w2, ld_bias = sem("ld_win"), sem("ld_w1"), sem("ld_w2"), sem("ld_bias")
        ld_b2 = sem("ld_b2")
        wd_chain, wd_ready, oh_ready = sem("wd_chain"), sem("wd_ready"), sem("oh_ready")
        dft_done, sq_done, m2_done, root_done, mag_done = (sem(n) for n in (
            "dft_done", "sq_done", "m2_done", "root_done", "mag_done"))
        enc_done, t_zero, t_chain, ta_centred = sem("enc_done"), sem("t_zero"), sem("t_chain"), sem("ta_centred")
        tcT_done, tcT_ready = sem("tcT_done"), sem("tcT_ready")
        m_done, m_ready, q_done, k_done, qk_copied, qk_ready = (sem(n) for n in (
            "m_done", "m_ready", "q_done", "k_done", "qk_copied", "qk_ready"))
        v_done, v_chain, tb_centred, b_done, b_ready = (sem(n) for n in (
            "v_done", "v_chain", "tb_centred", "b_done", "b_ready"))
        tvT_done, tvT_ready, lr_done, tabs_ready = (sem(n) for n in (
            "tvT_done", "tvT_ready", "lr_done", "tabs_ready"))
        z_ready, mz_done, zm_ready, var_done, sd_ready, rinv_ready = (sem(n) for n in (
            "z_ready", "mz_done", "zm_ready", "var_done", "sd_ready", "rinv_ready"))
        u_ready, g_done, g_ready, s_done, masked, max_ready, nmax_ready = (sem(n) for n in (
            "u_ready", "g_done", "g_ready", "s_done", "masked", "max_ready", "nmax_ready"))
        exp_done, rec_ready, probs_ready, ut_done, ut_ready, pt_done = (sem(n) for n in (
            "exp_done", "rec_ready", "probs_ready", "ut_done", "ut_ready", "pt_done"))
        prT_ready, prE_ready, mix_done, mix_ready, zq_ready, o_done, hc_ready = (sem(n) for n in (
            "prT_ready", "prE_ready", "mix_done", "mix_ready", "zq_ready", "o_done", "hc_ready"))
        stats_ready, var_chain = sem("stats_ready"), sem("var_chain")
        ss_ready, hout_ready, pair_hi, pair_ready, stage_free = (sem(n) for n in (
            "ss_ready", "hout_ready", "pair_hi", "pair_ready", "stage_free"))
        sd2_ready, r2_ready, x_hi, x_lo, x2_sent = (sem(n) for n in (
            "sd2_ready", "r2_ready", "x_hi", "x_lo", "x2_sent"))
        rt_chain, logits_ready, exps_ready, counts_ready, ranks_done, vals_ready = (sem(n) for n in (
            "rt_chain", "logits_ready", "exps_ready", "counts_ready", "ranks_done", "vals_ready"))
        eqs_ready, rhs_ready, tab_done, tab_copied, tab_chain, table_ready = (sem(n) for n in (
            "eqs_ready", "rhs_ready", "tab_done", "tab_copied", "tab_chain", "table_ready"))
        idx_ready, xt_done, xt_ready, l1_done, gelu_done, hi_ready, lo_ready = (sem(n) for n in (
            "idx_ready", "xt_done", "xt_ready", "l1_done", "gelu_done", "hi_ready", "lo_ready"))
        y_done, y_ready, b2_hi, b2_ready, misc_ready = (sem(n) for n in (
            "y_done", "y_ready", "b2_hi", "b2_ready", "misc_ready"))
        hout_sent = [sem(f"hout_sent{j}") for j in range(2)]
        gathered = [sem(f"gathered{j}") for j in range(2)]
        scattered = [sem(f"scattered{j}") for j in range(2)]
        gidx = sb("gidx", [P, 2, HS], I32)
        sidx = sb("sidx", [P, 2, HS], I32)

        iota_f = con[:, C_IOTA:C_IOTA + P]
        part_f = con[:, C_PART:C_PART + 1]
        ident = con[:, C_ID:C_ID + P]

        block = ctx.enter_context(nc.Block())

        chunks = [(c, min(FRAMES_PER_BANK, B * FR - c)) for c in range(0, B * FR, FRAMES_PER_BANK)]
        dft_bank = [bank[4], bank[5], bank[6], bank[7], bank[0]]

        @block.sync
        def _(sp):
            for half in range(2):
                sp.dma_start(ids_f[64 * half:64 * half + 64, :], ids_frames).then_inc(ld_ids, 16)
                sp.dma_start(win_s[64 * half:64 * half + 64, :], window).then_inc(ld_ids, 16)
            sp.dma_start(con[:, :], consts).then_inc(ld_con, 16)
            sp.dma_start(ids, ids_win.partition_broadcast(V)).then_inc(ld_win, 16)
            sp.dma_start(pw, proj_w).then_inc(ld_pw, 16)
            sp.dma_start(pbs[V:V + FR, :], proj_b.partition_broadcast(FR)).then_inc(ld_pw, 16)
            sp.dma_start(zall[V:KZ, :, :], frames_of).then_inc(ld_zc, 16)
            for dst, src in ((wq_s, wq), (wk_s, wk), (wv_s, wv), (wr_s[:, :, :], wr)):
                sp.dma_start(dst, src.rearrange("(k p) n -> p k n", p=P)).then_inc(ld_proj, 16)
            sp.dma_start(bqk_s[:, :, :], bqk).then_inc(ld_proj, 16)
            sp.dma_start(bv_s[:, :], bv).then_inc(ld_proj, 16)
            sp.dma_start(br_s[:, :], br.partition_broadcast(P)).then_inc(ld_proj, 16)
            sp.dma_start(b1s[:, :, :], b1).then_inc(ld_bias, 16)
            w1_v = w1.rearrange("e (k p) f -> p e k f", p=P)
            w2_v = w2.rearrange("e (k p) f -> p e k f", p=P)

            def stage_weights(e):
                wait(sp, stage_free, 4 * e - 2)
                sl = slice(e, e + 1) if isinstance(e, int) else bass.ds(e, 1)
                sp.dma_start(stage1, w1_v[:, sl, :, :].rearrange("p o k f -> p (o k) f")).then_inc(ld_w1, 16)
                wait(sp, stage_free, 4 * e)
                sp.dma_start(stage2, w2_v[:, sl, :, :].rearrange("p o k f -> p (o k) f")).then_inc(ld_w2, 16)

            stage_weights(0)
            sp.wait_ge(enc_done, 1)
            sp.dma_start(mask, masks).then_inc(ld_mask, 16)
            with sp.Fori(1, E) as e:
                stage_weights(e)

            with sp.Fori(0, NG // 2) as i:
                for j in range(2):
                    sp.wait_ge(hout_ready, (2 * i + j + 1) * TPG)
                    sp.dma_start(out[bass.ds((2 * i + j) * TPG, TPG), :, :].rearrange("t p c -> p t c"),
                                 hout[:, j, :, :]).then_inc(hout_sent[j], 16)
            with sp.Fori(0, NG) as g:
                sp.wait_ge(x_lo, (g + 1) * TPG)
                sp.dma_start(x2_dram.rearrange("(t p) c -> p t c", p=P)[:, bass.ds(g * TPG, TPG), :],
                             x2[:, bass.ds(g * TPG, TPG), :]).then_inc(x2_sent, 16)
            for j in range(2):
                sp.wait_ge(hout_sent[j], 8 * NG)
            for part in range(2):
                sp.dma_start(b2f[part:part + 1, :, :], b2).then_inc(ld_b2, 16)
            sp.wait_ge(x2_sent, 16 * NG)

        @block.gpsimd
        def _(pool):
            nc.gpsimd.memset(ta[:, :, :], 0.0).then_inc(t_zero, 1)
            nc.gpsimd.memset(tb[:, :, :], 0.0).then_inc(t_zero, 1)

            with pool.Fori(0, E) as e:
                for n, (stage, dst, ld) in enumerate(((stage1, w1s, ld_w1), (stage2, w2s, ld_w2))):
                    wait_apart(pool, ld, 16 * (e + 1))
                    hi = dst[:, 0, bass.ds(e, 1), :, :].rearrange("p o k c -> p (o k c)")
                    lo = dst[:, 1, bass.ds(e, 1), :, :].rearrange("p o k c -> p (o k c)")
                    flat = stage.rearrange("p k c -> p (k c)")
                    nc.gpsimd.tensor_scalar(flat, flat, W_SCALE, None, ALU.mult).then_inc(stage_free, 1)
                    pool.wait_ge(stage_free, 4 * e + 2 * n + 1)
                    nc.gpsimd.tensor_copy(hi, flat).then_inc(pair_hi, 1)
                    pool.wait_ge(pair_hi, 2 * e + n + 1)
                    nc.gpsimd.tensor_tensor(lo, flat, hi, ALU.subtract).then_inc(stage_free, 1)

            def residual(i, j):
                g = 2 * i + j
                pool.wait_ge(hc_ready, (g + 1) * TPG)
                wait(pool, hout_sent[j], 16 * i)
                for t in range(TPG):
                    tile = g * TPG + t
                    row = hc[:, tile:tile + 1, :] if isinstance(tile, int) else hc[:, bass.ds(tile, 1), :]
                    row = row.rearrange("p o c -> p (o c)")
                    nc.gpsimd.tensor_tensor(hout[:, j, t, :], row[:, 0:H],
                                            row[:, OW - 1:OW].to_broadcast([P, H]), ALU.add).then_inc(hout_ready, 1)

            for j in range(2):
                residual(0, j)
            with pool.Fori(1, NG // 2) as i:
                for j in range(2):
                    residual(i, j)

            def gather(e, h):
                k = 2 * e + h
                pool.wait_ge(table_ready, e + 1)
                wait(pool, gathered[h], 80 * e)
                cols = tok_idx[:, e, HS * h:HS * h + HS] if isinstance(e, int) else \
                    tok_idx[:, bass.ds(e, 1), HS * h:HS * h + HS].rearrange("p o s -> p (o s)")
                nc.gpsimd.tensor_copy(gidx[:, h, :], cols).then_inc(idx_ready, 1)
                wait(pool, xt_done, HS * (k - 1))
                return k

            def send_gather(h, count):
                wait_apart(pool, idx_ready, count)
                for s in range(HS):
                    nc.gpsimd.indirect_dma_start(
                        out=xg[:, h, s, :], out_offset=None, in_=x2_dram,
                        in_offset=bass.IndirectOffsetOnAxis(ap=gidx[:, h, s:s + 1], axis=0)).then_inc(gathered[h], 16)

            def scatter(e, h, count):
                k = 2 * e + h
                wait(pool, scattered[h], 80 * e)
                cols = tok_idx[:, e, HS * h:HS * h + HS] if isinstance(e, int) else \
                    tok_idx[:, bass.ds(e, 1), HS * h:HS * h + HS].rearrange("p o s -> p (o s)")
                nc.gpsimd.tensor_copy(sidx[:, h, :], cols).then_inc(idx_ready, 1)
                if h == 0:
                    wait(pool, scattered[1], 80 * e)
                pool.wait_ge(idx_ready, count)
                for s in range(HS):
                    wait_apart(pool, y_ready, HS * k + s + 1)
                    nc.gpsimd.indirect_dma_start(
                        out=out.rearrange("t p c -> (t p) c"),
                        out_offset=bass.IndirectOffsetOnAxis(ap=sidx[:, h, s:s + 1], axis=0),
                        in_=y[:, h, s, :], in_offset=None, compute_op=ALU.add).then_inc(scattered[h], 16)

            pool.wait_ge(x2_sent, 16 * NG)
            for k in range(4):
                gather(k // 2, k % 2)
                send_gather(k % 2, k + 1)
            for j in range(2):
                pool.wait_ge(hout_sent[j], 8 * NG)

            def step(i, more):
                base = 4 + 4 * i
                if more:
                    gather(i + 2, 0)
                    send_gather(0, base + 1)
                scatter(i, 0, base + (2 if more else 1))
                if more:
                    gather(i + 2, 1)
                    send_gather(1, base + 3)
                scatter(i, 1, base + (4 if more else 2))

            step(0, True)
            with pool.Fori(1, E - 2) as i:
                step(i, True)
            for i in (E - 2, E - 1):
                base = 4 + 4 * (E - 2) + 2 * (i - (E - 2))
                scatter(i, 0, base + 1)
                scatter(i, 1, base + 2)
            for h in range(2):
                pool.wait_ge(scattered[h], 80 * E)

        @block.scalar
        def _(act):
            for b in range(B):
                act.wait_ge(t_zero, 1)
                act.dma_start(ta[0:V, b, 0:DE], emb).then_inc(ld_emb, 16)
            for c, (first, n) in enumerate(chunks):
                act.wait_ge(dft_done, c + 1)
                nc.scalar.activation(sq[:, first:first + n, :, :].rearrange("p f r j -> p (f r j)"),
                                     dft_bank[c][:, 0:n * 2 * NFP], ACT.Square).then_inc(sq_done, 1)
            act.wait_ge(m2_done, 2)
            nc.scalar.activation(root.rearrange("p f j -> p (f j)"), sq_floor, ACT.Sqrt,
                                 scale=1.0 / DFT_SCALE ** 2).then_inc(root_done, 1)
            act.wait_ge(m_done, 1)
            nc.scalar.activation(mall[:, :, :].rearrange("p b k -> p (b k)"), bank[5][0:KZ, 0:B * KZ],
                                 ACT.Copy, scale=1.0 / H).then_inc(m_ready, 1)
            act.wait_ge(q_done, 1)
            nc.scalar.activation(qT[:, :, :, :].rearrange("p j b k -> p (j b k)"), bank[6][:, 0:2 * B * KZ],
                                 ACT.Copy).then_inc(qk_copied, 1)
            act.wait_ge(k_done, 1)
            nc.scalar.activation(kT[:, :, :, :].rearrange("p j b k -> p (j b k)"), bank[7][:, 0:2 * B * KZ],
                                 ACT.Copy).then_inc(qk_copied, 1)
            act.wait_ge(misc_ready, 2)
            for g in range(NG):
                act.wait_ge(var_done, g + 1)
                if g >= 1:
                    act.wait_ge(rinv_ready, g)
                for hf in range(2):
                    nc.scalar.activation(sd[:, hf, :], bank[2 + hf][0:KZ, 0:HW], ACT.Sqrt,
                                         bias=con[0:KZ, C_EPS:C_EPS + 1]).then_inc(sd_ready, 1)
                if g == 0:
                    act.wait_ge(b_done, 1)
                    nc.scalar.activation(ball[:, :, :].rearrange("p b k -> p (b k)"), bank[4][0:KZ, 0:B * KZ],
                                         ACT.Copy, scale=H ** -0.5).then_inc(b_ready, 1)
            def copy_g(g):
                act.wait_ge(g_done, g + 1)
                nc.scalar.activation(gT, bank[2][0:KZ, :], ACT.Copy).then_inc(g_ready, 1)

            def exps(g, t):
                if t == 0:
                    act.wait_ge(nmax_ready, g + 1)
                    wait(act, pt_done, g)
                nc.scalar.activation(pr[:, t, :], sm[:, t, :], ACT.Exp, bias=nmx[:, t:t + 1],
                                     accum_out=psum_row[:, t:t + 1]).then_inc(exp_done, 1)

            def attend(g, more):
                if more:
                    copy_g(g + 1)
                act.wait_ge(pt_done, g + 1)
                wait(act, mix_done, g)
                nc.scalar.activation(prT, bank[3][:, :], ACT.Copy).then_inc(prT_ready, 1)
                act.wait_ge(mix_done, g + 1)
                wait(act, o_done, TPG * g)
                nc.scalar.activation(yT, bank[2][0:KZ, :], ACT.Copy).then_inc(mix_ready, 1)
                for t in range(TPG):
                    if more:
                        exps(g + 1, t)
                    n = TPG * g + t
                    wait_apart(act, o_done, n + 1)
                    row = hc[:, n:n + 1, :] if isinstance(n, int) else hc[:, bass.ds(n, 1), :]
                    nc.scalar.activation(row.rearrange("p o c -> p (o c)"), bank[6 + t % 2][:, 0:OW],
                                         ACT.Copy).then_inc(hc_ready, 1)

            copy_g(0)
            for t in range(TPG):
                exps(0, t)
            attend(0, True)
            with act.Fori(1, NG - 1) as g:
                attend(g, True)
            attend(NG - 1, False)
            act.wait_ge(ss_ready, 1)
            act.wait_ge(misc_ready, 2)
            nc.scalar.activation(sd2[:, :], ss[:, :], ACT.Sqrt, scale=1.0 / H,
                                 bias=epsr[:, 0:1]).then_inc(sd2_ready, 1)
            act.wait_ge(r2_ready, 2)
            with act.Fori(0, NT) as t:
                nc.scalar.activation(x2[:, bass.ds(t, 1), 0:H].rearrange("p o c -> p (o c)"),
                                     hc[:, bass.ds(t, 1), 0:H].rearrange("p o c -> p (o c)"), ACT.Copy,
                                     scale=r16[:, bass.ds(t, 1)]).then_inc(x_hi, 1)
            act.wait_ge(logits_ready, 1)
            nc.scalar.activation(rt[1].rearrange("p e t -> p (e t)"), rt[0].rearrange("p e t -> p (e t)"),
                                 ACT.Exp).then_inc(exps_ready, 1)

            def rows_T(k, par):
                for s in range(HS):
                    act.wait_ge(xt_done, HS * k + s + 1)
                    if s == 0:
                        wait(act, l1_done, 8 * (k - 1))
                    tx = bank[(HS * par + s) % 2][:, 0:256].bitcast(F16).rearrange("p (c n) -> p c n", c=4)
                    nc.scalar.activation(xT[:, par, :, s * P:(s + 1) * P], tx, ACT.Copy).then_inc(xt_ready, 1)

            def gelus(e, par):
                for f in range(FT):
                    for c in range(2):
                        n = 8 * (2 * e + par) + 2 * f + c
                        act.wait_ge(l1_done, n + 1)
                        wait_apart(act, lo_ready, n - 1)
                        bias = b1s[:, e, f:f + 1] if isinstance(e, int) else \
                            b1s[:, bass.ds(e, 1), f:f + 1].rearrange("p o f -> p (o f)")
                        nc.scalar.activation(gel[:, c, :], bank[2 + c][:, 0:CH], ACT.Gelu, bias=bias,
                                             scale=1.0 / (X_SCALE * W_SCALE)).then_inc(gelu_done, 1)

            rows_T(0, 0)
            rows_T(1, 1)
            act.wait_ge(ld_bias, 16)
            gelus(0, 0)

            def step(i, more):
                gelus(i, 1)
                if more:
                    rows_T(2 * i + 2, 0)
                    gelus(i + 1, 0)
                    rows_T(2 * i + 3, 1)

            step(0, True)
            with act.Fori(1, E - 1) as i:
                step(i, True)
            step(E - 1, False)

        @block.vector
        def _(dve):
            chain = {}

            def then(ins, s):
                chain[id(s)] = chain.get(id(s), 0) + 1
                ins.then_inc(s, 1)
                dve.wait_ge(s, chain[id(s)])

            dve.wait_ge(ld_con, 16)
            dve.wait_ge(ld_ids, 64)
            wdf = wd[:, :, :].rearrange("p a b -> p (a b)")
            then(nc.vector.tensor_scalar(wdf, con[:, C_DFT:C_DFT + 4 * NFP], win_s[:, 0:1], DFT_SCALE,
                                         ALU.mult, ALU.mult), wd_chain)
            then(nc.vector.tensor_copy(wd_hi[:, :, :].rearrange("p a b -> p (a b)"), wdf), wd_chain)
            nc.vector.tensor_copy(wd16[0:V, :, :], wd_hi[0:V, :, :]).then_inc(wd_ready, 1)
            nc.vector.tensor_tensor(wd16[V:P, :, :], wd[V:P, :, :], wd_hi[V:P, :, :],
                                    ALU.subtract).then_inc(wd_ready, 1)
            for first, n in chunks:
                nc.vector.tensor_tensor(
                    onehot[:, first:first + n, :],
                    ids_f[:, first:first + n].unsqueeze(2).to_broadcast([P, n, V]),
                    con[:, C_IOTA:C_IOTA + V].unsqueeze(1).to_broadcast([P, n, V]),
                    ALU.is_equal).then_inc(oh_ready, 1)
            dve.wait_ge(ld_win, 16)
            nc.vector.tensor_scalar(zall[0:V, :, :].rearrange("p g w -> p (g w)"),
                                    ids.rearrange("p g w -> p (g w)"), part_f[0:V, :], None,
                                    ALU.is_equal).then_inc(z_ready, 1)
            nc.vector.memset(epsr[:, :], EPS).then_inc(misc_ready, 1)
            nc.vector.memset(ones16[:, :], X_SCALE).then_inc(misc_ready, 1)
            nc.vector.tensor_copy(iota_b[:, :], iota_f).then_inc(misc_ready, 1)
            nc.vector.tensor_copy(ident16[:, :], ident).then_inc(misc_ready, 1)
            dve.wait_ge(sq_done, len(chunks))
            nc.vector.tensor_tensor(m2, sq[:, :, 0, :], sq[:, :, 1, :], ALU.add).then_inc(m2_done, 1)
            dve.wait_ge(m2_done, 1)
            nc.vector.tensor_scalar(sq_floor, m2.rearrange("p f j -> p (f j)"), 1e-30, None,
                                    ALU.max).then_inc(m2_done, 1)
            dve.wait_ge(root_done, 1)
            nc.vector.scalar_tensor_tensor(mag.rearrange("p j f -> p f j"), m2, 0.0, root, ALU.is_gt,
                                           ALU.mult).then_inc(mag_done, 1)
            dve.wait_ge(ld_pw, 32)
            dve.wait_ge(ld_emb, 32)
            dve.wait_ge(t_zero, 2)
            dve.wait_ge(enc_done, 1)
            then(nc.vector.tensor_tensor(ta[V:V + FR, :, DE:H],
                                         bank[1][V:V + FR, 0:B * DS].rearrange("p (b d) -> p b d", b=B),
                                         pbs[V:V + FR, :].unsqueeze(1).to_broadcast([FR, B, DS]),
                                         ALU.add), t_chain)

            def centre(tab_ap, src, m, chain_sem, done):
                then(nc.vector.tensor_reduce(tmean[:, m, :], src, AX.X, ALU.add), chain_sem)
                then(nc.vector.tensor_scalar(tmean[:, m + 1, :], tmean[:, m, :], 1.0 / H, None,
                                             ALU.mult), chain_sem)
                nc.vector.tensor_tensor(tab_ap[:, :, 0:H], src,
                                        tmean[:, m + 1, :].unsqueeze(2).to_broadcast([KZ, B, H]),
                                        ALU.subtract).then_inc(done, 1)
                nc.vector.tensor_copy(tab_ap[:, :, OW - 1], tmean[:, m + 1, :]).then_inc(done, 1)

            centre(ta, ta[:, :, 0:H], 0, t_chain, ta_centred)
            dve.wait_ge(tcT_done, 1)
            nc.vector.tensor_copy(tcT[:, :, :, :].rearrange("p k b z -> p (k b z)"),
                                  bank[4][:, 0:2 * B * KZ]).then_inc(tcT_ready, 1)
            dve.wait_ge(qk_copied, 2)
            dve.wait_ge(ld_proj, 16 * 7)
            for n, dst in enumerate((qT, kT)):
                nc.vector.tensor_copy(dst[:, :, :, KZ - 1],
                                      bqk_s[:, n, :].unsqueeze(2).to_broadcast([P, 2, B])).then_inc(qk_ready, 1)
            dve.wait_ge(v_done, 1)
            centre(tb, bank[5][0:KZ, :].rearrange("p (b c) -> p b c", b=B), 2, v_chain, tb_centred)
            dve.wait_ge(ld_zc, 16)

            def times_z(g):
                dve.wait_ge(mz_done, g + 1)
                if g >= 1:
                    dve.wait_ge(var_done, g)
                for hf in range(2):
                    nc.vector.tensor_tensor(zm[:, hf, :], bank[hf][0:KZ, 0:HW],
                                            zall[:, g, hf * HW:(hf + 1) * HW], ALU.mult).then_inc(zm_ready, 1)

            times_z(0)
            for g in range(NG):
                if g + 1 < NG:
                    times_z(g + 1)
                dve.wait_ge(sd_ready, 2 * (g + 1))
                nc.vector.reciprocal(rinv[:, g, :], sd.rearrange("p h w -> p (h w)")).then_inc(rinv_ready, 1)
                if g == 0:
                    dve.wait_ge(tvT_done, 1)
                    nc.vector.tensor_copy(tvT[:, :, :, :].rearrange("p k b z -> p (k b z)"),
                                          bank[6][:, 0:2 * B * KZ]).then_inc(tvT_ready, 1)
                if g == 1:
                    dve.wait_ge(lr_done, 1)
                    for n, dst in enumerate((ta, tb)):
                        nc.vector.tensor_copy(dst[:, :, H:H + E],
                                              bank[7][0:KZ, n * B * E:(n + 1) * B * E].rearrange(
                                                  "p (b e) -> p b e", b=B)).then_inc(tabs_ready, 1)

            def pick(ap, g):
                if isinstance(g, int):
                    return ap[:, g, :]
                return ap[:, bass.ds(g, 1), :].rearrange("p o w -> p (o w)")

            def normed(g):
                dve.wait_ge(rinv_ready, NG)
                dve.wait_ge(b_ready, 1)
                wait(dve, ut_done, g)
                nc.vector.tensor_copy(bcur, pick(ball, g // (NG // B))).then_inc(u_ready, 1)
                nc.vector.tensor_tensor(u, pick(zall, g), pick(rinv, g), ALU.mult).then_inc(u_ready, 1)

            def scores(g):
                dve.wait_ge(s_done, g + 1)
                wait(dve, exp_done, TPG * g)
                if isinstance(g, int):
                    m = mask[:, g % 4, :, :]
                else:
                    m = mask[:, bass.ds(g % 4, 1), :, :].rearrange("p o t k -> p (o t) k")
                for hf in range(2):
                    nc.vector.tensor_tensor(sm[:, 2 * hf:2 * hf + 2, :],
                                            bank_s[hf][:, 0:2 * KEYS].rearrange("p (t k) -> p t k", t=2),
                                            m[:, 2 * hf:2 * hf + 2, :], ALU.add).then_inc(masked, 1)

            def maxima(g):
                dve.wait_ge(masked, 2 * (g + 1))
                nc.vector.tensor_reduce(mx, sm, AX.X, ALU.max).then_inc(max_ready, 1)
                dve.wait_ge(max_ready, g + 1)
                nc.vector.tensor_scalar(nmx, mx, -1.0, None, ALU.mult).then_inc(nmax_ready, 1)

            def keys_rows(g):
                dve.wait_ge(ut_done, g + 1)
                wait(dve, mix_done, g)
                nc.vector.tensor_copy(ut[:, 0:TPG, :].rearrange("p t k -> p (t k)"),
                                      bank[5][:, 0:TPG * KZ]).then_inc(ut_ready, 1)
                nc.vector.tensor_copy(ut[0:2 * WCTX, TPG, :],
                                      bank[5][0:2 * WCTX, TPG * KZ:(TPG + 1) * KZ]).then_inc(ut_ready, 1)

            def probs(g):
                dve.wait_ge(exp_done, TPG * (g + 1))
                nc.vector.reciprocal(prec, psum_row).then_inc(rec_ready, 1)
                dve.wait_ge(rec_ready, g + 1)
                nc.vector.tensor_tensor(pr, pr, prec.unsqueeze(2).to_broadcast([P, TPG, KEYS]),
                                        ALU.mult).then_inc(probs_ready, 1)

            def attend(g, more, more2):
                wait(dve, o_done, TPG * g)
                src = zall[:, g, WCTX:WCTX + GRP] if isinstance(g, int) else \
                    zall[:, bass.ds(g, 1), WCTX:WCTX + GRP].rearrange("p o w -> p (o w)")
                nc.vector.tensor_copy(zq, src).then_inc(zq_ready, 1)
                if more:
                    scores(g + 1)
                dve.wait_ge(pt_done, g + 1)
                nc.vector.tensor_copy(prE, bank[4][0:2 * WCTX, :]).then_inc(prE_ready, 1)
                if more:
                    maxima(g + 1)
                    keys_rows(g + 1)
                if more2:
                    normed(g + 2)
                if more:
                    probs(g + 1)
                for t in range(TPG):
                    n = TPG * g + t
                    dve.wait_ge(hc_ready, n + 1)
                    row = hc[:, n:n + 1, :] if isinstance(n, int) else hc[:, bass.ds(n, 1), :]
                    row = row.rearrange("p o c -> p (o c)")[:, 0:H]
                    to = stats[:, n:n + 1, :] if isinstance(n, int) else stats[:, bass.ds(n, 1), :]
                    nc.vector.bn_stats(to.rearrange("p o c -> p (o c)"), row).then_inc(stats_ready, 1)

            normed(0)
            dve.wait_ge(ld_mask, 16)
            scores(0)
            maxima(0)
            keys_rows(0)
            normed(1)
            probs(0)
            attend(0, True, True)
            with dve.Fori(1, NG - 2) as g:
                attend(g, True, True)
            attend(NG - 2, True, False)
            attend(NG - 1, False, False)

            dve.wait_ge(stats_ready, NT)
            nc.vector.tensor_tensor(half_gap, stats[:, :, 1], stats[:, :, 4], ALU.subtract).then_inc(var_chain, 1)
            nc.vector.tensor_tensor(ss[:, :], stats[:, :, 2], stats[:, :, 5], ALU.add).then_inc(var_chain, 1)
            dve.wait_ge(var_chain, 2)
            nc.vector.scalar_tensor_tensor(half_gap, half_gap, H / 4.0, half_gap, ALU.mult,
                                           ALU.mult).then_inc(var_chain, 1)
            dve.wait_ge(var_chain, 3)
            nc.vector.tensor_tensor(ss[:, :], ss[:, :], half_gap, ALU.add).then_inc(ss_ready, 1)
            dve.wait_ge(sd2_ready, 1)
            nc.vector.reciprocal(r2[:, :], sd2[:, :]).then_inc(r2_ready, 1)
            dve.wait_ge(r2_ready, 1)
            nc.vector.tensor_scalar(r16[:, :], r2[:, :], X_SCALE, None, ALU.mult).then_inc(r2_ready, 1)
            dve.wait_ge(r2_ready, 2)
            with dve.Fori(0, NT) as t:
                dve.wait_ge(x_hi, t + 1)
                xrow = x2[:, bass.ds(t, 1), :].rearrange("p o c -> p (o c)")
                nc.vector.scalar_tensor_tensor(xrow[:, H:2 * H],
                                               hc[:, bass.ds(t, 1), 0:H].rearrange("p o c -> p (o c)"),
                                               r16[:, bass.ds(t, 1)], xrow[:, 0:H], ALU.mult,
                                               ALU.subtract).then_inc(x_lo, 1)

            def et(v):
                return v.unsqueeze(1).to_broadcast([P, E, NT])

            def te(a):
                return a.rearrange("p e t -> p t e")

            def full(col):
                return con[:, col:col + NT].unsqueeze(1).to_broadcast([P, E, NT])

            tt, ts, red = nc.vector.tensor_tensor, nc.vector.tensor_scalar, nc.vector.tensor_reduce
            stt = nc.vector.scalar_tensor_tensor
            pref = con[:, C_PREF:C_PREF + E].unsqueeze(2).to_broadcast([P, E, NT])
            raw = hc[:, :, H:H + E].rearrange("p t e -> p e t")
            lg, ex, prb, c1, oh1, p2, c2, oh2, wt, cnt, ta_, tb_, incl, rank, alt, tmp = rt
            vm, vs, vr, m1, k1, m2_, k2, den, rden, wa, wb, spare = rv
            then(tt(lg, raw, et(r2[:, :]), ALU.mult), rt_chain)
            then(tt(lg, lg, br_s[:, :].unsqueeze(2).to_broadcast([P, E, NT]), ALU.add), rt_chain)
            then(red(vm, te(lg), AX.X, ALU.max), rt_chain)
            tt(lg, lg, et(vm), ALU.subtract).then_inc(logits_ready, 1)
            dve.wait_ge(exps_ready, 1)
            then(red(vs, te(ex), AX.X, ALU.add), rt_chain)
            then(nc.vector.reciprocal(vr, vs), rt_chain)
            then(tt(prb, ex, et(vr), ALU.mult), rt_chain)

            def top(probs_ap, m, c, k, oh):
                then(red(m, te(probs_ap), AX.X, ALU.max), rt_chain)
                then(tt(c, probs_ap, et(m), ALU.is_equal), rt_chain)
                then(tt(c, c, pref, ALU.mult), rt_chain)
                then(red(k, te(c), AX.X, ALU.max), rt_chain)
                then(tt(oh, c, et(k), ALU.is_equal), rt_chain)

            top(prb, m1, c1, k1, oh1)
            then(stt(p2, oh1, -2.0, prb, ALU.mult, ALU.add), rt_chain)
            top(p2, m2_, c2, k2, oh2)
            then(tt(den, m1, m2_, ALU.add), rt_chain)
            then(ts(den, den, 1e-9, None, ALU.max), rt_chain)
            then(nc.vector.reciprocal(rden, den), rt_chain)
            then(tt(wa, m1, rden, ALU.mult), rt_chain)
            then(tt(wb, m2_, rden, ALU.mult), rt_chain)
            then(tt(cnt, oh1, oh2, ALU.add), rt_chain)
            nc.vector.tensor_copy(count_b, cnt).then_inc(counts_ready, 1)
            nc.vector.tensor_copy(tri_b, con[:, C_TRI:C_TRI + P]).then_inc(counts_ready, 1)
            nc.vector.memset(ones_b, 1.0).then_inc(counts_ready, 1)
            then(tt(wt, oh1, et(wa), ALU.mult), rt_chain)
            then(tt(tmp, oh2, et(wb), ALU.mult), rt_chain)
            then(tt(wt, wt, tmp, ALU.add), rt_chain)
            nc.vector.tensor_copy(vals[:, :, :, 0], part_f.unsqueeze(1).to_broadcast([P, E, NT])
                                  ).then_inc(vals_ready, 1)
            nc.vector.tensor_copy(vals[:, :, :, 1], full(C_TILE)).then_inc(vals_ready, 1)
            then(nc.vector.tensor_copy(vals[:, :, :, 2], wt), rt_chain)
            then(tt(wt, wt, vals[:, :, :, 2], ALU.subtract), rt_chain)
            then(nc.vector.tensor_copy(vals[:, :, :, 3], wt), rt_chain)
            tt(vals[:, :, :, 4], wt, vals[:, :, :, 3], ALU.subtract).then_inc(vals_ready, 1)
            dve.wait_ge(ranks_done, 1)
            per_tile = bank[0][:, 0:E * NT]
            before = bank[0][:, E * NT:2 * E * NT].rearrange("p (e t) -> p e t", e=E)
            then(nc.vector.tensor_copy(ta_, full(C_RESET)), rt_chain)
            then(nc.vector.tensor_tensor_scan(incl.rearrange("p e t -> p (e t)"),
                                              ta_.rearrange("p e t -> p (e t)"), per_tile, 0.0,
                                              ALU.mult, ALU.add), rt_chain)
            then(tt(rank, incl, per_tile.rearrange("p (e t) -> p e t", e=E), ALU.subtract), rt_chain)
            then(tt(rank, rank, before, ALU.add), rt_chain)
            then(tt(alt, full(C_TOK), rank, ALU.subtract), rt_chain)
            then(tt(alt, alt, incl[:, :, NT - 1:NT].to_broadcast([P, E, NT]), ALU.add), rt_chain)
            then(tt(tmp, rank, alt, ALU.subtract), rt_chain)
            then(tt(tmp, tmp, cnt, ALU.mult), rt_chain)
            then(tt(posi, alt, tmp, ALU.add), rt_chain)
            low = tb_.bitcast(I32)
            then(ts(low, posi, P - 1, None, ALU.bitwise_and), rt_chain)
            then(ts(posi, posi, 7, None, ALU.arith_shift_right), rt_chain)
            then(nc.vector.tensor_copy(pos_lo[:, :, :], low), rt_chain)
            then(nc.vector.tensor_copy(pos_hi[:, :, :], posi), rt_chain)

            def of(ap, e):
                one = slice(e, e + 1) if isinstance(e, int) else bass.ds(e, 1)
                if len(ap.shape) == 3:
                    return ap[:, one, :].rearrange("p o a -> p (o a)")
                return ap[:, one, :, :].rearrange("p o a b -> p (o a) b")

            def spread(e):
                wait(dve, tab_done, e)
                lo_e, hi_e = of(pos_lo[:, :, :], e), of(pos_hi[:, :, :], e)
                for t in range(NT):
                    ins = ts(oh_lo[:, t, :], iota_b[:, :], lo_e[:, t:t + 1], None, ALU.is_equal)
                    if t == NT - 1:
                        ins.then_inc(eqs_ready, 1)
                tt(eqs, hi_e.unsqueeze(2).to_broadcast([P, NT, ST]),
                   con[:, C_IOTA:C_IOTA + ST].unsqueeze(1).to_broadcast([P, NT, ST]),
                   ALU.is_equal).then_inc(eqs_ready, 1)
                dve.wait_ge(eqs_ready, 2 * (e + 1))
                tt(rhs_t, of(vals[:, :, :, :], e).unsqueeze(3).to_broadcast([P, NT, NV, ST]),
                   eqs.unsqueeze(2).to_broadcast([P, NT, NV, ST]), ALU.mult).then_inc(rhs_ready, 1)

            def table(e):
                dve.wait_ge(tab_done, e + 1)
                nc.vector.tensor_copy(tab.rearrange("p v s -> p (v s)"),
                                      bank[6][:, 0:NV * ST]).then_inc(tab_copied, 1)
                dve.wait_ge(tab_copied, e + 1)
                stt(of(tok_idx[:, :, :], e), tab[:, 1, :], float(P), tab[:, 0, :], ALU.mult, ALU.add
                    ).then_inc(tab_chain, 1)
                tt(tab[:, 2, :], tab[:, 2, :], tab[:, 3, :], ALU.add).then_inc(tab_chain, 1)
                dve.wait_ge(tab_chain, 3 * e + 2)
                tt(tab[:, 2, :], tab[:, 2, :], tab[:, 4, :], ALU.add).then_inc(tab_chain, 1)
                dve.wait_ge(tab_chain, 3 * e + 3)
                ts(of(tok_w[:, :, :], e), tab[:, 2, :], 1.0 / (X_SCALE * W_SCALE), None, ALU.mult
                   ).then_inc(table_ready, 1)

            dve.wait_ge(stage_free, 4 * E)
            spread(0)
            table(0)
            spread(1)
            table(1)
            dve.wait_ge(ld_b2, 32)
            then(ts(notp[:, :], con[0:2, C_PART:C_PART + 1], -1.0, 1.0, ALU.mult, ALU.add), b2_hi)
            then(ts(b2f[:, :, :], b2f[:, :, :], W_SCALE, None, ALU.mult), b2_hi)
            then(nc.vector.tensor_copy(b2s[:, :, :], b2f[:, :, :]), b2_hi)
            then(tt(b2f[:, :, :], b2f[:, :, :], b2s[:, :, :], ALU.subtract), b2_hi)
            then(ts(b2f[:, :, :], b2f[:, :, :], con[0:2, C_PART:C_PART + 1], None, ALU.mult), b2_hi)
            stt(b2s[:, :, :].rearrange("p e c -> p (e c)"), b2s[:, :, :].rearrange("p e c -> p (e c)"),
                notp[:, 0:1], b2f[:, :, :].rearrange("p e c -> p (e c)"), ALU.mult,
                ALU.add).then_inc(b2_ready, 1)

            def pairs(e, par):
                for f in range(FT):
                    for c in range(2):
                        n = 8 * (2 * e + par) + 2 * f + c
                        dve.wait_ge(gelu_done, n + 1)
                        if f == 0 and c == 0:
                            wait(dve, y_done, HS * (2 * e + par - 1))
                        cols = slice(c * CH, (c + 1) * CH)
                        ts(hT[:, par, 0, f, cols], gel[:, c, :], X_SCALE, None, ALU.mult).then_inc(hi_ready, 1)
                        dve.wait_ge(hi_ready, n + 1)
                        stt(hT[:, par, 1, f, cols], gel[:, c, :], X_SCALE, hT[:, par, 0, f, cols],
                            ALU.mult, ALU.subtract).then_inc(lo_ready, 1)

            def weighted(e, par):
                k = 2 * e + par
                wait(dve, scattered[par], 80 * e)
                dve.wait_ge(table_ready, e + 1)
                w_e = of(tok_w[:, :, :], e)
                for s in range(HS):
                    dve.wait_ge(y_done, HS * k + s + 1)
                    ts(y[:, par, s, :], bank[4 + (HS * par + s) % 2][:, 0:H],
                       w_e[:, HS * par + s:HS * par + s + 1], None, ALU.mult).then_inc(y_ready, 1)

            def step(i, more, tables):
                pairs(i, 1)
                if tables:
                    spread(i + 2)
                weighted(i, 0)
                if tables:
                    table(i + 2)
                if more:
                    pairs(i + 1, 0)
                weighted(i, 1)

            pairs(0, 0)
            step(0, True, True)
            with dve.Fori(1, E - 2) as i:
                step(i, True, True)
            step(E - 2, True, False)
            step(E - 1, False, False)

        @block.tensor
        def _(pe):
            mm = nc.tensor.matmul
            pe.wait_ge(wd_ready, 2)
            for c, (first, n) in enumerate(chunks):
                pe.wait_ge(oh_ready, c + 1)
                for f in range(n):
                    for par in range(2):
                        last = mm(dft_bank[c][64 * par:64 * par + 64, f * 2 * NFP:(f + 1) * 2 * NFP],
                                  onehot[:, first + f, :], wd16[:, par, :], start=True, stop=True)
                last.then_inc(dft_done, 1)
            pe.wait_ge(mag_done, 1)
            pe.wait_ge(ld_pw, 32)
            for b in range(B):
                for j in range(NFP):
                    kk = P if j < NFP - 1 else V
                    last = mm(bank[1][V:V + FR, b * DS:(b + 1) * DS], mag[0:kk, j, b * FR:(b + 1) * FR],
                              pw[0:kk, j, :], start=(j == 0), stop=(j == NFP - 1))
            last.then_inc(enc_done, 1)
            pe.wait_ge(ta_centred, 2)
            for kt in range(2):
                for b in range(B):
                    at_ = (kt * B + b) * KZ
                    last = nc.tensor.transpose(bank[4][:, at_:at_ + KZ], ta[:, b, kt * P:(kt + 1) * P],
                                               ident[0:KZ, 0:KZ])
            last.then_inc(tcT_done, 1)
            pe.wait_ge(tcT_ready, 1)
            for b in range(B):
                for kt in range(2):
                    last = mm(bank[5][0:KZ, b * KZ:(b + 1) * KZ], tcT[:, kt, b, :], tcT[:, kt, b, :],
                              start=(kt == 0), stop=(kt == 1))
            last.then_inc(m_done, 1)
            pe.wait_ge(ld_proj, 16 * 7)
            for w_s, bk, done in ((wq_s, bank[6], q_done), (wk_s, bank[7], k_done)):
                for j in range(2):
                    for kt in range(2):
                        last = mm(bk[:, j * B * KZ:(j + 1) * B * KZ], w_s[:, kt, j * P:(j + 1) * P],
                                  tcT[:, kt, :, :].rearrange("p b z -> p (b z)"), start=(kt == 0), stop=(kt == 1))
                last.then_inc(done, 1)

            def mz(g):
                pe.wait_ge(z_ready, 1)
                pe.wait_ge(ld_zc, 16)
                pe.wait_ge(m_ready, 1)
                if g >= 1:
                    pe.wait_ge(zm_ready, 2 * g)
                for hf in range(2):
                    last = mm(bank[hf][0:KZ, 0:HW], mall[:, g // (NG // B), :],
                              zall[:, g, hf * HW:(hf + 1) * HW], start=True, stop=True)
                last.then_inc(mz_done, 1)

            pe.wait_ge(m_ready, 1)
            for b in range(B):
                for kt in range(2):
                    mm(bank[5][0:KZ, b * H:(b + 1) * H], tcT[:, kt, b, :], wv_s[:, kt, :],
                       start=(kt == 0), stop=False)
                last = mm(bank[5][0:KZ, b * H:(b + 1) * H], con[0:1, C_ROW97:C_ROW97 + KZ], bv_s[0:1, :],
                          start=False, stop=True)
            last.then_inc(v_done, 1)
            mz(0)
            pe.wait_ge(qk_ready, 2)
            for b in range(B):
                for j in range(2):
                    last = mm(bank[4][0:KZ, b * KZ:(b + 1) * KZ], qT[:, j, b, :], kT[:, j, b, :],
                              start=(j == 0), stop=(j == 1))
            last.then_inc(b_done, 1)
            for g in range(NG):
                if g + 1 < NG:
                    mz(g + 1)
                pe.wait_ge(zm_ready, 2 * (g + 1))
                if g >= 1:
                    pe.wait_ge(sd_ready, 2 * g)
                for hf in range(2):
                    last = mm(bank[2 + hf][0:KZ, 0:HW], con[0:KZ, C_SUM:C_SUM + KZ], zm[:, hf, :],
                              start=True, stop=True)
                last.then_inc(var_done, 1)
                if g == 0:
                    pe.wait_ge(tb_centred, 2)
                    for kt in range(2):
                        for b in range(B):
                            at_ = (kt * B + b) * KZ
                            last = nc.tensor.transpose(bank[6][:, at_:at_ + KZ], tb[:, b, kt * P:(kt + 1) * P],
                                                       ident[0:KZ, 0:KZ])
                    last.then_inc(tvT_done, 1)
                if g == 1:
                    pe.wait_ge(tvT_ready, 1)
                    for n, src in enumerate((tcT, tvT)):
                        for b in range(B):
                            at_ = (n * B + b) * E
                            for kt in range(2):
                                last = mm(bank[7][0:KZ, at_:at_ + E], src[:, kt, b, :], wr_s[:, kt, :],
                                          start=(kt == 0), stop=(kt == 1))
                    last.then_inc(lr_done, 1)

            def front(g):
                pe.wait_ge(u_ready, 2 * (g + 1))
                wait(pe, mix_ready, g - 1)
                mm(bank[2][0:KZ, :], bcur, u[:, WCTX:WCTX + GRP], start=True, stop=True).then_inc(g_done, 1)
                pe.wait_ge(g_ready, g + 1)
                wait(pe, masked, 2 * g)
                for t in range(TPG):
                    last = mm(bank_s[t // 2][:, (t % 2) * KEYS:(t % 2 + 1) * KEYS], gT[:, t * P:(t + 1) * P],
                              u[:, t * P:t * P + KEYS], start=True, stop=True)
                last.then_inc(s_done, 1)
                wait(pe, ut_ready, 2 * g)
                for t in range(TPG):
                    nc.tensor.transpose(bank[5][:, t * KZ:(t + 1) * KZ], u[:, t * P:(t + 1) * P],
                                        ident[0:KZ, 0:KZ])
                nc.tensor.transpose(bank[5][0:2 * WCTX, TPG * KZ:(TPG + 1) * KZ], u[:, GRP:WIN],
                                    ident[0:KZ, 0:KZ]).then_inc(ut_done, 1)

            def back(g, more):
                pe.wait_ge(probs_ready, g + 1)
                wait(pe, prT_ready, g)
                wait(pe, prE_ready, g)
                for t in range(TPG):
                    nc.tensor.transpose(bank[3][:, t * P:(t + 1) * P], pr[:, t, 0:P], ident)
                    last = nc.tensor.transpose(bank[4][0:2 * WCTX, t * P:(t + 1) * P], pr[:, t, P:KEYS], ident)
                last.then_inc(pt_done, 1)
                pe.wait_ge(prT_ready, g + 1)
                pe.wait_ge(prE_ready, g + 1)
                pe.wait_ge(ut_ready, 2 * (g + 1))
                pe.wait_ge(g_ready, g + 2 if more else NG)
                for t in range(TPG):
                    mm(bank[2][0:KZ, t * P:(t + 1) * P], ut[:, t, :], prT[:, t * P:(t + 1) * P],
                       start=True, stop=False)
                    last = mm(bank[2][0:KZ, t * P:(t + 1) * P], ut[0:2 * WCTX, t + 1, :],
                              prE[:, t * P:(t + 1) * P], start=False, stop=True)
                last.then_inc(mix_done, 1)
                pe.wait_ge(mix_ready, g + 1)
                pe.wait_ge(zq_ready, g + 1)
                if isinstance(g, int):
                    ta_b, tb_b = ta[:, g // (NG // B), :], tb[:, g // (NG // B), :]
                else:
                    ta_b = ta[:, bass.ds(g // (NG // B), 1), :].rearrange("p o c -> p (o c)")
                    tb_b = tb[:, bass.ds(g // (NG // B), 1), :].rearrange("p o c -> p (o c)")
                for t in range(TPG):
                    wait(pe, hc_ready, TPG * g + t - 1)
                    mm(bank[6 + t % 2][:, 0:OW], zq[:, t * P:(t + 1) * P], ta_b, start=True, stop=False)
                    mm(bank[6 + t % 2][:, 0:OW], yT[:, t * P:(t + 1) * P], tb_b, start=False,
                       stop=True).then_inc(o_done, 1)

            pe.wait_ge(tabs_ready, 2)
            front(0)
            front(1)
            back(0, True)
            with pe.Fori(1, NG - 1) as g:
                front(g + 1)
                back(g, True)
            back(NG - 1, False)

            pe.wait_ge(counts_ready, 3)
            cb = count_b.rearrange("p e t -> p (e t)")
            mm(bank[0][:, 0:E * NT], ones_b, cb, start=True, stop=True)
            mm(bank[0][:, E * NT:2 * E * NT], tri_b, cb, start=True, stop=True).then_inc(ranks_done, 1)

            def table(e):
                pe.wait_ge(rhs_ready, e + 1)
                wait(pe, tab_copied, e)
                for t in range(NT):
                    last = mm(bank[6][:, 0:NV * ST], oh_lo[:, t, :],
                              rhs_t[:, t, :, :].rearrange("p v s -> p (v s)"), start=(t == 0), stop=(t == NT - 1))
                last.then_inc(tab_done, 1)

            pe.wait_ge(vals_ready, 3)
            table(0)
            table(1)

            def rows_T(k, par):
                pe.wait_ge(gathered[par], 80 * (k // 2 + 1))
                for s in range(HS):
                    wait(pe, xt_ready, HS * k + s - 1)
                    tx = bank[(HS * par + s) % 2][:, 0:256].bitcast(F16)
                    for c in range(4):
                        last = nc.tensor.transpose(tx[:, c * P:(c + 1) * P], xg[:, par, s, c * P:(c + 1) * P],
                                                   ident16[:, :])
                    last.then_inc(xt_done, 1)

            def w_cols(w_s, part, e, kt, c0, n):
                if isinstance(e, int):
                    return w_s[:, part, e, kt, c0:c0 + n]
                return w_s[:, part, bass.ds(e, 1), kt, c0:c0 + n].rearrange("p o c -> p (o c)")

            def layer1(e, par):
                k = 2 * e + par
                pe.wait_ge(xt_ready, HS * (k + 1))
                for f in range(FT):
                    for c in range(2):
                        wait(pe, gelu_done, 8 * k + 2 * f + c - 1)
                    for kt in range(2):
                        for part, rhs_parts in ((0, (0, 1)), (1, (0,))):
                            w_ = w_cols(w1s, part, e, kt, f * P, P)
                            for rp in rhs_parts:
                                for c in range(2):
                                    end = kt == 1 and part == 1
                                    last = mm(bank[2 + c][:, 0:CH], w_,
                                              xT[:, par, 2 * rp + kt, c * CH:(c + 1) * CH],
                                              start=(kt == 0 and part == 0 and rp == 0), stop=end)
                                    if end:
                                        last.then_inc(l1_done, 1)

            def layer2(e, par):
                k = 2 * e + par
                pe.wait_ge(lo_ready, 8 * (k + 1))
                for s in range(HS):
                    bk = bank[4 + (HS * par + s) % 2][:, 0:H]
                    wait(pe, y_ready, HS * k + s - 1)
                    for f in range(FT):
                        for hp, wp in ((0, 0), (0, 1), (1, 0)):
                            mm(bk, hT[:, par, hp, f, s * P:(s + 1) * P], w_cols(w2s, wp, e, f, 0, H),
                               start=(f == 0 and hp == 0 and wp == 0), stop=False)
                    b2_e = b2s[:, e, :] if isinstance(e, int) else \
                        b2s[:, bass.ds(e, 1), :].rearrange("p o c -> p (o c)")
                    mm(bk, ones16[:, :], b2_e, start=False, stop=True).then_inc(y_done, 1)

            pe.wait_ge(stage_free, 4 * E)
            pe.wait_ge(misc_ready, 4)
            rows_T(0, 0)
            rows_T(1, 1)
            layer1(0, 0)
            pe.wait_ge(b2_ready, 1)

            def step(i, more, tables):
                layer1(i, 1)
                if more:
                    rows_T(2 * i + 2, 0)
                if tables:
                    table(i + 2)
                layer2(i, 0)
                if more:
                    layer1(i + 1, 0)
                    rows_T(2 * i + 3, 1)
                layer2(i, 1)

            step(0, True, True)
            with pe.Fori(1, E - 2) as i:
                step(i, True, True)
            step(E - 2, True, False)
            step(E - 1, False, False)


def constants():
    con = np.zeros((P, NCONST), np.float32)
    n = np.arange(V)
    dft = np.zeros((V, 2, 2, NFP), np.float64)
    for par in range(2):
        for j in range(NFP):
            f = 2 * j + par
            if f < NF:
                turn = (f * n) % V
                dft[:, par, 0, j] = np.cos(2 * np.pi * turn / V)
                dft[:, par, 1, j] = np.where(turn % (V // 2) == 0, 0.0, -np.sin(2 * np.pi * turn / V))
                dft[:, par, 0, j] = np.where(turn % (V // 2) == V // 4, 0.0, dft[:, par, 0, j])
    con[:, C_DFT:C_DFT + 4 * NFP] = np.tile(dft.reshape(V, -1), (2, 1))
    con[:, C_IOTA:C_IOTA + P] = np.arange(P)
    con[:, C_PART] = np.arange(P)
    con[:, C_ID:C_ID + P] = np.eye(P)
    con[:, C_TRI:C_TRI + P] = np.triu(np.ones((P, P)), 1)
    con[:, C_EPS] = EPS
    con[KZ - 1, C_EPS] = 1.0
    con[:, C_SUM:C_SUM + KZ - 1] = 1.0
    con[0, C_ROW97 + KZ - 1] = 1.0
    con[:, C_TILE:C_TILE + NT] = np.arange(NT)
    con[:, C_TOK:C_TOK + NT] = np.arange(NT) * P + np.arange(P)[:, None]
    con[:, C_RESET:C_RESET + NT] = np.arange(NT) > 0
    con[:, C_PREF:C_PREF + E] = E - np.arange(E)

    t = np.arange(L)
    coord = np.clip((t + 0.5) * (FR / L) - 0.5, 0.0, FR - 1.0)
    i0 = np.floor(coord).astype(np.int64)
    i1 = np.minimum(i0 + 1, FR - 1)
    w = (coord - i0).astype(np.float32)
    z = np.zeros((FR, L), np.float32)
    np.add.at(z, (i0, t), np.float32(1.0) - w)
    np.add.at(z, (i1, t), w)
    frames_of = np.zeros((FR + 1, NG, WIN), np.float32)
    frames_of[FR] = 1.0
    masks = np.full((P, NG // B, TPG, KEYS), -1e30, np.float32)
    for g in range(NG):
        first = (g % (NG // B)) * GRP - WCTX
        for c in range(WIN):
            if 0 <= first + c < L:
                frames_of[:FR, g, c] = z[:, first + c]
    for g in range(NG // B):
        for tile in range(TPG):
            for q in range(P):
                for k in range(q, q + 2 * WCTX + 1):
                    if 0 <= g * GRP + tile * P + k - WCTX < L:
                        masks[q, g, tile, k] = 0.0
    return con, frames_of, masks


def kernel(**inputs):
    import concourse.bacc as bacc
    from concourse.bass_utils import run_bass_kernel_spmd

    a = {k: np.asarray(v) for k, v in inputs.items()}
    x = a["x"].astype(np.int32, copy=False)
    half = V // 2
    padded = np.pad(x, ((0, 0), (half, half)), mode="reflect")
    ids_frames = np.ascontiguousarray(
        np.stack([padded[:, f * V:f * V + V] for f in range(FR)], 1).reshape(B * FR, V).T)
    flat = np.pad(x.reshape(-1), (WCTX, WCTX), mode="edge")
    ids_win = np.stack([flat[g * GRP:g * GRP + WIN] for g in range(NG)])
    pw = np.pad(a["L0_tok_proj_w"].reshape(DS, NF, V), ((0, 0), (0, 2 * NFP - NF), (0, 0)))
    pw = np.ascontiguousarray(pw.reshape(DS, NFP, 2, V).transpose(2, 3, 1, 0).reshape(P, NFP, DS))
    bqk = np.ascontiguousarray(np.stack([a["L0_attn_bq"].reshape(2, P), a["L0_attn_bk"].reshape(2, P)]
                                        ).transpose(2, 0, 1))
    b1 = np.ascontiguousarray(a["L0_ffn_b1"].reshape(E, FT, P).transpose(2, 0, 1))
    con, frames_of, masks = constants()
    arrays = {
        "ids_frames": ids_frames, "ids_win": ids_win, "window": a["L0_tok_window"].reshape(V, 1),
        "emb": a["L0_tok_emb_table"], "proj_w": pw, "proj_b": a["L0_tok_proj_b"],
        "wq": a["L0_attn_Wq"], "wk": a["L0_attn_Wk"], "wv": a["L0_attn_Wv"], "bqk": bqk,
        "bv": a["L0_attn_bv"].reshape(1, H), "wr": a["L0_ffn_router_w"], "br": a["L0_ffn_router_b"],
        "w1": a["L0_ffn_w1"], "b1": b1, "w2": a["L0_ffn_w2"], "b2": a["L0_ffn_b2"].reshape(1, E, H),
        "consts": con, "frames_of": frames_of, "masks": masks,
    }
    nc = bacc.Bacc("TRN2", target_bir_lowering=False, num_devices=1)
    aps = [nc.dram_tensor(name, v.shape, mybir.dt.from_np(v.dtype), kind="ExternalInput").ap()
           for name, v in arrays.items()]
    out = nc.dram_tensor("out", (NT, P, H), F32, kind="ExternalOutput").ap()
    build(nc, *aps, out)
    result = run_bass_kernel_spmd(nc, [arrays], core_ids=[0])
    return result.results[0]["out"].reshape(B, L, H)
```

```python
from contextlib import ExitStack

import numpy as np
import concourse.bass as bass
from concourse import mybir

ALU = mybir.AluOpType
ACT = mybir.ActivationFunctionType
AX = mybir.AxisListType
F32 = mybir.dt.float32
F16 = mybir.dt.float16
BF16 = mybir.dt.bfloat16
I32 = mybir.dt.int32

P = 128
B, L = 2, 2048
TOK = B * L
V, NF, FR = 64, 33, 33
H, DE = 256, 179
DS = H - DE
NFP = 17
KZ = V + FR + 1
GRP, NG = 512, TOK // 512
NT = TOK // P
TPG = GRP // P
WCTX = 2
WIN = GRP + 2 * WCTX
KEYS = P + 2 * WCTX
HW = WIN // 2
OW = H + 8 + 1
E, FF = 8, 512
CAP = 1280
ST = CAP // P
HS = ST // 2
HALF = HS * P
CH = HALF // 2
NHALF = 2 * E
FT = FF // P
TC = 8
XR = 4
NV = 5
EPS = 1e-5
DFT_SCALE = 256.0
X_SCALE = 16.0
W_SCALE = 256.0
FRAMES_PER_BANK = 512 // (2 * NFP)

C_DFT = 0
C_IOTA = C_DFT + 4 * NFP
C_PART = C_IOTA + P
C_ID = C_PART + 1
C_TRI = C_ID + P
C_EPS = C_TRI + P
C_SUM = C_EPS + 1
C_SPREAD = C_SUM + NG * (NG + 1)
C_PICK = C_SPREAD + KZ
C_ROW97 = C_PICK + NG
C_TILE = C_ROW97 + KZ
C_TOK = C_TILE + NT
C_RESET = C_TOK + NT
C_PREF = C_RESET + NT
NCONST = C_PREF + E


def wait(eng, sem, value):
    if isinstance(value, int) and value <= 0:
        return
    eng.wait_ge(sem, value)


def wait_apart(eng, sem, value):
    if isinstance(value, int) and value <= 0:
        return
    eng.wait_ge(sem, value)
    if not isinstance(value, int):
        eng.nop(nofuse=True)


def build(nc, ids_frames, ids_win, window, emb, proj_w, proj_b, wq, wk, wv, bqk, bv, wr, br,
          w1, b1, w2, b2, consts, frames_of, masks, out):
    with ExitStack() as ctx:
        def sb(name, shape, dt=F32):
            return ctx.enter_context(nc.sbuf_tensor(name, shape, dt))

        def sem(name):
            return ctx.enter_context(nc.semaphore(name))

        w1s = sb("w1s", [P, 2, E, 2, FF], F16)
        w2s = sb("w2s", [P, 2, E, FT, H], F16)
        b1s = sb("b1s", [P, E, FT])
        b2s = sb("b2s", [2, E, H], F16)
        con = sb("con", [P, NCONST])
        tok_idx = sb("tok_idx", [P, E, ST], I32)
        tok_w = sb("tok_w", [P, E, ST])
        vals = sb("vals", [P, E, NV, NT], BF16)
        pos_lo = sb("pos_lo", [P, E, NT], BF16)
        pos_hi = sb("pos_hi", [P, E, NT], BF16)
        lane_of = sb("lane_of", [P, P, TC], BF16)
        slot_of = sb("slot_of", [P, ST, NT], BF16)
        ident16 = sb("ident16", [P, P], F16)
        notp = sb("notp", [2, 1])
        ones16 = sb("ones16", [2, P], F16)

        reg_h = sb("reg_h", [P, NT * OW])
        reg_z = sb("reg_z", [P, 2 * NG * WIN])
        reg_w = sb("reg_w", [P, 2048])
        reg_a = sb("reg_a", [P, 8960])
        reg_p = sb("reg_p", [P, 2 * TPG * H])

        def carve(region, at, parts, dims, dt=F32, first=0):
            size = {F32: 4, I32: 4, F16: 2, BF16: 2}[dt]
            n = int(np.prod(dims))
            words = (n * size + 3) // 4
            ap = region[first:first + parts, at:at + words]
            if dt != F32:
                ap = ap.bitcast(dt)
            if len(dims) > 1:
                names = [f"d{i}" for i in range(len(dims))]
                ap = ap.rearrange(f"p ({' '.join(names)}) -> p {' '.join(names)}",
                                  **{m: d for m, d in zip(names[1:], dims[1:])})
            return ap

        onehot = carve(reg_h, 0, P, [B * FR, V], F16)
        sq = carve(reg_h, 2112, P, [B * FR, 2, NFP])
        sq_floor = carve(reg_h, 2112, P, [B * FR * NFP])
        m2 = carve(reg_h, 4356, P, [B * FR, NFP])
        root = carve(reg_h, 5478, P, [B * FR, NFP])
        mag = carve(reg_h, 6600, P, [NFP, B * FR])
        pw = carve(reg_a, 0, P, [NFP, DS])
        hc = reg_h[:, :].rearrange("p (t c) -> p t c", c=OW)
        hT = carve(reg_h, 0, P, [2, 2, FT, HALF], F16)
        y = carve(reg_h, 5120, P, [2, HS, H])
        gel = carve(reg_h, 7680, P, [2, CH])
        assert 7680 + 2 * CH <= NT * OW and 6600 + NFP * B * FR <= NT * OW
        zall = carve(reg_z, 0, KZ, [NG, WIN])
        ids = carve(reg_z, NG * WIN, V, [NG, WIN], I32)
        x2 = carve(reg_z, NG * WIN, P, [XR * TPG, 2 * H], F16)
        xg = carve(reg_z, 0, P, [2, HS, 2 * H], F16)
        xT = carve(reg_z, 2560, P, [2, 4, HALF], F16)
        stage1 = carve(reg_w, 0, P, [2, FF])
        stage2 = carve(reg_w, 1024, P, [FT, H])
        oh_lo = carve(reg_w, 0, P, [P, NT], BF16)
        mask = carve(reg_a, 0, P, [4, TPG, KEYS])
        at = 4 * TPG * KEYS

        def work(parts, dims, dt=F32):
            nonlocal at
            ap = carve(reg_a, at, parts, dims, dt)
            at += (int(np.prod(dims)) * (2 if dt in (F16, BF16) else 4) + 3) // 4
            return ap

        u = work(KZ, [WIN])
        zq = work(KZ, [GRP])
        gT = work(KZ, [GRP])
        sm = work(P, [TPG, KEYS])
        pr = work(P, [TPG, KEYS])
        prT = work(P, [GRP])
        prE = work(2 * WCTX, [GRP])
        ut = work(P, [TPG + 1, KZ])
        yT = work(KZ, [GRP])
        zm = work(KZ, [2, HW])
        sd = work(NG + 1, [2, HW])
        rinv = work(NG + 1, [2, HW])
        rpick = work(NG + 1, [2, HW])
        bcur = work(KZ, [KZ])
        mx = work(P, [TPG])
        nmx = work(P, [TPG])
        psum_row = work(P, [TPG])
        prec = work(P, [TPG])
        half_gap = work(P, [TPG])
        var2 = work(P, [TPG])
        sd2 = work(P, [TPG])
        r16 = work(P, [TPG])
        stats = work(P, [TPG, 6])
        assert at <= 8960
        rt = [carve(reg_a, E * NT * i, P, [E, NT]) for i in range(16)]
        rv = [carve(reg_a, E * NT * 16 + NT * i, P, [NT]) for i in range(12)]
        count_b = carve(reg_a, E * NT * 17 + NT * 12, P, [E, NT], BF16)
        tri_b = carve(reg_a, E * NT * 18 + NT * 12, P, [P], BF16)
        ones_b = carve(reg_a, E * NT * 19 + NT * 12, P, [P], BF16)
        eqs = carve(reg_a, E * NT * 20 + NT * 12, P, [ST, NT], BF16)
        rhs_t = carve(reg_a, E * NT * 22 + NT * 12, P, [NV, ST, NT], BF16)
        tab = carve(reg_a, E * NT * 26 + NT * 12, P, [NV, ST])
        posi = carve(reg_a, E * NT * 28 + NT * 12, P, [E, NT], I32)
        wq_s = carve(reg_p, 0, P, [2, H])
        wk_s = carve(reg_p, 512, P, [2, H])
        wv_s = carve(reg_p, 1024, P, [2, H])
        wr_s = sb("wr_s", [P, 2, E])
        ta = sb("ta", [KZ, B, OW])
        tb = sb("tb", [KZ, B, OW])
        tcT = sb("tcT", [P, 2, B, KZ])
        tvT = sb("tvT", [P, 2, B, KZ])
        qT = sb("qT", [P, 2, B, KZ])
        kT = sb("kT", [P, 2, B, KZ])
        ball = sb("ball", [KZ, B, KZ])
        mall = sb("mall", [KZ, B, KZ])
        tmean = sb("tmean", [KZ, 4, B])
        bqk_s = sb("bqk_s", [P, 2, 2])
        br_s = sb("br_s", [P, E])
        win_s = sb("win_s", [P, 1])
        ids_f = carve(reg_h, 7722, P, [B * FR], I32)
        wd = carve(reg_h, 7788, P, [2, 2 * NFP])
        wd_hi = carve(reg_h, 7856, P, [2, 2 * NFP], F16)
        wd16 = carve(reg_h, 7890, P, [2, 2 * NFP], F16)
        bv_s = carve(reg_h, 7924, 1, [H])
        pbs = carve(reg_h, 8180, P, [DS])
        epsr = sb("epsr", [P, 1])
        r2 = sb("r2", [P, NT])
        hout = carve(reg_p, 0, P, [2, TPG, H])
        b2f = carve(reg_p, 0, 2, [E, H])

        bank = [ctx.enter_context(nc.psum_tensor(f"bank{i}", [P, 512], F32)) for i in range(8)]
        bank_s = [bank[0], bank[1]]

        x2_dram = nc.dram_tensor("x2_rows", [TOK, 2 * H], F16, kind="Internal").ap()

        ld_con, ld_ids, ld_emb, ld_pw = sem("ld_con"), sem("ld_ids"), sem("ld_emb"), sem("ld_pw")
        ld_proj, ld_zc, ld_mask = sem("ld_proj"), sem("ld_zc"), sem("ld_mask")
        ld_win, ld_w1, ld_w2, ld_bias = sem("ld_win"), sem("ld_w1"), sem("ld_w2"), sem("ld_bias")
        ld_b2 = sem("ld_b2")
        wd_chain, wd_ready, oh_ready = sem("wd_chain"), sem("wd_ready"), sem("oh_ready")
        dft_done, sq_done, m2_done, root_done, mag_done = (sem(n) for n in (
            "dft_done", "sq_done", "m2_done", "root_done", "mag_done"))
        enc_done, t_zero, t_chain, ta_centred = sem("enc_done"), sem("t_zero"), sem("t_chain"), sem("ta_centred")
        tcT_done, tcT_ready = sem("tcT_done"), sem("tcT_ready")
        m_done, m_ready, q_done, k_done, qk_copied, qk_ready = (sem(n) for n in (
            "m_done", "m_ready", "q_done", "k_done", "qk_copied", "qk_ready"))
        v_done, v_chain, tb_centred, b_done, b_ready = (sem(n) for n in (
            "v_done", "v_chain", "tb_centred", "b_done", "b_ready"))
        tvT_done, tvT_ready, lr_done, tabs_ready = (sem(n) for n in (
            "tvT_done", "tvT_ready", "lr_done", "tabs_ready"))
        z_ready, mz_done, zm_ready, zm_used, sd_ready, rinv_ready, rpick_ready, spread_done = (sem(n) for n in (
            "z_ready", "mz_done", "zm_ready", "zm_used", "sd_ready", "rinv_ready", "rpick_ready", "spread_done"))
        u_ready, g_done, g_ready, s_done, masked, max_ready, nmax_ready = (sem(n) for n in (
            "u_ready", "g_done", "g_ready", "s_done", "masked", "max_ready", "nmax_ready"))
        exp_done, rec_ready, probs_ready, ut_done, ut_ready, pt_done = (sem(n) for n in (
            "exp_done", "rec_ready", "probs_ready", "ut_done", "ut_ready", "pt_done"))
        prT_ready, prE_ready, mix_done, mix_ready, zq_ready, o_done, hc_ready = (sem(n) for n in (
            "prT_ready", "prE_ready", "mix_done", "mix_ready", "zq_ready", "o_done", "hc_ready"))
        stats_ready, var_chain = sem("stats_ready"), sem("var_chain")
        var2_ready, hout_ready, scaled, pair_hi, stage_free = (sem(n) for n in (
            "var2_ready", "hout_ready", "scaled", "pair_hi", "stage_free"))
        sd2_ready, r2_ready, x_hi, x_lo, x2_sent = (sem(n) for n in (
            "sd2_ready", "r2_ready", "x_hi", "x_lo", "x2_sent"))
        rt_chain, logits_ready, exps_ready, counts_ready, ranks_done, vals_ready = (sem(n) for n in (
            "rt_chain", "logits_ready", "exps_ready", "counts_ready", "ranks_done", "vals_ready"))
        eqs_ready, rhs_ready, tab_done, tab_copied, tab_chain, table_ready = (sem(n) for n in (
            "eqs_ready", "rhs_ready", "tab_done", "tab_copied", "tab_chain", "table_ready"))
        idx_ready, xt_done, xt_ready, l1_done, gelu_done, hi_ready, lo_ready = (sem(n) for n in (
            "idx_ready", "xt_done", "xt_ready", "l1_done", "gelu_done", "hi_ready", "lo_ready"))
        y_done, y_ready, b2_hi, b2_ready, misc_ready = (sem(n) for n in (
            "y_done", "y_ready", "b2_hi", "b2_ready", "misc_ready"))
        hout_sent = [sem(f"hout_sent{j}") for j in range(2)]
        gathered = [sem(f"gathered{j}") for j in range(2)]
        scattered = [sem(f"scattered{j}") for j in range(2)]
        gidx = sb("gidx", [P, 2, HS], I32)
        sidx = sb("sidx", [P, 2, HS], I32)

        iota_f = con[:, C_IOTA:C_IOTA + P]
        part_f = con[:, C_PART:C_PART + 1]
        ident = con[:, C_ID:C_ID + P]

        block = ctx.enter_context(nc.Block())

        chunks = [(c, min(FRAMES_PER_BANK, B * FR - c)) for c in range(0, B * FR, FRAMES_PER_BANK)]
        dft_bank = [bank[4], bank[5], bank[6], bank[7], bank[0]]

        @block.sync
        def _(sp):
            for half in range(2):
                sp.dma_start(ids_f[64 * half:64 * half + 64, :], ids_frames).then_inc(ld_ids, 16)
                sp.dma_start(win_s[64 * half:64 * half + 64, :], window).then_inc(ld_ids, 16)
            sp.dma_start(con[:, :], consts).then_inc(ld_con, 16)
            sp.dma_start(ids, ids_win.partition_broadcast(V)).then_inc(ld_win, 16)
            sp.dma_start(pw, proj_w).then_inc(ld_pw, 16)
            sp.dma_start(pbs[V:V + FR, :], proj_b.partition_broadcast(FR)).then_inc(ld_pw, 16)
            sp.dma_start(zall[V:KZ, :, :], frames_of).then_inc(ld_zc, 16)
            for dst, src in ((wq_s, wq), (wk_s, wk), (wv_s, wv), (wr_s[:, :, :], wr)):
                sp.dma_start(dst, src.rearrange("(k p) n -> p k n", p=P)).then_inc(ld_proj, 16)
            sp.dma_start(bqk_s[:, :, :], bqk).then_inc(ld_proj, 16)
            sp.dma_start(bv_s, bv).then_inc(ld_proj, 16)
            sp.dma_start(br_s[:, :], br.partition_broadcast(P)).then_inc(ld_proj, 16)
            sp.dma_start(b1s[:, :, :], b1).then_inc(ld_bias, 16)
            w1_v = w1.rearrange("e (k p) f -> p e k f", p=P)
            w2_v = w2.rearrange("e (k p) f -> p e k f", p=P)

            def stage_weights(e):
                wait(sp, stage_free, 2 * e - 1)
                sl = slice(e, e + 1) if isinstance(e, int) else bass.ds(e, 1)
                sp.dma_start(stage1, w1_v[:, sl, :, :].rearrange("p o k f -> p (o k) f")).then_inc(ld_w1, 16)
                wait(sp, stage_free, 2 * e)
                sp.dma_start(stage2, w2_v[:, sl, :, :].rearrange("p o k f -> p (o k) f")).then_inc(ld_w2, 16)

            stage_weights(0)
            sp.wait_ge(enc_done, 1)
            sp.dma_start(mask, masks).then_inc(ld_mask, 16)
            with sp.Fori(1, E) as e:
                stage_weights(e)

            def send(i):
                for j in range(2):
                    g = 2 * i + j
                    wait_apart(sp, hout_ready, (g + 1) * TPG)
                    sp.dma_start(out[bass.ds(g * TPG, TPG), :, :].rearrange("t p c -> p t c"),
                                 hout[:, j, :, :]).then_inc(hout_sent[j], 16)
                    wait_apart(sp, x_lo, (g + 1) * TPG)
                    wait_apart(sp, x2_sent, 16 * g)
                    sp.dma_start(x2_dram.rearrange("(t p) c -> p t c", p=P)[:, bass.ds(g * TPG, TPG), :],
                                 x2[:, bass.ds((g % XR) * TPG, TPG), :]).then_inc(x2_sent, 16)

            send(0)
            with sp.Fori(1, NG // 2) as i:
                send(i)
            for j in range(2):
                sp.wait_ge(hout_sent[j], 8 * NG)
            for part in range(2):
                sp.dma_start(b2f[part:part + 1, :, :], b2).then_inc(ld_b2, 16)
            sp.wait_ge(x2_sent, 16 * NG)

        @block.gpsimd
        def _(pool):
            nc.gpsimd.memset(ta[:, :, :], 0.0).then_inc(t_zero, 1)
            nc.gpsimd.memset(tb[:, :, :], 0.0).then_inc(t_zero, 1)

            for n in range(2 * E):
                stage, dst = ((stage1, w1s), (stage2, w2s))[n % 2]
                pool.wait_ge(pair_hi, n + 1)
                nc.gpsimd.tensor_tensor(
                    dst[:, 1, n // 2, :, :].rearrange("p k c -> p (k c)"), stage.rearrange("p k c -> p (k c)"),
                    dst[:, 0, n // 2, :, :].rearrange("p k c -> p (k c)"), ALU.subtract).then_inc(stage_free, 1)

            def residual(i, j):
                g = 2 * i + j
                pool.wait_ge(hc_ready, (g + 1) * TPG)
                wait(pool, hout_sent[j], 16 * i)
                for t in range(TPG):
                    tile = g * TPG + t
                    row = hc[:, tile:tile + 1, :] if isinstance(tile, int) else hc[:, bass.ds(tile, 1), :]
                    row = row.rearrange("p o c -> p (o c)")
                    nc.gpsimd.tensor_tensor(hout[:, j, t, :], row[:, 0:H],
                                            row[:, OW - 1:OW].to_broadcast([P, H]), ALU.add).then_inc(hout_ready, 1)

            for j in range(2):
                residual(0, j)
            with pool.Fori(1, NG // 2) as i:
                for j in range(2):
                    residual(i, j)

            def gather(e, h):
                k = 2 * e + h
                pool.wait_ge(table_ready, e + 1)
                wait(pool, gathered[h], 80 * e)
                cols = tok_idx[:, e, HS * h:HS * h + HS] if isinstance(e, int) else \
                    tok_idx[:, bass.ds(e, 1), HS * h:HS * h + HS].rearrange("p o s -> p (o s)")
                nc.gpsimd.tensor_copy(gidx[:, h, :], cols).then_inc(idx_ready, 1)
                wait(pool, xt_done, HS * (k - 1))
                return k

            def send_gather(h, count):
                wait_apart(pool, idx_ready, count)
                for s in range(HS):
                    nc.gpsimd.indirect_dma_start(
                        out=xg[:, h, s, :], out_offset=None, in_=x2_dram,
                        in_offset=bass.IndirectOffsetOnAxis(ap=gidx[:, h, s:s + 1], axis=0)).then_inc(gathered[h], 16)

            def scatter(e, h, count):
                k = 2 * e + h
                wait(pool, scattered[h], 80 * e)
                cols = tok_idx[:, e, HS * h:HS * h + HS] if isinstance(e, int) else \
                    tok_idx[:, bass.ds(e, 1), HS * h:HS * h + HS].rearrange("p o s -> p (o s)")
                nc.gpsimd.tensor_copy(sidx[:, h, :], cols).then_inc(idx_ready, 1)
                if h == 0:
                    wait(pool, scattered[1], 80 * e)
                pool.wait_ge(idx_ready, count)
                for s in range(HS):
                    wait_apart(pool, y_ready, HS * k + s + 1)
                    nc.gpsimd.indirect_dma_start(
                        out=out.rearrange("t p c -> (t p) c"),
                        out_offset=bass.IndirectOffsetOnAxis(ap=sidx[:, h, s:s + 1], axis=0),
                        in_=y[:, h, s, :], in_offset=None, compute_op=ALU.add).then_inc(scattered[h], 16)

            pool.wait_ge(x2_sent, 16 * NG)
            for k in range(4):
                gather(k // 2, k % 2)
                send_gather(k % 2, k + 1)
            for j in range(2):
                pool.wait_ge(hout_sent[j], 8 * NG)

            def step(i, more):
                base = 4 + 4 * i
                scatter(i, 0, base + 1)
                if more:
                    gather(i + 2, 0)
                    send_gather(0, base + 2)
                    gather(i + 2, 1)
                    send_gather(1, base + 3)
                scatter(i, 1, base + (4 if more else 2))

            step(0, True)
            with pool.Fori(1, E - 2) as i:
                step(i, True)
            for i in (E - 2, E - 1):
                base = 4 + 4 * (E - 2) + 2 * (i - (E - 2))
                scatter(i, 0, base + 1)
                scatter(i, 1, base + 2)
            for h in range(2):
                pool.wait_ge(scattered[h], 80 * E)

        @block.scalar
        def _(act):
            for b in range(B):
                act.wait_ge(t_zero, 1)
                act.dma_start(ta[0:V, b, 0:DE], emb).then_inc(ld_emb, 16)
            def pair_high(n):
                stage, dst, ld = ((stage1, w1s, ld_w1), (stage2, w2s, ld_w2))[n % 2]
                e = n // 2
                flat = stage.rearrange("p k c -> p (k c)")
                act.wait_ge(ld, 16 * (e + 1))
                nc.scalar.activation(flat, flat, ACT.Copy, scale=W_SCALE).then_inc(scaled, 1)
                act.wait_ge(scaled, n + 1)
                nc.scalar.activation(dst[:, 0, e, :, :].rearrange("p k c -> p (k c)"), flat,
                                     ACT.Copy).then_inc(pair_hi, 1)

            for c, (first, n) in enumerate(chunks):
                act.wait_ge(dft_done, c + 1)
                nc.scalar.activation(sq[:, first:first + n, :, :].rearrange("p f r j -> p (f r j)"),
                                     dft_bank[c][:, 0:n * 2 * NFP], ACT.Square).then_inc(sq_done, 1)
            act.wait_ge(m2_done, 2)
            nc.scalar.activation(root.rearrange("p f j -> p (f j)"), sq_floor, ACT.Sqrt,
                                 scale=1.0 / DFT_SCALE ** 2).then_inc(root_done, 1)
            pair_high(0)
            pair_high(1)
            act.wait_ge(m_done, 1)
            nc.scalar.activation(mall[:, :, :].rearrange("p b k -> p (b k)"), bank[5][0:KZ, 0:B * KZ],
                                 ACT.Copy).then_inc(m_ready, 1)
            act.wait_ge(q_done, 1)
            nc.scalar.activation(qT[:, :, :, :].rearrange("p j b k -> p (j b k)"), bank[6][:, 0:2 * B * KZ],
                                 ACT.Copy).then_inc(qk_copied, 1)
            act.wait_ge(k_done, 1)
            nc.scalar.activation(kT[:, :, :, :].rearrange("p j b k -> p (j b k)"), bank[7][:, 0:2 * B * KZ],
                                 ACT.Copy).then_inc(qk_copied, 1)
            act.wait_ge(b_done, 1)
            nc.scalar.activation(ball[:, :, :].rearrange("p b k -> p (b k)"), bank[4][0:KZ, 0:B * KZ],
                                 ACT.Copy, scale=H ** -0.5).then_inc(b_ready, 1)
            for n in range(2, 7):
                pair_high(n)
            act.wait_ge(zm_used, NG)
            for hf in range(2):
                nc.scalar.activation(sd[:, hf, :], bank[2 + hf][0:NG + 1, 0:HW], ACT.Sqrt, scale=1.0 / H,
                                     bias=con[0:NG + 1, C_EPS:C_EPS + 1]).then_inc(sd_ready, 1)
            pair_high(7)
            def copy_g(g):
                act.wait_ge(g_done, g + 1)
                nc.scalar.activation(gT, bank[2][0:KZ, :], ACT.Copy).then_inc(g_ready, 1)

            def exps(g, t):
                if t == 0:
                    act.wait_ge(nmax_ready, g + 1)
                    wait(act, pt_done, g)
                nc.scalar.activation(pr[:, t, :], sm[:, t, :], ACT.Exp, bias=nmx[:, t:t + 1],
                                     accum_out=psum_row[:, t:t + 1]).then_inc(exp_done, 1)

            def std2(g):
                act.wait_ge(var2_ready, g + 1)
                nc.scalar.activation(sd2, var2, ACT.Sqrt, scale=1.0 / H, bias=epsr[:, 0:1]).then_inc(sd2_ready, 1)

            def rows_high(g, tiles):
                for t in tiles:
                    if t == 0:
                        act.wait_ge(r2_ready, 2 * (g + 1))
                        wait_apart(act, x2_sent, 16 * (g - XR + 1))
                    n, to = TPG * g + t, (g % XR) * TPG + t
                    if isinstance(g, int):
                        src, dst = hc[:, n, 0:H], x2[:, to, 0:H]
                    else:
                        src = hc[:, bass.ds(n, 1), 0:H].rearrange("p o c -> p (o c)")
                        dst = x2[:, bass.ds(to, 1), 0:H].rearrange("p o c -> p (o c)")
                    nc.scalar.activation(dst, src, ACT.Copy, scale=r16[:, t:t + 1]).then_inc(x_hi, 1)

            def attend(g, more):
                later = not isinstance(g, int) or g >= 1
                if more:
                    copy_g(g + 1)
                if later:
                    std2(g - 1)
                act.wait_ge(pt_done, g + 1)
                wait(act, mix_done, g)
                nc.scalar.activation(prT, bank[3][:, :], ACT.Copy).then_inc(prT_ready, 1)
                if later:
                    rows_high(g - 1, (0, 1))
                act.wait_ge(mix_done, g + 1)
                wait(act, o_done, TPG * g)
                nc.scalar.activation(yT, bank[2][0:KZ, :], ACT.Copy).then_inc(mix_ready, 1)
                for t in range(TPG):
                    if more:
                        exps(g + 1, t)
                    n = TPG * g + t
                    wait_apart(act, o_done, n + 1)
                    row = hc[:, n:n + 1, :] if isinstance(n, int) else hc[:, bass.ds(n, 1), :]
                    nc.scalar.activation(row.rearrange("p o c -> p (o c)"), bank[6 + t % 2][:, 0:OW],
                                         ACT.Copy).then_inc(hc_ready, 1)
                if later:
                    rows_high(g - 1, (2, 3))

            act.wait_ge(misc_ready, 2)
            copy_g(0)
            for t in range(TPG):
                exps(0, t)
            for g in range(XR + 1):
                attend(g, True)
                for n in (8 + 2 * g, 9 + 2 * g):
                    if n < 2 * E:
                        pair_high(n)
            with act.Fori(XR + 1, NG - 1) as g:
                attend(g, True)
            attend(NG - 1, False)
            std2(NG - 1)
            rows_high(NG - 1, range(TPG))
            act.wait_ge(logits_ready, 1)
            nc.scalar.activation(rt[1].rearrange("p e t -> p (e t)"), rt[0].rearrange("p e t -> p (e t)"),
                                 ACT.Exp).then_inc(exps_ready, 1)

            def rows_T(k, par, tiles=range(HS)):
                for s in tiles:
                    act.wait_ge(xt_done, HS * k + s + 1)
                    if s == 0:
                        wait(act, l1_done, 8 * (k - 1))
                    tx = bank[(HS * par + s) % 2][:, 0:256].bitcast(F16).rearrange("p (c n) -> p c n", c=4)
                    nc.scalar.activation(xT[:, par, :, s * P:(s + 1) * P], tx, ACT.Copy).then_inc(xt_ready, 1)

            def gelus(e, par):
                for f in range(FT):
                    for c in range(2):
                        n = 8 * (2 * e + par) + 2 * f + c
                        act.wait_ge(l1_done, n + 1)
                        wait_apart(act, lo_ready, n - 1)
                        bias = b1s[:, e, f:f + 1] if isinstance(e, int) else \
                            b1s[:, bass.ds(e, 1), f:f + 1].rearrange("p o f -> p (o f)")
                        nc.scalar.activation(gel[:, c, :], bank[2 + c][:, 0:CH], ACT.Gelu, bias=bias,
                                             scale=1.0 / (X_SCALE * W_SCALE)).then_inc(gelu_done, 1)

            def weighted(e, par, more):
                k = 2 * e + par
                act.wait_ge(table_ready, e + 1)
                wait(act, scattered[par], 80 * e)
                for s in range(HS):
                    if more:
                        rows_T(k + 2, par, (s,))
                    wait_apart(act, y_done, HS * k + s + 1)
                    col = HS * par + s
                    w_ = tok_w[:, e, col:col + 1] if isinstance(e, int) else \
                        tok_w[:, bass.ds(e, 1), col:col + 1].rearrange("p o s -> p (o s)")
                    nc.scalar.activation(y[:, par, s, :], bank[4 + (HS * par + s) % 2][:, 0:H], ACT.Copy,
                                         scale=w_).then_inc(y_ready, 1)

            rows_T(0, 0)
            act.wait_ge(ld_bias, 16)
            gelus(0, 0)
            rows_T(1, 1)

            def step(i, more):
                gelus(i, 1)
                weighted(i, 0, more)
                if more:
                    gelus(i + 1, 0)
                weighted(i, 1, more)

            step(0, True)
            with act.Fori(1, E - 1) as i:
                step(i, True)
            step(E - 1, False)

        @block.vector
        def _(dve):
            chain = {}

            def then(ins, s):
                chain[id(s)] = chain.get(id(s), 0) + 1
                ins.then_inc(s, 1)
                dve.wait_ge(s, chain[id(s)])

            dve.wait_ge(ld_con, 16)
            dve.wait_ge(ld_ids, 64)
            wdf = wd.rearrange("p a b -> p (a b)")
            then(nc.vector.tensor_scalar(wdf, con[:, C_DFT:C_DFT + 4 * NFP], win_s[:, 0:1], DFT_SCALE,
                                         ALU.mult, ALU.mult), wd_chain)
            then(nc.vector.tensor_copy(wd_hi.rearrange("p a b -> p (a b)"), wdf), wd_chain)
            nc.vector.tensor_copy(wd16[0:V, :, :], wd_hi[0:V, :, :]).then_inc(wd_ready, 1)
            nc.vector.tensor_tensor(wd16[V:P, :, :], wd[V:P, :, :], wd_hi[V:P, :, :],
                                    ALU.subtract).then_inc(wd_ready, 1)
            for first, n in chunks:
                nc.vector.tensor_tensor(
                    onehot[:, first:first + n, :],
                    ids_f[:, first:first + n].unsqueeze(2).to_broadcast([P, n, V]),
                    con[:, C_IOTA:C_IOTA + V].unsqueeze(1).to_broadcast([P, n, V]),
                    ALU.is_equal).then_inc(oh_ready, 1)
            dve.wait_ge(ld_win, 16)
            nc.vector.tensor_scalar(zall[0:V, :, :].rearrange("p g w -> p (g w)"),
                                    ids.rearrange("p g w -> p (g w)"), part_f[0:V, :], None,
                                    ALU.is_equal).then_inc(z_ready, 1)
            nc.vector.memset(epsr[:, :], EPS).then_inc(misc_ready, 1)
            nc.vector.memset(ones16[:, :], X_SCALE).then_inc(misc_ready, 1)
            nc.vector.tensor_copy(lane_of[:, :, :], iota_f.unsqueeze(2).to_broadcast([P, P, TC])
                                  ).then_inc(misc_ready, 1)
            nc.vector.tensor_copy(slot_of[:, :, :], con[:, C_IOTA:C_IOTA + ST].unsqueeze(2).to_broadcast([P, ST, NT])
                                  ).then_inc(misc_ready, 1)
            nc.vector.tensor_copy(ident16[:, :], ident).then_inc(misc_ready, 1)
            dve.wait_ge(sq_done, len(chunks))
            nc.vector.tensor_tensor(m2, sq[:, :, 0, :], sq[:, :, 1, :], ALU.add).then_inc(m2_done, 1)
            dve.wait_ge(m2_done, 1)
            nc.vector.tensor_scalar(sq_floor, m2.rearrange("p f j -> p (f j)"), 1e-30, None,
                                    ALU.max).then_inc(m2_done, 1)
            dve.wait_ge(root_done, 1)
            nc.vector.scalar_tensor_tensor(mag.rearrange("p j f -> p f j"), m2, 0.0, root, ALU.is_gt,
                                           ALU.mult).then_inc(mag_done, 1)
            dve.wait_ge(ld_pw, 32)
            dve.wait_ge(ld_emb, 32)
            dve.wait_ge(t_zero, 2)
            dve.wait_ge(enc_done, 1)
            then(nc.vector.tensor_tensor(ta[V:V + FR, :, DE:H],
                                         bank[1][V:V + FR, 0:B * DS].rearrange("p (b d) -> p b d", b=B),
                                         pbs[V:V + FR, :].unsqueeze(1).to_broadcast([FR, B, DS]),
                                         ALU.add), t_chain)

            def centre(tab_ap, src, m, chain_sem, done):
                then(nc.vector.tensor_reduce(tmean[:, m, :], src, AX.X, ALU.add), chain_sem)
                then(nc.vector.tensor_scalar(tmean[:, m + 1, :], tmean[:, m, :], 1.0 / H, None,
                                             ALU.mult), chain_sem)
                nc.vector.tensor_tensor(tab_ap[:, :, 0:H], src,
                                        tmean[:, m + 1, :].unsqueeze(2).to_broadcast([KZ, B, H]),
                                        ALU.subtract).then_inc(done, 1)
                nc.vector.tensor_copy(tab_ap[:, :, OW - 1], tmean[:, m + 1, :]).then_inc(done, 1)

            centre(ta, ta[:, :, 0:H], 0, t_chain, ta_centred)
            dve.wait_ge(tcT_done, 1)
            nc.vector.tensor_copy(tcT[:, :, :, :].rearrange("p k b z -> p (k b z)"),
                                  bank[4][:, 0:2 * B * KZ]).then_inc(tcT_ready, 1)
            dve.wait_ge(qk_copied, 2)
            dve.wait_ge(ld_proj, 16 * 7)
            for n, dst in enumerate((qT, kT)):
                nc.vector.tensor_copy(dst[:, :, :, KZ - 1],
                                      bqk_s[:, n, :].unsqueeze(2).to_broadcast([P, 2, B])).then_inc(qk_ready, 1)
            dve.wait_ge(v_done, 1)
            centre(tb, bank[5][0:KZ, :].rearrange("p (b c) -> p b c", b=B), 2, v_chain, tb_centred)
            dve.wait_ge(ld_zc, 16)

            def times_z(g):
                dve.wait_ge(mz_done, g + 1)
                if g >= 1:
                    dve.wait_ge(zm_used, g)
                for hf in range(2):
                    nc.vector.tensor_tensor(zm[:, hf, :], bank[hf][0:KZ, 0:HW],
                                            zall[:, g, hf * HW:(hf + 1) * HW], ALU.mult).then_inc(zm_ready, 1)

            for g in range(NG):
                times_z(g)
            dve.wait_ge(tvT_done, 1)
            nc.vector.tensor_copy(tvT[:, :, :, :].rearrange("p k b z -> p (k b z)"),
                                  bank[6][:, 0:2 * B * KZ]).then_inc(tvT_ready, 1)
            dve.wait_ge(sd_ready, 2)
            nc.vector.reciprocal(rinv.rearrange("p h w -> p (h w)"),
                                 sd.rearrange("p h w -> p (h w)")).then_inc(rinv_ready, 1)
            dve.wait_ge(lr_done, 1)
            for n, dst in enumerate((ta, tb)):
                nc.vector.tensor_copy(dst[:, :, H:H + E],
                                      bank[7][0:KZ, n * B * E:(n + 1) * B * E].rearrange(
                                          "p (b e) -> p b e", b=B)).then_inc(tabs_ready, 1)

            def pick(ap, g):
                if isinstance(g, int):
                    return ap[:, g, :]
                return ap[:, bass.ds(g, 1), :].rearrange("p o w -> p (o w)")

            def normed(g):
                dve.wait_ge(b_ready, 1)
                wait(dve, ut_done, g)
                nc.vector.tensor_copy(bcur, pick(ball, g // (NG // B))).then_inc(u_ready, 1)
                dve.wait_ge(spread_done, g + 1)
                for hf in range(2):
                    z_g = zall[:, g, hf * HW:(hf + 1) * HW] if isinstance(g, int) else \
                        zall[:, bass.ds(g, 1), hf * HW:(hf + 1) * HW].rearrange("p o w -> p (o w)")
                    nc.vector.tensor_tensor(u[:, hf * HW:(hf + 1) * HW], z_g, bank[hf][0:KZ, 0:HW],
                                            ALU.mult).then_inc(u_ready, 1)

            def pick_std(g):
                dve.wait_ge(rinv_ready, 1)
                wait(dve, spread_done, g)
                col = con[0:NG + 1, C_PICK + g:C_PICK + g + 1] if isinstance(g, int) else \
                    con[0:NG + 1, bass.ds(C_PICK + g, 1)]
                nc.vector.tensor_scalar(rpick.rearrange("p h w -> p (h w)"), rinv.rearrange("p h w -> p (h w)"),
                                        col, None, ALU.mult).then_inc(rpick_ready, 1)

            def scores(g):
                dve.wait_ge(s_done, g + 1)
                wait(dve, exp_done, TPG * g)
                if isinstance(g, int):
                    m = mask[:, g % 4, :, :]
                else:
                    m = mask[:, bass.ds(g % 4, 1), :, :].rearrange("p o t k -> p (o t) k")
                for hf in range(2):
                    nc.vector.tensor_tensor(sm[:, 2 * hf:2 * hf + 2, :],
                                            bank_s[hf][:, 0:2 * KEYS].rearrange("p (t k) -> p t k", t=2),
                                            m[:, 2 * hf:2 * hf + 2, :], ALU.add).then_inc(masked, 1)

            def maxima(g):
                dve.wait_ge(masked, 2 * (g + 1))
                nc.vector.tensor_reduce(mx, sm, AX.X, ALU.max).then_inc(max_ready, 1)
                dve.wait_ge(max_ready, g + 1)
                nc.vector.tensor_scalar(nmx, mx, -1.0, None, ALU.mult).then_inc(nmax_ready, 1)

            def keys_rows(g):
                dve.wait_ge(ut_done, g + 1)
                wait(dve, mix_done, g)
                nc.vector.tensor_copy(ut[:, 0:TPG, :].rearrange("p t k -> p (t k)"),
                                      bank[5][:, 0:TPG * KZ]).then_inc(ut_ready, 1)
                nc.vector.tensor_copy(ut[0:2 * WCTX, TPG, :],
                                      bank[5][0:2 * WCTX, TPG * KZ:(TPG + 1) * KZ]).then_inc(ut_ready, 1)

            def probs(g):
                dve.wait_ge(exp_done, TPG * (g + 1))
                nc.vector.reciprocal(prec, psum_row).then_inc(rec_ready, 1)
                dve.wait_ge(rec_ready, g + 1)
                nc.vector.tensor_tensor(pr, pr, prec.unsqueeze(2).to_broadcast([P, TPG, KEYS]),
                                        ALU.mult).then_inc(probs_ready, 1)

            def variance(g):
                dve.wait_ge(stats_ready, TPG * (g + 1))
                nc.vector.tensor_tensor(half_gap, stats[:, :, 1], stats[:, :, 4], ALU.subtract
                                        ).then_inc(var_chain, 1)
                nc.vector.tensor_tensor(var2, stats[:, :, 2], stats[:, :, 5], ALU.add).then_inc(var_chain, 1)
                dve.wait_ge(var_chain, 3 * g + 2)
                nc.vector.scalar_tensor_tensor(half_gap, half_gap, H / 4.0, half_gap, ALU.mult,
                                               ALU.mult).then_inc(var_chain, 1)
                dve.wait_ge(var_chain, 3 * g + 3)
                nc.vector.tensor_tensor(var2, var2, half_gap, ALU.add).then_inc(var2_ready, 1)

            def inverse(g):
                dve.wait_ge(sd2_ready, g + 1)
                wait(dve, x_hi, TPG * g)
                dst = r2[:, TPG * g:TPG * (g + 1)] if isinstance(g, int) else r2[:, bass.ds(TPG * g, TPG)]
                nc.vector.reciprocal(dst, sd2).then_inc(r2_ready, 1)
                dve.wait_ge(r2_ready, 2 * g + 1)
                nc.vector.tensor_scalar(r16, dst, X_SCALE, None, ALU.mult).then_inc(r2_ready, 1)

            def rows_low(g, tiles):
                for t in tiles:
                    n, to = TPG * g + t, (g % XR) * TPG + t
                    dve.wait_ge(x_hi, n + 1)
                    if isinstance(g, int):
                        src, row = hc[:, n, 0:H], x2[:, to, :]
                    else:
                        src = hc[:, bass.ds(n, 1), 0:H].rearrange("p o c -> p (o c)")
                        row = x2[:, bass.ds(to, 1), :].rearrange("p o c -> p (o c)")
                    nc.vector.scalar_tensor_tensor(row[:, H:2 * H], src, r16[:, t:t + 1], row[:, 0:H],
                                                   ALU.mult, ALU.subtract).then_inc(x_lo, 1)

            def attend(g, more, more2):
                later = not isinstance(g, int) or g >= 1
                if later:
                    variance(g - 1)
                wait(dve, o_done, TPG * g)
                src = zall[:, g, WCTX:WCTX + GRP] if isinstance(g, int) else \
                    zall[:, bass.ds(g, 1), WCTX:WCTX + GRP].rearrange("p o w -> p (o w)")
                nc.vector.tensor_copy(zq, src).then_inc(zq_ready, 1)
                if more:
                    scores(g + 1)
                if later:
                    inverse(g - 1)
                dve.wait_ge(pt_done, g + 1)
                nc.vector.tensor_copy(prE, bank[4][0:2 * WCTX, :]).then_inc(prE_ready, 1)
                if more2:
                    pick_std(g + 2)
                if more:
                    maxima(g + 1)
                    keys_rows(g + 1)
                if more2:
                    normed(g + 2)
                if later:
                    rows_low(g - 1, (0, 1))
                if more:
                    probs(g + 1)
                for t in range(TPG):
                    n = TPG * g + t
                    dve.wait_ge(hc_ready, n + 1)
                    row = hc[:, n:n + 1, :] if isinstance(n, int) else hc[:, bass.ds(n, 1), :]
                    row = row.rearrange("p o c -> p (o c)")[:, 0:H]
                    nc.vector.bn_stats(stats[:, t, :], row).then_inc(stats_ready, 1)
                if later:
                    rows_low(g - 1, (2, 3))

            pick_std(0)
            normed(0)
            dve.wait_ge(ld_mask, 16)
            scores(0)
            pick_std(1)
            maxima(0)
            keys_rows(0)
            normed(1)
            probs(0)
            attend(0, True, True)
            attend(1, True, True)
            with dve.Fori(2, NG - 2) as g:
                attend(g, True, True)
            attend(NG - 2, True, False)
            attend(NG - 1, False, False)
            variance(NG - 1)
            inverse(NG - 1)
            rows_low(NG - 1, range(TPG))

            def et(v):
                return v.unsqueeze(1).to_broadcast([P, E, NT])

            def te(a):
                return a.rearrange("p e t -> p t e")

            def full(col):
                return con[:, col:col + NT].unsqueeze(1).to_broadcast([P, E, NT])

            tt, ts, red = nc.vector.tensor_tensor, nc.vector.tensor_scalar, nc.vector.tensor_reduce
            stt = nc.vector.scalar_tensor_tensor
            pref = con[:, C_PREF:C_PREF + E].unsqueeze(2).to_broadcast([P, E, NT])
            raw = hc[:, :, H:H + E].rearrange("p t e -> p e t")
            lg, ex, prb, c1, oh1, p2, c2, oh2, wt, cnt, ta_, tb_, incl, rank, alt, tmp = rt
            vm, vs, vr, m1, k1, m2_, k2, den, rden, wa, wb, spare = rv
            then(tt(lg, raw, et(r2[:, :]), ALU.mult), rt_chain)
            then(tt(lg, lg, br_s[:, :].unsqueeze(2).to_broadcast([P, E, NT]), ALU.add), rt_chain)
            then(red(vm, te(lg), AX.X, ALU.max), rt_chain)
            tt(lg, lg, et(vm), ALU.subtract).then_inc(logits_ready, 1)
            dve.wait_ge(exps_ready, 1)
            then(red(vs, te(ex), AX.X, ALU.add), rt_chain)
            then(nc.vector.reciprocal(vr, vs), rt_chain)
            then(tt(prb, ex, et(vr), ALU.mult), rt_chain)

            def top(probs_ap, m, c, k, oh):
                then(red(m, te(probs_ap), AX.X, ALU.max), rt_chain)
                then(tt(c, probs_ap, et(m), ALU.is_equal), rt_chain)
                then(tt(c, c, pref, ALU.mult), rt_chain)
                then(red(k, te(c), AX.X, ALU.max), rt_chain)
                then(tt(oh, c, et(k), ALU.is_equal), rt_chain)

            top(prb, m1, c1, k1, oh1)
            then(stt(p2, oh1, -2.0, prb, ALU.mult, ALU.add), rt_chain)
            top(p2, m2_, c2, k2, oh2)
            then(tt(den, m1, m2_, ALU.add), rt_chain)
            then(ts(den, den, 1e-9, None, ALU.max), rt_chain)
            then(nc.vector.reciprocal(rden, den), rt_chain)
            then(tt(wa, m1, rden, ALU.mult), rt_chain)
            then(tt(wb, m2_, rden, ALU.mult), rt_chain)
            then(tt(cnt, oh1, oh2, ALU.add), rt_chain)
            nc.vector.tensor_copy(count_b, cnt).then_inc(counts_ready, 1)
            nc.vector.tensor_copy(tri_b, con[:, C_TRI:C_TRI + P]).then_inc(counts_ready, 1)
            nc.vector.memset(ones_b, 1.0).then_inc(counts_ready, 1)
            then(tt(wt, oh1, et(wa), ALU.mult), rt_chain)
            then(tt(tmp, oh2, et(wb), ALU.mult), rt_chain)
            then(tt(wt, wt, tmp, ALU.add), rt_chain)
            nc.vector.tensor_copy(vals[:, :, 0, :], part_f.unsqueeze(1).to_broadcast([P, E, NT])
                                  ).then_inc(vals_ready, 1)
            nc.vector.tensor_copy(vals[:, :, 1, :], full(C_TILE)).then_inc(vals_ready, 1)
            then(nc.vector.tensor_copy(vals[:, :, 2, :], wt), rt_chain)
            then(tt(wt, wt, vals[:, :, 2, :], ALU.subtract), rt_chain)
            then(nc.vector.tensor_copy(vals[:, :, 3, :], wt), rt_chain)
            tt(vals[:, :, 4, :], wt, vals[:, :, 3, :], ALU.subtract).then_inc(vals_ready, 1)
            dve.wait_ge(ranks_done, 1)
            per_tile = bank[0][:, 0:E * NT]
            before = bank[0][:, E * NT:2 * E * NT].rearrange("p (e t) -> p e t", e=E)
            then(nc.vector.tensor_copy(ta_, full(C_RESET)), rt_chain)
            then(nc.vector.tensor_tensor_scan(incl.rearrange("p e t -> p (e t)"),
                                              ta_.rearrange("p e t -> p (e t)"), per_tile, 0.0,
                                              ALU.mult, ALU.add), rt_chain)
            then(tt(rank, incl, per_tile.rearrange("p (e t) -> p e t", e=E), ALU.subtract), rt_chain)
            then(tt(rank, rank, before, ALU.add), rt_chain)
            then(tt(alt, full(C_TOK), rank, ALU.subtract), rt_chain)
            then(tt(alt, alt, incl[:, :, NT - 1:NT].to_broadcast([P, E, NT]), ALU.add), rt_chain)
            then(tt(tmp, rank, alt, ALU.subtract), rt_chain)
            then(tt(tmp, tmp, cnt, ALU.mult), rt_chain)
            then(tt(posi, alt, tmp, ALU.add), rt_chain)
            low = tb_.bitcast(I32)
            then(ts(low, posi, P - 1, None, ALU.bitwise_and), rt_chain)
            then(ts(posi, posi, 7, None, ALU.arith_shift_right), rt_chain)
            then(nc.vector.tensor_copy(pos_lo[:, :, :], low), rt_chain)
            then(nc.vector.tensor_copy(pos_hi[:, :, :], posi), rt_chain)

            def of(ap, e):
                one = slice(e, e + 1) if isinstance(e, int) else bass.ds(e, 1)
                if len(ap.shape) == 3:
                    return ap[:, one, :].rearrange("p o a -> p (o a)")
                return ap[:, one, :, :].rearrange("p o a b -> p (o a) b")

            def spread(e):
                wait(dve, tab_done, e)
                lo_e, hi_e = of(pos_lo[:, :, :], e), of(pos_hi[:, :, :], e)
                tt(eqs, hi_e.unsqueeze(1).to_broadcast([P, ST, NT]), slot_of[:, :, :],
                   ALU.is_equal).then_inc(eqs_ready, 1)
                for c in range(0, NT, TC):
                    tt(oh_lo[:, :, c:c + TC], lane_of[:, :, :],
                       lo_e[:, c:c + TC].unsqueeze(1).to_broadcast([P, P, TC]), ALU.is_equal).then_inc(rhs_ready, 1)
                dve.wait_ge(eqs_ready, e + 1)
                tt(rhs_t, of(vals[:, :, :, :], e).unsqueeze(2).to_broadcast([P, NV, ST, NT]),
                   eqs.unsqueeze(1).to_broadcast([P, NV, ST, NT]), ALU.mult).then_inc(rhs_ready, 1)

            def table(e):
                dve.wait_ge(tab_done, e + 1)
                nc.vector.tensor_copy(tab.rearrange("p v s -> p (v s)"),
                                      bank[6][:, 0:NV * ST]).then_inc(tab_copied, 1)
                dve.wait_ge(tab_copied, e + 1)
                stt(of(tok_idx[:, :, :], e), tab[:, 1, :], float(P), tab[:, 0, :], ALU.mult, ALU.add
                    ).then_inc(tab_chain, 1)
                tt(tab[:, 2, :], tab[:, 2, :], tab[:, 3, :], ALU.add).then_inc(tab_chain, 1)
                dve.wait_ge(tab_chain, 3 * e + 2)
                tt(tab[:, 2, :], tab[:, 2, :], tab[:, 4, :], ALU.add).then_inc(tab_chain, 1)
                dve.wait_ge(tab_chain, 3 * e + 3)
                ts(of(tok_w[:, :, :], e), tab[:, 2, :], 1.0 / (X_SCALE * W_SCALE), None, ALU.mult
                   ).then_inc(table_ready, 1)

            dve.wait_ge(stage_free, 2 * E)
            spread(0)
            table(0)
            spread(1)
            table(1)
            dve.wait_ge(ld_b2, 32)
            then(ts(notp[:, :], con[0:2, C_PART:C_PART + 1], -1.0, 1.0, ALU.mult, ALU.add), b2_hi)
            then(ts(b2f[:, :, :], b2f[:, :, :], W_SCALE, None, ALU.mult), b2_hi)
            then(nc.vector.tensor_copy(b2s[:, :, :], b2f[:, :, :]), b2_hi)
            then(tt(b2f[:, :, :], b2f[:, :, :], b2s[:, :, :], ALU.subtract), b2_hi)
            then(ts(b2f[:, :, :], b2f[:, :, :], con[0:2, C_PART:C_PART + 1], None, ALU.mult), b2_hi)
            stt(b2s[:, :, :].rearrange("p e c -> p (e c)"), b2s[:, :, :].rearrange("p e c -> p (e c)"),
                notp[:, 0:1], b2f[:, :, :].rearrange("p e c -> p (e c)"), ALU.mult,
                ALU.add).then_inc(b2_ready, 1)

            def pairs(e, par):
                for f in range(FT):
                    for c in range(2):
                        n = 8 * (2 * e + par) + 2 * f + c
                        dve.wait_ge(gelu_done, n + 1)
                        if f == 0 and c == 0:
                            wait(dve, y_done, HS * (2 * e + par - 1))
                        cols = slice(c * CH, (c + 1) * CH)
                        ts(hT[:, par, 0, f, cols], gel[:, c, :], X_SCALE, None, ALU.mult).then_inc(hi_ready, 1)
                        dve.wait_ge(hi_ready, n + 1)
                        stt(hT[:, par, 1, f, cols], gel[:, c, :], X_SCALE, hT[:, par, 0, f, cols],
                            ALU.mult, ALU.subtract).then_inc(lo_ready, 1)

            def step(i, more, tables):
                pairs(i, 1)
                if tables:
                    spread(i + 2)
                if more:
                    pairs(i + 1, 0)
                if tables:
                    table(i + 2)

            pairs(0, 0)
            step(0, True, True)
            with dve.Fori(1, E - 2) as i:
                step(i, True, True)
            step(E - 2, True, False)
            step(E - 1, False, False)

        @block.tensor
        def _(pe):
            mm = nc.tensor.matmul
            pe.wait_ge(wd_ready, 2)
            for c, (first, n) in enumerate(chunks):
                pe.wait_ge(oh_ready, c + 1)
                for f in range(n):
                    for par in range(2):
                        last = mm(dft_bank[c][64 * par:64 * par + 64, f * 2 * NFP:(f + 1) * 2 * NFP],
                                  onehot[:, first + f, :], wd16[:, par, :], start=True, stop=True)
                last.then_inc(dft_done, 1)
            pe.wait_ge(mag_done, 1)
            pe.wait_ge(ld_pw, 32)
            for b in range(B):
                for j in range(NFP):
                    kk = P if j < NFP - 1 else V
                    last = mm(bank[1][V:V + FR, b * DS:(b + 1) * DS], mag[0:kk, j, b * FR:(b + 1) * FR],
                              pw[0:kk, j, :], start=(j == 0), stop=(j == NFP - 1))
            last.then_inc(enc_done, 1)
            pe.wait_ge(ta_centred, 2)
            for kt in range(2):
                for b in range(B):
                    at_ = (kt * B + b) * KZ
                    last = nc.tensor.transpose(bank[4][:, at_:at_ + KZ], ta[:, b, kt * P:(kt + 1) * P],
                                               ident[0:KZ, 0:KZ])
            last.then_inc(tcT_done, 1)
            pe.wait_ge(tcT_ready, 1)
            for b in range(B):
                for kt in range(2):
                    last = mm(bank[5][0:KZ, b * KZ:(b + 1) * KZ], tcT[:, kt, b, :], tcT[:, kt, b, :],
                              start=(kt == 0), stop=(kt == 1))
            last.then_inc(m_done, 1)
            pe.wait_ge(ld_proj, 16 * 7)
            for w_s, bk, done in ((wq_s, bank[6], q_done), (wk_s, bank[7], k_done)):
                for j in range(2):
                    for kt in range(2):
                        last = mm(bk[:, j * B * KZ:(j + 1) * B * KZ], w_s[:, kt, j * P:(j + 1) * P],
                                  tcT[:, kt, :, :].rearrange("p b z -> p (b z)"), start=(kt == 0), stop=(kt == 1))
                last.then_inc(done, 1)

            def mz(g):
                pe.wait_ge(z_ready, 1)
                pe.wait_ge(ld_zc, 16)
                pe.wait_ge(m_ready, 1)
                if g >= 1:
                    pe.wait_ge(zm_ready, 2 * g)
                for hf in range(2):
                    last = mm(bank[hf][0:KZ, 0:HW], mall[:, g // (NG // B), :],
                              zall[:, g, hf * HW:(hf + 1) * HW], start=True, stop=True)
                last.then_inc(mz_done, 1)

            pe.wait_ge(m_ready, 1)
            for b in range(B):
                for kt in range(2):
                    mm(bank[5][0:KZ, b * H:(b + 1) * H], tcT[:, kt, b, :], wv_s[:, kt, :],
                       start=(kt == 0), stop=False)
                last = mm(bank[5][0:KZ, b * H:(b + 1) * H], con[0:1, C_ROW97:C_ROW97 + KZ], bv_s[0:1, :],
                          start=False, stop=True)
            last.then_inc(v_done, 1)
            mz(0)
            pe.wait_ge(qk_ready, 2)
            for b in range(B):
                for j in range(2):
                    last = mm(bank[4][0:KZ, b * KZ:(b + 1) * KZ], qT[:, j, b, :], kT[:, j, b, :],
                              start=(j == 0), stop=(j == 1))
            last.then_inc(b_done, 1)
            for g in range(NG):
                pe.wait_ge(zm_ready, 2 * (g + 1))
                for hf in range(2):
                    last = mm(bank[2 + hf][0:NG + 1, 0:HW], con[0:KZ, C_SUM + g * (NG + 1):C_SUM + (g + 1) * (NG + 1)],
                              zm[:, hf, :], start=(g == 0), stop=(g == NG - 1))
                last.then_inc(zm_used, 1)
                if g + 1 < NG:
                    mz(g + 1)
                if g == 1:
                    pe.wait_ge(tb_centred, 2)
                    for kt in range(2):
                        for b in range(B):
                            at_ = (kt * B + b) * KZ
                            last = nc.tensor.transpose(bank[6][:, at_:at_ + KZ], tb[:, b, kt * P:(kt + 1) * P],
                                                       ident[0:KZ, 0:KZ])
                    last.then_inc(tvT_done, 1)
            pe.wait_ge(tvT_ready, 1)
            for n, src in enumerate((tcT, tvT)):
                for b in range(B):
                    at_ = (n * B + b) * E
                    for kt in range(2):
                        last = mm(bank[7][0:KZ, at_:at_ + E], src[:, kt, b, :], wr_s[:, kt, :],
                                  start=(kt == 0), stop=(kt == 1))
            last.then_inc(lr_done, 1)

            def front(g):
                pe.wait_ge(u_ready, 3 * (g + 1))
                wait(pe, mix_ready, g - 1)
                mm(bank[2][0:KZ, :], bcur, u[:, WCTX:WCTX + GRP], start=True, stop=True).then_inc(g_done, 1)
                pe.wait_ge(g_ready, g + 1)
                wait(pe, masked, 2 * g)
                for t in range(TPG):
                    last = mm(bank_s[t // 2][:, (t % 2) * KEYS:(t % 2 + 1) * KEYS], gT[:, t * P:(t + 1) * P],
                              u[:, t * P:t * P + KEYS], start=True, stop=True)
                last.then_inc(s_done, 1)
                wait(pe, ut_ready, 2 * g)
                for t in range(TPG):
                    nc.tensor.transpose(bank[5][:, t * KZ:(t + 1) * KZ], u[:, t * P:(t + 1) * P],
                                        ident[0:KZ, 0:KZ])
                nc.tensor.transpose(bank[5][0:2 * WCTX, TPG * KZ:(TPG + 1) * KZ], u[:, GRP:WIN],
                                    ident[0:KZ, 0:KZ]).then_inc(ut_done, 1)

            def spread_std(g):
                pe.wait_ge(rpick_ready, g + 1)
                wait(pe, masked, 2 * g)
                for hf in range(2):
                    last = mm(bank[hf][0:KZ, 0:HW], con[0:NG + 1, C_SPREAD:C_SPREAD + KZ], rpick[:, hf, :],
                              start=True, stop=True)
                last.then_inc(spread_done, 1)

            def back(g, more, more2):
                pe.wait_ge(probs_ready, g + 1)
                wait(pe, prT_ready, g)
                wait(pe, prE_ready, g)
                for t in range(TPG):
                    nc.tensor.transpose(bank[3][:, t * P:(t + 1) * P], pr[:, t, 0:P], ident)
                    last = nc.tensor.transpose(bank[4][0:2 * WCTX, t * P:(t + 1) * P], pr[:, t, P:KEYS], ident)
                last.then_inc(pt_done, 1)
                pe.wait_ge(prT_ready, g + 1)
                pe.wait_ge(prE_ready, g + 1)
                pe.wait_ge(ut_ready, 2 * (g + 1))
                pe.wait_ge(g_ready, g + 2 if more else NG)
                for t in range(TPG):
                    mm(bank[2][0:KZ, t * P:(t + 1) * P], ut[:, t, :], prT[:, t * P:(t + 1) * P],
                       start=True, stop=False)
                    last = mm(bank[2][0:KZ, t * P:(t + 1) * P], ut[0:2 * WCTX, t + 1, :],
                              prE[:, t * P:(t + 1) * P], start=False, stop=True)
                last.then_inc(mix_done, 1)
                if more2:
                    spread_std(g + 2)
                pe.wait_ge(mix_ready, g + 1)
                pe.wait_ge(zq_ready, g + 1)
                if isinstance(g, int):
                    ta_b, tb_b = ta[:, g // (NG // B), :], tb[:, g // (NG // B), :]
                else:
                    ta_b = ta[:, bass.ds(g // (NG // B), 1), :].rearrange("p o c -> p (o c)")
                    tb_b = tb[:, bass.ds(g // (NG // B), 1), :].rearrange("p o c -> p (o c)")
                for t in range(TPG):
                    wait(pe, hc_ready, TPG * g + t - 1)
                    mm(bank[6 + t % 2][:, 0:OW], zq[:, t * P:(t + 1) * P], ta_b, start=True, stop=False)
                    mm(bank[6 + t % 2][:, 0:OW], yT[:, t * P:(t + 1) * P], tb_b, start=False,
                       stop=True).then_inc(o_done, 1)

            pe.wait_ge(tabs_ready, 2)
            spread_std(0)
            front(0)
            spread_std(1)
            front(1)
            back(0, True, True)
            with pe.Fori(1, NG - 2) as g:
                front(g + 1)
                back(g, True, True)
            front(NG - 1)
            back(NG - 2, True, False)
            back(NG - 1, False, False)

            pe.wait_ge(counts_ready, 3)
            cb = count_b.rearrange("p e t -> p (e t)")
            mm(bank[0][:, 0:E * NT], ones_b, cb, start=True, stop=True)
            mm(bank[0][:, E * NT:2 * E * NT], tri_b, cb, start=True, stop=True).then_inc(ranks_done, 1)

            def table(e):
                pe.wait_ge(rhs_ready, (NT // TC + 1) * (e + 1))
                wait(pe, tab_copied, e)
                for t in range(NT):
                    last = mm(bank[6][:, 0:NV * ST], oh_lo[:, :, t],
                              rhs_t.rearrange("p v s t -> p (v s) t")[:, :, t], start=(t == 0), stop=(t == NT - 1))
                last.then_inc(tab_done, 1)

            pe.wait_ge(vals_ready, 3)
            table(0)
            table(1)

            def rows_T(k, par, tiles=range(HS)):
                for s in tiles:
                    if s == 0:
                        pe.wait_ge(gathered[par], 80 * (k // 2 + 1))
                    wait(pe, xt_ready, HS * k + s - 1)
                    tx = bank[(HS * par + s) % 2][:, 0:256].bitcast(F16)
                    for c in range(4):
                        last = nc.tensor.transpose(tx[:, c * P:(c + 1) * P], xg[:, par, s, c * P:(c + 1) * P],
                                                   ident16[:, :])
                    last.then_inc(xt_done, 1)

            def w_cols(w_s, part, e, kt, c0, n):
                if isinstance(e, int):
                    return w_s[:, part, e, kt, c0:c0 + n]
                return w_s[:, part, bass.ds(e, 1), kt, c0:c0 + n].rearrange("p o c -> p (o c)")

            def layer1(e, par):
                k = 2 * e + par
                pe.wait_ge(xt_ready, HS * (k + 1))
                for f in range(FT):
                    for c in range(2):
                        wait(pe, gelu_done, 8 * k + 2 * f + c - 1)
                        for kt in range(2):
                            for wp, xp in ((0, 0), (0, 1), (1, 0)):
                                last = mm(bank[2 + c][:, 0:CH], w_cols(w1s, wp, e, kt, f * P, P),
                                          xT[:, par, 2 * xp + kt, c * CH:(c + 1) * CH],
                                          start=(kt == 0 and wp == 0 and xp == 0), stop=(kt == 1 and wp == 1))
                        last.then_inc(l1_done, 1)

            def layer2(e, par, more):
                k = 2 * e + par
                pe.wait_ge(lo_ready, 8 * (k + 1))
                for s in range(HS):
                    if more:
                        rows_T(k + 2, par, (s,))
                    bk = bank[4 + (HS * par + s) % 2][:, 0:H]
                    wait(pe, y_ready, HS * k + s - 1)
                    for f in range(FT):
                        for hp, wp in ((0, 0), (0, 1), (1, 0)):
                            mm(bk, hT[:, par, hp, f, s * P:(s + 1) * P], w_cols(w2s, wp, e, f, 0, H),
                               start=(f == 0 and hp == 0 and wp == 0), stop=False)
                    b2_e = b2s[:, e, :] if isinstance(e, int) else \
                        b2s[:, bass.ds(e, 1), :].rearrange("p o c -> p (o c)")
                    mm(bk, ones16[:, :], b2_e, start=False, stop=True).then_inc(y_done, 1)

            pe.wait_ge(stage_free, 2 * E)
            pe.wait_ge(misc_ready, 5)
            rows_T(0, 0)
            layer1(0, 0)
            rows_T(1, 1)
            pe.wait_ge(b2_ready, 1)

            def step(i, more, tables):
                layer1(i, 1)
                layer2(i, 0, more)
                if more:
                    layer1(i + 1, 0)
                if tables:
                    table(i + 2)
                layer2(i, 1, more)

            step(0, True, True)
            with pe.Fori(1, E - 2) as i:
                step(i, True, True)
            step(E - 2, True, False)
            step(E - 1, False, False)


def constants():
    con = np.zeros((P, NCONST), np.float32)
    n = np.arange(V)
    dft = np.zeros((V, 2, 2, NFP), np.float64)
    for par in range(2):
        for j in range(NFP):
            f = 2 * j + par
            if f < NF:
                turn = (f * n) % V
                dft[:, par, 0, j] = np.cos(2 * np.pi * turn / V)
                dft[:, par, 1, j] = np.where(turn % (V // 2) == 0, 0.0, -np.sin(2 * np.pi * turn / V))
                dft[:, par, 0, j] = np.where(turn % (V // 2) == V // 4, 0.0, dft[:, par, 0, j])
    con[:, C_DFT:C_DFT + 4 * NFP] = np.tile(dft.reshape(V, -1), (2, 1))
    con[:, C_IOTA:C_IOTA + P] = np.arange(P)
    con[:, C_PART] = np.arange(P)
    con[:, C_ID:C_ID + P] = np.eye(P)
    con[:, C_TRI:C_TRI + P] = np.triu(np.ones((P, P)), 1)
    con[:, C_EPS] = EPS
    con[NG, C_EPS] = 1.0
    for g in range(NG):
        con[:, C_SUM + g * (NG + 1) + g] = 1.0
    con[0:NG, C_SPREAD:C_SPREAD + KZ - 1] = 1.0
    con[NG, C_SPREAD + KZ - 1] = 1.0
    con[0:NG, C_PICK:C_PICK + NG] = np.eye(NG)
    con[NG, C_PICK:C_PICK + NG] = 1.0
    con[0, C_ROW97 + KZ - 1] = 1.0
    con[:, C_TILE:C_TILE + NT] = np.arange(NT)
    con[:, C_TOK:C_TOK + NT] = np.arange(NT) * P + np.arange(P)[:, None]
    con[:, C_RESET:C_RESET + NT] = np.arange(NT) > 0
    con[:, C_PREF:C_PREF + E] = E - np.arange(E)

    t = np.arange(L)
    coord = np.clip((t + 0.5) * (FR / L) - 0.5, 0.0, FR - 1.0)
    i0 = np.floor(coord).astype(np.int64)
    i1 = np.minimum(i0 + 1, FR - 1)
    w = (coord - i0).astype(np.float32)
    z = np.zeros((FR, L), np.float32)
    np.add.at(z, (i0, t), np.float32(1.0) - w)
    np.add.at(z, (i1, t), w)
    frames_of = np.zeros((FR + 1, NG, WIN), np.float32)
    frames_of[FR] = 1.0
    masks = np.full((P, NG // B, TPG, KEYS), -1e30, np.float32)
    for g in range(NG):
        first = (g % (NG // B)) * GRP - WCTX
        for c in range(WIN):
            if 0 <= first + c < L:
                frames_of[:FR, g, c] = z[:, first + c]
    for g in range(NG // B):
        for tile in range(TPG):
            for q in range(P):
                for k in range(q, q + 2 * WCTX + 1):
                    if 0 <= g * GRP + tile * P + k - WCTX < L:
                        masks[q, g, tile, k] = 0.0
    return con, frames_of, masks


def kernel(**inputs):
    import concourse.bacc as bacc
    from concourse.bass_utils import run_bass_kernel_spmd

    a = {k: np.asarray(v) for k, v in inputs.items()}
    x = a["x"].astype(np.int32, copy=False)
    half = V // 2
    padded = np.pad(x, ((0, 0), (half, half)), mode="reflect")
    ids_frames = np.ascontiguousarray(
        np.stack([padded[:, f * V:f * V + V] for f in range(FR)], 1).reshape(B * FR, V).T)
    flat = np.pad(x.reshape(-1), (WCTX, WCTX), mode="edge")
    ids_win = np.stack([flat[g * GRP:g * GRP + WIN] for g in range(NG)])
    pw = np.pad(a["L0_tok_proj_w"].reshape(DS, NF, V), ((0, 0), (0, 2 * NFP - NF), (0, 0)))
    pw = np.ascontiguousarray(pw.reshape(DS, NFP, 2, V).transpose(2, 3, 1, 0).reshape(P, NFP, DS))
    bqk = np.ascontiguousarray(np.stack([a["L0_attn_bq"].reshape(2, P), a["L0_attn_bk"].reshape(2, P)]
                                        ).transpose(2, 0, 1))
    b1 = np.ascontiguousarray(a["L0_ffn_b1"].reshape(E, FT, P).transpose(2, 0, 1))
    con, frames_of, masks = constants()
    arrays = {
        "ids_frames": ids_frames, "ids_win": ids_win, "window": a["L0_tok_window"].reshape(V, 1),
        "emb": a["L0_tok_emb_table"], "proj_w": pw, "proj_b": a["L0_tok_proj_b"],
        "wq": a["L0_attn_Wq"], "wk": a["L0_attn_Wk"], "wv": a["L0_attn_Wv"], "bqk": bqk,
        "bv": a["L0_attn_bv"].reshape(1, H), "wr": a["L0_ffn_router_w"], "br": a["L0_ffn_router_b"],
        "w1": a["L0_ffn_w1"], "b1": b1, "w2": a["L0_ffn_w2"], "b2": a["L0_ffn_b2"].reshape(1, E, H),
        "consts": con, "frames_of": frames_of, "masks": masks,
    }
    nc = bacc.Bacc("TRN2", target_bir_lowering=False, num_devices=1)
    aps = [nc.dram_tensor(name, v.shape, mybir.dt.from_np(v.dtype), kind="ExternalInput").ap()
           for name, v in arrays.items()]
    out = nc.dram_tensor("out", (NT, P, H), F32, kind="ExternalOutput").ap()
    build(nc, *aps, out)
    result = run_bass_kernel_spmd(nc, [arrays], core_ids=[0])
    return result.results[0]["out"].reshape(B, L, H)
```

```python
from contextlib import ExitStack

import numpy as np
import concourse.bass as bass
from concourse import mybir

ALU = mybir.AluOpType
ACT = mybir.ActivationFunctionType
AX = mybir.AxisListType
F32 = mybir.dt.float32
F16 = mybir.dt.float16
BF16 = mybir.dt.bfloat16
I32 = mybir.dt.int32

P = 128
B, L = 2, 2048
TOK = B * L
V, NF, FR = 64, 33, 33
H, DE = 256, 179
DS = H - DE
NFP = 17
KZ = V + FR + 1
GRP, NG = 512, TOK // 512
NT = TOK // P
TPG = GRP // P
WCTX = 2
WIN = GRP + 2 * WCTX
KEYS = P + 2 * WCTX
HW = WIN // 2
OW = H + 8 + 1
E, FF = 8, 512
CAP = 1280
ST = CAP // P
HS = ST // 2
HALF = HS * P
CH = HALF // 2
NHALF = 2 * E
FT = FF // P
STAGES = 10
PEEL = 3
TC = 8
XR = 4
EXTRA = 384
NV = 5
EPS = 1e-5
DFT_SCALE = 256.0
X_SCALE = 16.0
W_SCALE = 256.0
FRAMES_PER_BANK = 512 // (2 * NFP)

C_DFT = 0
C_IOTA = C_DFT + 4 * NFP
C_PART = C_IOTA + P
C_ID = C_PART + 1
C_TRI = C_ID + P
C_SUM = C_TRI + P
C_ROW97 = C_SUM + (NG // 2) ** 2
C_TILE = C_ROW97 + KZ
C_TOK = C_TILE + NT
C_RESET = C_TOK + NT
C_PREF = C_RESET + E * NT
NCONST = C_PREF + E


def wait(eng, sem, value):
    if isinstance(value, int) and value <= 0:
        return
    eng.wait_ge(sem, value)


def wait_apart(eng, sem, value):
    if isinstance(value, int) and value <= 0:
        return
    eng.wait_ge(sem, value)
    if not isinstance(value, int):
        eng.nop(nofuse=True)


def at(ap, i):
    if isinstance(i, int):
        return ap[:, i]
    rest = " ".join("abc"[:len(ap.shape) - 2])
    return ap[:, bass.ds(i, 1)].rearrange(f"p o {rest} -> p (o {rest[0]}){rest[1:]}")


def build(nc, ids_frames, ids_win, window, emb, proj_w, proj_b, wq, wk, wv, bqk, bv, wr, br,
          w1, b1, w2, b2, consts, frames_of, masks, out):
    with ExitStack() as ctx:
        def sb(name, shape, dt=F32):
            return ctx.enter_context(nc.sbuf_tensor(name, shape, dt))

        def sem(name):
            return ctx.enter_context(nc.semaphore(name))

        w1s = sb("w1s", [P, 2, E, 2, FF], F16)
        w2s = sb("w2s", [P, 2, E, FT, H], F16)
        b1s = sb("b1s", [P, E, FT])
        con = sb("con", [P, NCONST])
        tok_idx = sb("tok_idx", [P, E, ST], I32)
        tok_w = sb("tok_w", [P, E, ST])
        vals = sb("vals", [P, E, NV, NT], BF16)
        pos_lo = sb("pos_lo", [P, E, NT], BF16)
        pos_hi = sb("pos_hi", [P, E, NT], BF16)
        lane_of = sb("lane_of", [P, P, TC], BF16)
        slot_of = sb("slot_of", [P, ST, NT], BF16)
        ident16 = sb("ident16", [P, P], F16)
        tri_b = sb("tri_b", [P, P], BF16)
        ones_b = sb("ones_b", [P, P], BF16)
        sixteen = sb("sixteen", [P, TPG])

        reg_h = sb("reg_h", [P, NT * OW])
        reg_z = sb("reg_z", [P, 2 * NG * WIN])
        reg_w = sb("reg_w", [P, 2048])
        reg_a = sb("reg_a", [P, 8960])
        reg_p = sb("reg_p", [P, 2 * TPG * H])

        def carve(region, at, parts, dims, dt=F32, first=0):
            size = {F32: 4, I32: 4, F16: 2, BF16: 2}[dt]
            n = int(np.prod(dims))
            words = (n * size + 3) // 4
            ap = region[first:first + parts, at:at + words]
            if dt != F32:
                ap = ap.bitcast(dt)
            if len(dims) > 1:
                names = [f"d{i}" for i in range(len(dims))]
                ap = ap.rearrange(f"p ({' '.join(names)}) -> p {' '.join(names)}",
                                  **{m: d for m, d in zip(names[1:], dims[1:])})
            return ap

        onehot = carve(reg_h, 0, P, [B * FR, V], F16)
        sq = carve(reg_h, 2112, P, [B * FR, 2, NFP])
        sq_floor = carve(reg_h, 2112, P, [B * FR * NFP])
        m2 = carve(reg_h, 4356, P, [B * FR, NFP])
        root = carve(reg_h, 5478, P, [B * FR, NFP])
        mag = carve(reg_h, 6600, P, [NFP, B * FR])
        pw = carve(reg_a, 0, P, [NFP, DS])
        hc = reg_h[:, :].rearrange("p (t c) -> p t c", c=OW)
        hT = carve(reg_h, 0, P, [2, 2, FT, HALF], F16)
        y = carve(reg_h, 5120, P, [2, HS, H])
        gel = carve(reg_h, 7680, P, [2, CH])
        assert 7680 + 2 * CH <= NT * OW and 6600 + NFP * B * FR <= NT * OW
        zall = carve(reg_z, 0, KZ, [NG, WIN])
        ids = carve(reg_z, NG * WIN, V, [NG, WIN], I32)
        x2 = carve(reg_z, NG * WIN, P, [XR * TPG, 2 * H], F16)
        xg = carve(reg_z, 0, P, [2, HS, 2 * H], F16)
        xT = carve(reg_z, 2560, P, [2, 4, HALF], F16)
        stage = [carve(reg_w, 2 * FF * n, P, [2 * FF]) if n < 2 else
                 carve(reg_h, 2 * FF * (n - 2), P, [2 * FF]) for n in range(STAGES)]
        stage += stage[:2 * E - STAGES]
        oh_lo = carve(reg_w, 0, P, [P, NT], BF16)
        mask = carve(reg_a, 0, P, [4, TPG, KEYS])
        used = 4 * TPG * KEYS

        def work(parts, dims, dt=F32):
            nonlocal used
            ap = carve(reg_a, used, parts, dims, dt)
            used += (int(np.prod(dims)) * (2 if dt in (F16, BF16) else 4) + 3) // 4
            return ap

        u = work(KZ, [WIN])
        zq = work(KZ, [GRP])
        gT = work(KZ, [GRP])
        sm = work(P, [TPG, KEYS])
        pr = work(P, [TPG, KEYS])
        zm, zm_odd = (carve(reg_a, used - k * TPG * KEYS, KZ, [2, HW]) for k in (1, 2))
        prT = work(P, [GRP])
        prE = work(2 * WCTX, [TPG, 32])
        ut = work(P, [TPG + 1, KZ])
        yT = work(KZ, [GRP])
        inv_std = work(KZ, [2, WIN])
        sd = work(NG // 2, [2, HW])
        rinv = work(NG // 2, [2, HW])
        bcur = work(KZ, [KZ])
        mx = work(P, [TPG])
        nmx = work(P, [TPG])
        psum_row = work(P, [TPG])
        prec = work(P, [TPG])
        half_gap = work(P, [TPG])
        var2 = work(P, [TPG])
        seed = work(P, [TPG], I32)
        root_a = work(P, [TPG])
        root_t = work(P, [TPG])
        stats = work(P, [TPG, 6])
        low_tmp = work(P, [H])
        assert used <= 8960
        qT, kT, tvT = (carve(reg_a, 4 * TPG * KEYS + k, P, [2, B, KZ]) for k in (
            WIN + GRP, WIN, WIN + 2 * GRP + 2 * TPG * KEYS))
        rt = [carve(reg_a, E * NT * i, P, [E, NT]) for i in range(14)]
        rv = [carve(reg_a, E * NT * 16 + NT * i, P, [NT]) for i in range(11)]
        count_b = carve(reg_a, E * NT * 17 + NT * 12, P, [E, NT], BF16)
        eqs = carve(reg_a, E * NT * 20 + NT * 12, P, [ST, NT], BF16)
        rhs_t = carve(reg_a, E * NT * 22 + NT * 12, P, [NV, ST, NT], BF16)
        tab = carve(reg_a, E * NT * 26 + NT * 12, P, [NV, ST])
        posi = carve(reg_a, E * NT * 28 + NT * 12, P, [E, NT], I32)
        wq_s = carve(reg_p, 0, P, [2, H])
        wk_s = carve(reg_p, 512, P, [2, H])
        wv_s = carve(reg_p, 1024, P, [2, H])
        wr_s = sb("wr_s", [P, 2, E])
        ta = sb("ta", [KZ, B, OW])
        tb = sb("tb", [KZ, B, OW])
        tcT = sb("tcT", [P, 2, B, KZ])
        ball = sb("ball", [KZ, B, KZ])
        mall = sb("mall", [KZ, B, KZ])
        tmean = sb("tmean", [KZ, 4, B])
        bqk_s = sb("bqk_s", [P, 2, 2])
        br_s = sb("br_s", [P, E])
        win_s = sb("win_s", [P, 1])
        ids_f = carve(reg_h, 7722, P, [B * FR], I32)
        wd = carve(reg_h, 7788, P, [2, 2 * NFP])
        wd_hi = carve(reg_h, 7856, P, [2, 2 * NFP], F16)
        wd16 = carve(reg_h, 7890, P, [2, 2 * NFP], F16)
        bv_s = carve(reg_h, 8192, 1, [H])
        pbs = carve(reg_h, 8192, P, [DS])
        epsr = sb("epsr", [P, 1])
        r16 = sb("r16", [P, NT])
        hout = carve(reg_p, 0, P, [2, TPG, H])
        b2s = carve(reg_p, 0, P, [E, H])

        bank = [ctx.enter_context(nc.psum_tensor(f"bank{i}", [P, 512], F32)) for i in range(8)]
        bank_s = [bank[0], bank[1]]

        x2_dram = nc.dram_tensor("x2_rows", [TOK, 2 * H], F16, kind="Internal").ap()
        inv_dram = nc.dram_tensor("inv_rows", [NG, WIN], F32, kind="Internal").ap()

        ld_con, ld_ids, ld_emb, ld_pw = sem("ld_con"), sem("ld_ids"), sem("ld_emb"), sem("ld_pw")
        ld_proj, ld_zc, ld_mask = sem("ld_proj"), sem("ld_zc"), sem("ld_mask")
        ld_win, ld_bias = sem("ld_win"), sem("ld_bias")
        ld_stage = [sem(f"ld_stage{k}") for k in range(STAGES)]
        ld_b2 = sem("ld_b2")
        wd_chain, wd_ready, oh_ready = sem("wd_chain"), sem("wd_ready"), sem("oh_ready")
        dft_done, sq_done, m2_done, root_done, mag_done = (sem(n) for n in (
            "dft_done", "sq_done", "m2_done", "root_done", "mag_done"))
        enc_done, t_zero, t_chain, ta_centred = sem("enc_done"), sem("t_zero"), sem("t_chain"), sem("ta_centred")
        tcT_done, tcT_ready = sem("tcT_done"), sem("tcT_ready")
        m_done, m_ready, q_done, k_done, qk_copied, qk_ready = (sem(n) for n in (
            "m_done", "m_ready", "q_done", "k_done", "qk_copied", "qk_ready"))
        v_done, v_chain, tb_centred, b_done, b_ready = (sem(n) for n in (
            "v_done", "v_chain", "tb_centred", "b_done", "b_ready"))
        tvT_done, tvT_ready, lr_done, tabs_ready = (sem(n) for n in (
            "tvT_done", "tvT_ready", "lr_done", "tabs_ready"))
        z_ready, mz_done, zm_ready, zm_used, sd_ready, rinv_ready, inv_landed, one_landed = (sem(n) for n in (
            "z_ready", "mz_done", "zm_ready", "zm_used", "sd_ready", "rinv_ready", "inv_landed", "one_landed"))
        u_ready, g_done, g_ready, s_done, masked, max_ready, nmax_ready = (sem(n) for n in (
            "u_ready", "g_done", "g_ready", "s_done", "masked", "max_ready", "nmax_ready"))
        exp_done, rec_ready, probs_ready, ut_done, ut_ready, pt_done = (sem(n) for n in (
            "exp_done", "rec_ready", "probs_ready", "ut_done", "ut_ready", "pt_done"))
        prT_ready, mix_done, mix_ready, zq_ready, o_done, hc_ready = (sem(n) for n in (
            "prT_ready", "mix_done", "mix_ready", "zq_ready", "o_done", "hc_ready"))
        stats_ready, var_chain = sem("stats_ready"), sem("var_chain")
        hout_ready, scaled, pair_hi, stage_free = (sem(n) for n in (
            "hout_ready", "scaled", "pair_hi", "stage_free"))
        seed_ready, var_chain2, newton, x_hi, x_lo, low_chain, rows_sent = (sem(n) for n in (
            "seed_ready", "var_chain2", "newton", "x_hi", "x_lo", "low_chain", "rows_sent"))
        rt_chain, logits_ready, exps_ready, counts_ready, ranks_done, vals_ready = (sem(n) for n in (
            "rt_chain", "logits_ready", "exps_ready", "counts_ready", "ranks_done", "vals_ready"))
        eqs_ready, rhs_ready, tab_done, tab_copied, tab_chain, table_ready = (sem(n) for n in (
            "eqs_ready", "rhs_ready", "tab_done", "tab_copied", "tab_chain", "table_ready"))
        idx_ready, xt_done, xt_ready, l1_done, gelu_done, hi_ready, lo_ready = (sem(n) for n in (
            "idx_ready", "xt_done", "xt_ready", "l1_done", "gelu_done", "hi_ready", "lo_ready"))
        y_done, y_scaled, y_ready, b2_ready, misc_ready = (sem(n) for n in (
            "y_done", "y_scaled", "y_ready", "b2_ready", "misc_ready"))
        hout_sent = [sem(f"hout_sent{j}") for j in range(2)]
        gathered = [[sem(f"gathered{j}_{s}") for s in range(HS)] for j in range(2)]
        scattered = [sem(f"scattered{j}") for j in range(2)]
        gidx = sb("gidx", [P, 2, HS], I32)
        sidx = sb("sidx", [P, 2, HS], I32)

        iota_f = con[:, C_IOTA:C_IOTA + P]
        part_f = con[:, C_PART:C_PART + 1]
        ident = con[:, C_ID:C_ID + P]

        w1_v = w1.rearrange("e (k p) f -> p e k f", p=P)
        w2_v = w2.rearrange("e (k p) f -> p e k f", p=P)

        def load_stage(eng, n):
            src, k = ((w1_v, 2), (w2_v, FT))[n % 2]
            eng.dma_start(stage[n].rearrange("p (k c) -> p k c", k=k), src[:, n // 2, :, :]
                          ).then_inc(ld_stage[n % STAGES], 16)

        block = ctx.enter_context(nc.Block())

        chunks = [(c, min(FRAMES_PER_BANK, B * FR - c)) for c in range(0, B * FR, FRAMES_PER_BANK)]
        dft_bank = [bank[4], bank[5], bank[6], bank[7], bank[0]]

        @block.sync
        def _(sp):
            for half in range(2):
                sp.dma_start(ids_f[64 * half:64 * half + 64, :], ids_frames).then_inc(ld_ids, 16)
                sp.dma_start(win_s[64 * half:64 * half + 64, :], window).then_inc(ld_ids, 16)
            sp.dma_start(con[:, :], consts).then_inc(ld_con, 16)
            sp.dma_start(ids, ids_win.partition_broadcast(V)).then_inc(ld_win, 16)
            sp.dma_start(pw, proj_w).then_inc(ld_pw, 16)
            sp.dma_start(pbs[V:V + FR, :], proj_b.partition_broadcast(FR)).then_inc(ld_pw, 16)
            sp.dma_start(zall[V:KZ, :, :], frames_of).then_inc(ld_zc, 16)
            for dst, src in ((wq_s, wq), (wk_s, wk), (wv_s, wv), (wr_s[:, :, :], wr)):
                sp.dma_start(dst, src.rearrange("(k p) n -> p k n", p=P)).then_inc(ld_proj, 16)
            sp.dma_start(bqk_s[:, :, :], bqk).then_inc(ld_proj, 16)
            sp.dma_start(bv_s, bv).then_inc(ld_proj, 16)
            sp.dma_start(br_s[:, :], br.partition_broadcast(P)).then_inc(ld_proj, 16)
            sp.dma_start(b1s[:, :, :], b1).then_inc(ld_bias, 16)
            load_stage(sp, 0)
            load_stage(sp, 1)
            sp.wait_ge(enc_done, 1)
            for n in range(2, STAGES):
                load_stage(sp, n)
            sp.dma_start(mask, masks).then_inc(ld_mask, 16)
            for n in range(STAGES, 2 * E):
                sp.wait_ge(stage_free, n - STAGES + 1)
                load_stage(sp, n)
            sp.dma_start(inv_std[KZ - 1:KZ, :, :], frames_of[FR:FR + 1, 0:2, :]).then_inc(one_landed, 16)

            def send_inverse(half):
                sp.wait_ge(rinv_ready, half + 1)
                sp.dma_start(inv_dram[half * (NG // 2):(half + 1) * (NG // 2), :],
                             rinv.rearrange("p h w -> p (h w)")).then_inc(rows_sent, 16)
                sp.wait_ge(rows_sent, 16 * (half + 1))

            def spread_inverse(g):
                wait(sp, u_ready, 2 * (g - 1))
                wait(sp, inv_landed, 16 * g)
                src = inv_dram[g:g + 1, :] if isinstance(g, int) else inv_dram[bass.ds(g, 1), :]
                dst = inv_std[0:KZ - 1, g % 2, :] if isinstance(g, int) else \
                    inv_std[0:KZ - 1, bass.ds(g % 2, 1), :].rearrange("p o w -> p (o w)")
                sp.dma_start(dst, src.partition_broadcast(KZ - 1)).then_inc(inv_landed, 16)

            def send_residual(i, j):
                g = 2 * i + j
                wait_apart(sp, hout_ready, (g + 1) * TPG)
                sp.dma_start(out[bass.ds(g * TPG, TPG), :, :].rearrange("t p c -> p t c"),
                             hout[:, j, :, :]).then_inc(hout_sent[j], 16)

            def send_rows(g):
                wait_apart(sp, x_lo, (g + 1) * TPG)
                wait_apart(sp, rows_sent, 16 * (g + 2))
                sp.dma_start(x2_dram.rearrange("(t p) c -> p t c", p=P)[:, bass.ds(g * TPG, TPG), :],
                             x2[:, bass.ds((g % XR) * TPG, TPG), :]).then_inc(rows_sent, 16)

            send_inverse(0)
            spread_inverse(0)
            spread_inverse(1)
            send_inverse(1)
            spread_inverse(2)
            spread_inverse(3)
            for g in range(NG + 2):
                if 4 <= g + 3 < NG:
                    spread_inverse(g + 3)
                if 1 <= g <= NG:
                    send_residual((g - 1) // 2, (g - 1) % 2)
                if g >= 2:
                    send_rows(g - 2)
            for j in range(2):
                sp.wait_ge(hout_sent[j], 8 * NG)
            sp.dma_start(b2s, b2.partition_broadcast(P)).then_inc(ld_b2, 16)
            sp.wait_ge(rows_sent, 16 * (NG + 2))

        @block.gpsimd
        def _(pool):
            nc.gpsimd.memset(ta[:, :, :], 0.0).then_inc(t_zero, 1)
            nc.gpsimd.memset(tb[:, :, :], 0.0).then_inc(t_zero, 1)
            nc.gpsimd.memset(sixteen[:, :], X_SCALE).then_inc(t_zero, 1)

            def pair_low(n):
                dst = (w1s, w2s)[n % 2]
                pool.wait_ge(pair_hi, n + 1)
                nc.gpsimd.tensor_tensor(dst[:, 1, n // 2, :, :].rearrange("p k c -> p (k c)"), stage[n],
                                        dst[:, 0, n // 2, :, :].rearrange("p k c -> p (k c)"),
                                        ALU.subtract).then_inc(stage_free, 1)

            def inverse(g):
                pool.wait_ge(seed_ready, g + 1)
                r = seed.bitcast(F32)
                k = 13 * g
                for it in range(3):
                    if it:
                        pool.wait_ge(newton, k)
                    nc.gpsimd.tensor_tensor(root_t, r, r, ALU.mult).then_inc(newton, 1)
                    pool.wait_ge(newton, k + 1)
                    nc.gpsimd.tensor_tensor(root_t, root_t, var2, ALU.mult).then_inc(newton, 1)
                    pool.wait_ge(newton, k + 2)
                    nc.gpsimd.tensor_scalar(root_t, root_t, -0.5, 1.5, ALU.mult, ALU.add).then_inc(newton, 1)
                    pool.wait_ge(newton, k + 3)
                    nc.gpsimd.tensor_tensor(root_a, r, root_t, ALU.mult).then_inc(newton, 1)
                    r = root_a
                    k = k + 4
                pool.wait_ge(newton, k)
                dst = r16[:, TPG * g:TPG * (g + 1)] if isinstance(g, int) else r16[:, bass.ds(TPG * g, TPG)]
                nc.gpsimd.tensor_tensor(dst, root_a, sixteen[:, :], ALU.mult).then_inc(newton, 1)

            def residual(g, j):
                pool.wait_ge(hc_ready, (g + 1) * TPG)
                wait(pool, hout_sent[j], 8 * (g - j))
                for t in range(TPG):
                    row = at(hc, g * TPG + t)
                    nc.gpsimd.tensor_tensor(hout[:, j, t, :], row[:, 0:H],
                                            row[:, OW - 1:OW].to_broadcast([P, H]), ALU.add).then_inc(hout_ready, 1)

            for n in range(2 * E):
                pair_low(n)
            for g in range(NG):
                inverse(g)
                residual(g, g % 2)
            for n in range(TPG * (NG - 1), NT):
                row = x2[:, n % (XR * TPG), :]
                k = n - TPG * (NG - 1)
                pool.wait_ge(x_hi, n + 1)
                pool.wait_ge(x_lo, n)
                nc.gpsimd.tensor_scalar(low_tmp, hc[:, n, 0:H], r16[:, n:n + 1], None,
                                        ALU.mult).then_inc(low_chain, 1)
                pool.wait_ge(low_chain, k + 1)
                nc.gpsimd.tensor_tensor(row[:, H:2 * H], low_tmp, row[:, 0:H],
                                        ALU.subtract).then_inc(x_lo, 1)

            def gather(e, h):
                k = 2 * e + h
                pool.wait_ge(table_ready, e + 1)
                for s in range(HS):
                    wait(pool, gathered[h][s], 16 * e)
                cols = tok_idx[:, e, HS * h:HS * h + HS] if isinstance(e, int) else \
                    tok_idx[:, bass.ds(e, 1), HS * h:HS * h + HS].rearrange("p o s -> p (o s)")
                nc.gpsimd.tensor_copy(gidx[:, h, :], cols).then_inc(idx_ready, 1)
                wait(pool, xt_done, HS * (k - 1))
                return k

            def send_gather(h, count):
                wait_apart(pool, idx_ready, count)
                for s in range(HS):
                    nc.gpsimd.indirect_dma_start(
                        out=xg[:, h, s, :], out_offset=None, in_=x2_dram,
                        in_offset=bass.IndirectOffsetOnAxis(ap=gidx[:, h, s:s + 1], axis=0)).then_inc(gathered[h][s], 16)

            def scatter(e, h, count):
                k = 2 * e + h
                wait(pool, scattered[h], 80 * e)
                cols = tok_idx[:, e, HS * h:HS * h + HS] if isinstance(e, int) else \
                    tok_idx[:, bass.ds(e, 1), HS * h:HS * h + HS].rearrange("p o s -> p (o s)")
                nc.gpsimd.tensor_copy(sidx[:, h, :], cols).then_inc(idx_ready, 1)
                if h == 0:
                    wait(pool, scattered[1], 80 * e)
                pool.wait_ge(idx_ready, count)
                for s in range(HS):
                    wait_apart(pool, y_ready, HS * k + s + 1)
                    nc.gpsimd.indirect_dma_start(
                        out=out.rearrange("t p c -> (t p) c"),
                        out_offset=bass.IndirectOffsetOnAxis(ap=sidx[:, h, s:s + 1], axis=0),
                        in_=y[:, h, s, :], in_offset=None, compute_op=ALU.add).then_inc(scattered[h], 16)

            pool.wait_ge(rows_sent, 16 * (NG + 2))
            for k in range(4):
                gather(k // 2, k % 2)
                send_gather(k % 2, k + 1)
            for j in range(2):
                pool.wait_ge(hout_sent[j], 8 * NG)

            def step(i, more):
                base = 4 + 4 * i
                scatter(i, 0, base + 1)
                if more:
                    gather(i + 2, 0)
                    send_gather(0, base + 2)
                    gather(i + 2, 1)
                    send_gather(1, base + 3)
                scatter(i, 1, base + (4 if more else 2))

            step(0, True)
            with pool.Fori(1, E - 2) as i:
                step(i, True)
            for i in (E - 2, E - 1):
                base = 4 + 4 * (E - 2) + 2 * (i - (E - 2))
                scatter(i, 0, base + 1)
                scatter(i, 1, base + 2)
            for h in range(2):
                pool.wait_ge(scattered[h], 80 * E)

        @block.scalar
        def _(act):
            for b in range(B):
                act.wait_ge(t_zero, 1)
                act.dma_start(ta[0:V, b, 0:DE], emb).then_inc(ld_emb, 16)
            def pair_high(n):
                act.wait_ge(ld_stage[n % STAGES], 16 * (n // STAGES + 1))
                nc.scalar.activation(stage[n], stage[n], ACT.Copy, scale=W_SCALE).then_inc(scaled, 1)
                act.wait_ge(scaled, n + 1)
                nc.scalar.activation((w1s, w2s)[n % 2][:, 0, n // 2, :, :].rearrange("p k c -> p (k c)"), stage[n],
                                     ACT.Copy).then_inc(pair_hi, 1)

            for c, (first, n) in enumerate(chunks):
                act.wait_ge(dft_done, c + 1)
                nc.scalar.activation(sq[:, first:first + n, :, :].rearrange("p f r j -> p (f r j)"),
                                     dft_bank[c][:, 0:n * 2 * NFP], ACT.Square).then_inc(sq_done, 1)
            act.wait_ge(m2_done, 2)
            nc.scalar.activation(root.rearrange("p f j -> p (f j)"), sq_floor, ACT.Sqrt,
                                 scale=1.0 / DFT_SCALE ** 2).then_inc(root_done, 1)
            pair_high(0)
            pair_high(1)
            act.wait_ge(m_done, 1)
            nc.scalar.activation(mall[:, :, :].rearrange("p b k -> p (b k)"), bank[5][0:KZ, 0:B * KZ],
                                 ACT.Copy).then_inc(m_ready, 1)
            pair_high(2)
            act.wait_ge(q_done, 1)
            nc.scalar.activation(qT[:, :, :, :].rearrange("p j b k -> p (j b k)"), bank[6][:, 0:2 * B * KZ],
                                 ACT.Copy).then_inc(qk_copied, 1)
            act.wait_ge(k_done, 1)
            nc.scalar.activation(kT[:, :, :, :].rearrange("p j b k -> p (j b k)"), bank[7][:, 0:2 * B * KZ],
                                 ACT.Copy).then_inc(qk_copied, 1)
            pair_high(3)
            pair_high(4)
            act.wait_ge(b_done, 1)
            nc.scalar.activation(ball[:, :, :].rearrange("p b k -> p (b k)"), bank[4][0:KZ, 0:B * KZ],
                                 ACT.Copy, scale=H ** -0.5).then_inc(b_ready, 1)
            for half in range(2):
                for n in (range(5, 8), range(8, 12))[half]:
                    pair_high(n)
                act.wait_ge(zm_used, NG // 2 * (half + 1))
                wait(act, rinv_ready, half)
                for hf in range(2):
                    nc.scalar.activation(sd[:, hf, :], bank[2 + hf][0:NG // 2, 0:HW], ACT.Sqrt, scale=1.0 / H,
                                         bias=epsr[0:NG // 2, 0:1]).then_inc(sd_ready, 1)
            def copy_g(g):
                act.wait_ge(g_done, g + 1)
                wait(act, s_done, g)
                nc.scalar.activation(gT, bank[4][0:KZ, :], ACT.Copy).then_inc(g_ready, 1)

            def copy_ut(g):
                act.wait_ge(ut_done, g + 1)
                wait(act, mix_done, g)
                nc.scalar.activation(ut[:, 0:TPG, :].rearrange("p t k -> p (t k)"), bank[5][:, 0:TPG * KZ],
                                     ACT.Copy).then_inc(ut_ready, 1)
                nc.scalar.activation(ut[0:2 * WCTX, TPG, :], bank[5][0:2 * WCTX, TPG * KZ:(TPG + 1) * KZ],
                                     ACT.Copy).then_inc(ut_ready, 1)

            def exps(g, t):
                if t == 0:
                    act.wait_ge(nmax_ready, g + 1)
                    wait(act, pt_done, g)
                nc.scalar.activation(pr[:, t, :], sm[:, t, :], ACT.Exp, bias=nmx[:, t:t + 1],
                                     accum_out=psum_row[:, t:t + 1]).then_inc(exp_done, 1)

            def copy_prT(g):
                act.wait_ge(pt_done, g + 1)
                wait(act, mix_done, g)
                nc.scalar.activation(prT, bank[3][:, :], ACT.Copy).then_inc(prT_ready, 1)
                nc.scalar.activation(prE.rearrange("p t q -> p (t q)"), bank[7][0:2 * WCTX, EXTRA:EXTRA + TPG * 32],
                                     ACT.Copy).then_inc(prT_ready, 1)

            def rows_high(g):
                act.wait_ge(newton, 13 * (g + 1))
                wait_apart(act, rows_sent, 16 * (g - XR + 3))
                for t in range(TPG):
                    n, to = TPG * g + t, (g % XR) * TPG + t
                    scale = r16[:, n:n + 1] if isinstance(n, int) else r16[:, bass.ds(n, 1)]
                    nc.scalar.activation(at(x2, to)[:, 0:H], at(hc, n)[:, 0:H], ACT.Copy,
                                         scale=scale).then_inc(x_hi, 1)

            def attend(g):
                num = isinstance(g, int)
                more, more2 = not num or g + 1 < NG, not num or g + 2 < NG
                act.wait_ge(mix_done, g + 1)
                wait(act, o_done, TPG * g)
                nc.scalar.activation(yT, bank[2][0:KZ, :], ACT.Copy).then_inc(mix_ready, 1)
                if more:
                    copy_ut(g + 1)
                if num and g == 0:
                    act.wait_ge(stage_free, 2 * E)
                for t in range(TPG):
                    if more:
                        exps(g + 1, t)
                    n = TPG * g + t
                    wait_apart(act, o_done, n + 1)
                    nc.scalar.activation(at(hc, n), bank[6 + t % 2][:, 0:OW], ACT.Copy).then_inc(hc_ready, 1)
                if more:
                    copy_prT(g + 1)
                if more2:
                    copy_g(g + 2)
                if not num or g >= 1:
                    rows_high(g - 1)
            copy_g(0)
            pair_high(12)
            copy_ut(0)
            for t in range(TPG):
                exps(0, t)
            pair_high(13)
            copy_prT(0)
            copy_g(1)
            pair_high(14)
            pair_high(15)
            for g in range(PEEL):
                attend(g)
            with act.Fori(PEEL, NG - 2) as g:
                attend(g)
            attend(NG - 2)
            attend(NG - 1)
            rows_high(NG - 1)
            act.wait_ge(logits_ready, 1)
            nc.scalar.activation(rt[1].rearrange("p e t -> p (e t)"), rt[0].rearrange("p e t -> p (e t)"),
                                 ACT.Exp).then_inc(exps_ready, 1)

            def rows_T(k, par, tiles=range(HS)):
                for s in tiles:
                    act.wait_ge(xt_done, HS * k + s + 1)
                    if s == 0:
                        wait(act, l1_done, 8 * (k - 1))
                    tx = bank[(HS * par + s) % 2][:, 0:256].bitcast(F16).rearrange("p (c n) -> p c n", c=4)
                    nc.scalar.activation(xT[:, par, :, s * P:(s + 1) * P], tx, ACT.Copy).then_inc(xt_ready, 1)

            def gelus(e, par):
                for f in range(FT):
                    for c in range(2):
                        n = 8 * (2 * e + par) + 2 * f + c
                        act.wait_ge(l1_done, n + 1)
                        wait_apart(act, lo_ready, n - 1)
                        bias = b1s[:, e, f:f + 1] if isinstance(e, int) else \
                            b1s[:, bass.ds(e, 1), f:f + 1].rearrange("p o f -> p (o f)")
                        nc.scalar.activation(gel[:, c, :], bank[2 + c][:, 0:CH], ACT.Gelu, bias=bias,
                                             scale=1.0 / (X_SCALE * W_SCALE)).then_inc(gelu_done, 1)

            def weighted(e, par, more):
                k = 2 * e + par
                act.wait_ge(table_ready, e + 1)
                wait(act, scattered[par], 80 * e)
                for s in range(HS):
                    if more:
                        rows_T(k + 2, par, (s,))
                    wait_apart(act, y_done, HS * k + s + 1)
                    col = HS * par + s
                    w_ = tok_w[:, e, col:col + 1] if isinstance(e, int) else \
                        tok_w[:, bass.ds(e, 1), col:col + 1].rearrange("p o s -> p (o s)")
                    nc.scalar.activation(y[:, par, s, :], bank[4 + (HS * par + s) % 2][:, 0:H], ACT.Copy,
                                         scale=w_).then_inc(y_scaled, 1)

            rows_T(0, 0)
            act.wait_ge(ld_bias, 16)
            gelus(0, 0)
            rows_T(1, 1)

            def step(i, more):
                gelus(i, 1)
                weighted(i, 0, more)
                if more:
                    gelus(i + 1, 0)
                weighted(i, 1, more)

            step(0, True)
            with act.Fori(1, E - 1) as i:
                step(i, True)
            step(E - 1, False)

        @block.vector
        def _(dve):
            chain = {}

            def then(ins, s):
                chain[id(s)] = chain.get(id(s), 0) + 1
                ins.then_inc(s, 1)
                dve.wait_ge(s, chain[id(s)])

            dve.wait_ge(ld_con, 16)
            dve.wait_ge(ld_ids, 64)
            wdf = wd.rearrange("p a b -> p (a b)")
            then(nc.vector.tensor_scalar(wdf, con[:, C_DFT:C_DFT + 4 * NFP], win_s[:, 0:1], DFT_SCALE,
                                         ALU.mult, ALU.mult), wd_chain)
            then(nc.vector.tensor_copy(wd_hi.rearrange("p a b -> p (a b)"), wdf), wd_chain)
            nc.vector.tensor_copy(wd16[0:V, :, :], wd_hi[0:V, :, :]).then_inc(wd_ready, 1)
            nc.vector.tensor_tensor(wd16[V:P, :, :], wd[V:P, :, :], wd_hi[V:P, :, :],
                                    ALU.subtract).then_inc(wd_ready, 1)
            for first, n in chunks:
                nc.vector.tensor_tensor(
                    onehot[:, first:first + n, :],
                    ids_f[:, first:first + n].unsqueeze(2).to_broadcast([P, n, V]),
                    con[:, C_IOTA:C_IOTA + V].unsqueeze(1).to_broadcast([P, n, V]),
                    ALU.is_equal).then_inc(oh_ready, 1)
            dve.wait_ge(ld_win, 16)
            nc.vector.tensor_scalar(zall[0:V, :, :].rearrange("p g w -> p (g w)"),
                                    ids.rearrange("p g w -> p (g w)"), part_f[0:V, :], None,
                                    ALU.is_equal).then_inc(z_ready, 1)
            nc.vector.memset(epsr[:, :], EPS).then_inc(misc_ready, 1)
            nc.vector.tensor_copy(lane_of[:, :, :], iota_f.unsqueeze(2).to_broadcast([P, P, TC])
                                  ).then_inc(misc_ready, 1)
            nc.vector.tensor_copy(slot_of[:, :, :], con[:, C_IOTA:C_IOTA + ST].unsqueeze(2).to_broadcast([P, ST, NT])
                                  ).then_inc(misc_ready, 1)
            nc.vector.tensor_copy(ident16[:, :], ident).then_inc(misc_ready, 1)
            nc.vector.tensor_copy(tri_b[:, :], con[:, C_TRI:C_TRI + P]).then_inc(misc_ready, 1)
            nc.vector.memset(ones_b[:, :], 1.0).then_inc(misc_ready, 1)
            nc.vector.tensor_copy(vals[:, :, 0, :], part_f.unsqueeze(1).to_broadcast([P, E, NT])
                                  ).then_inc(vals_ready, 1)
            nc.vector.tensor_copy(vals[:, :, 1, :], con[:, C_TILE:C_TILE + NT].unsqueeze(1).to_broadcast([P, E, NT])
                                  ).then_inc(vals_ready, 1)
            dve.wait_ge(sq_done, len(chunks))
            nc.vector.tensor_tensor(m2, sq[:, :, 0, :], sq[:, :, 1, :], ALU.add).then_inc(m2_done, 1)
            dve.wait_ge(m2_done, 1)
            nc.vector.tensor_scalar(sq_floor, m2.rearrange("p f j -> p (f j)"), 1e-30, None,
                                    ALU.max).then_inc(m2_done, 1)
            dve.wait_ge(root_done, 1)
            nc.vector.scalar_tensor_tensor(mag.rearrange("p j f -> p f j"), m2, 0.0, root, ALU.is_gt,
                                           ALU.mult).then_inc(mag_done, 1)
            dve.wait_ge(ld_pw, 32)
            dve.wait_ge(ld_emb, 32)
            dve.wait_ge(t_zero, 3)
            dve.wait_ge(enc_done, 1)
            then(nc.vector.tensor_tensor(ta[V:V + FR, :, DE:H],
                                         bank[1][V:V + FR, 0:B * DS].rearrange("p (b d) -> p b d", b=B),
                                         pbs[V:V + FR, :].unsqueeze(1).to_broadcast([FR, B, DS]),
                                         ALU.add), t_chain)

            def centre(tab_ap, src, m, chain_sem, done):
                then(nc.vector.tensor_reduce(tmean[:, m, :], src, AX.X, ALU.add), chain_sem)
                then(nc.vector.tensor_scalar(tmean[:, m + 1, :], tmean[:, m, :], 1.0 / H, None,
                                             ALU.mult), chain_sem)
                nc.vector.tensor_tensor(tab_ap[:, :, 0:H], src,
                                        tmean[:, m + 1, :].unsqueeze(2).to_broadcast([KZ, B, H]),
                                        ALU.subtract).then_inc(done, 1)
                nc.vector.tensor_copy(tab_ap[:, :, OW - 1], tmean[:, m + 1, :]).then_inc(done, 1)

            centre(ta, ta[:, :, 0:H], 0, t_chain, ta_centred)
            dve.wait_ge(tcT_done, 1)
            nc.vector.tensor_copy(tcT[:, :, :, :].rearrange("p k b z -> p (k b z)"),
                                  bank[4][:, 0:2 * B * KZ]).then_inc(tcT_ready, 1)
            dve.wait_ge(qk_copied, 2)
            dve.wait_ge(ld_proj, 16 * 7)
            for n, dst in enumerate((qT, kT)):
                nc.vector.tensor_copy(dst[:, :, :, KZ - 1],
                                      bqk_s[:, n, :].unsqueeze(2).to_broadcast([P, 2, B])).then_inc(qk_ready, 1)
            dve.wait_ge(ld_zc, 16)

            def times_z(g):
                dve.wait_ge(mz_done, g + 1)
                if g >= 2:
                    dve.wait_ge(zm_used, g - 1)
                bk, to = ((0, zm), (6, zm_odd))[g % 2]
                for hf in range(2):
                    nc.vector.tensor_tensor(to[:, hf, :], bank[bk + hf][0:KZ, 0:HW],
                                            zall[:, g, hf * HW:(hf + 1) * HW], ALU.mult).then_inc(zm_ready, 1)

            def invert(half):
                dve.wait_ge(sd_ready, 2 * (half + 1))
                wait(dve, rows_sent, 16 * half)
                nc.vector.reciprocal(rinv.rearrange("p h w -> p (h w)"),
                                     sd.rearrange("p h w -> p (h w)")).then_inc(rinv_ready, 1)

            times_z(0)
            dve.wait_ge(v_done, 1)
            centre(tb, bank[5][0:KZ, :].rearrange("p (b c) -> p b c", b=B), 2, v_chain, tb_centred)
            for g in range(1, 6):
                times_z(g)
            invert(0)
            dve.wait_ge(tvT_done, 1)
            nc.vector.tensor_copy(tvT[:, :, :, :].rearrange("p k b z -> p (k b z)"),
                                  bank[5][:, 0:2 * B * KZ]).then_inc(tvT_ready, 1)
            times_z(6)
            times_z(7)

            def normed(g):
                dve.wait_ge(b_ready, 1)
                wait(dve, ut_done, g)
                nc.vector.tensor_copy(bcur, at(ball, g // (NG // B))).then_inc(u_ready, 1)
                dve.wait_ge(one_landed, 16)
                dve.wait_ge(inv_landed, 16 * (g + 1))
                nc.vector.tensor_tensor(u, at(zall, g), at(inv_std, g % 2), ALU.mult).then_inc(u_ready, 1)

            def scores(g):
                dve.wait_ge(s_done, g + 1)
                wait(dve, exp_done, TPG * g)
                m = at(mask, g % 4)
                for hf in range(2):
                    nc.vector.tensor_tensor(sm[:, 2 * hf:2 * hf + 2, :],
                                            bank_s[hf][:, 0:2 * KEYS].rearrange("p (t k) -> p t k", t=2),
                                            m[:, 2 * hf:2 * hf + 2, :], ALU.add).then_inc(masked, 1)
                dve.wait_ge(masked, 2 * (g + 1))
                nc.vector.tensor_reduce(mx, sm, AX.X, ALU.max).then_inc(max_ready, 1)
                dve.wait_ge(max_ready, g + 1)
                nc.vector.tensor_scalar(nmx, mx, -1.0, None, ALU.mult).then_inc(nmax_ready, 1)

            def probs(g):
                dve.wait_ge(exp_done, TPG * (g + 1))
                nc.vector.reciprocal(prec, psum_row).then_inc(rec_ready, 1)
                dve.wait_ge(rec_ready, g + 1)
                nc.vector.tensor_tensor(pr, pr, prec.unsqueeze(2).to_broadcast([P, TPG, KEYS]),
                                        ALU.mult).then_inc(probs_ready, 1)

            def queries(g):
                wait(dve, o_done, TPG * g)
                nc.vector.tensor_copy(zq, at(zall, g)[:, WCTX:WCTX + GRP]).then_inc(zq_ready, 1)

            def spreads(g):
                for t in range(TPG):
                    n = TPG * g + t
                    dve.wait_ge(hc_ready, n + 1)
                    if t == 0:
                        wait(dve, var_chain, 4 * g)
                    nc.vector.bn_stats(stats[:, t, :], at(hc, n)[:, 0:H]).then_inc(stats_ready, 1)

            def variance(g):
                dve.wait_ge(stats_ready, TPG * (g + 1))
                wait(dve, newton, 13 * g)
                nc.vector.tensor_tensor(half_gap, stats[:, :, 1], stats[:, :, 4], ALU.subtract
                                        ).then_inc(var_chain, 1)
                nc.vector.tensor_tensor(var2, stats[:, :, 2], stats[:, :, 5], ALU.add).then_inc(var_chain, 1)
                dve.wait_ge(var_chain, 4 * g + 2)
                nc.vector.scalar_tensor_tensor(half_gap, half_gap, H / 4.0, half_gap, ALU.mult,
                                               ALU.mult).then_inc(var_chain, 1)
                dve.wait_ge(var_chain, 4 * g + 3)
                nc.vector.tensor_tensor(var2, var2, half_gap, ALU.add).then_inc(var_chain, 1)
                dve.wait_ge(var_chain, 4 * g + 4)
                nc.vector.tensor_scalar(var2, var2, 1.0 / H, EPS, ALU.mult, ALU.add).then_inc(var_chain2, 1)
                dve.wait_ge(var_chain2, g + 1)
                nc.vector.tensor_scalar(seed, var2.bitcast(I32), -0.5, float(0x5f3759df), ALU.mult,
                                        ALU.add).then_inc(seed_ready, 1)

            def rows_low(g, tiles):
                for t in tiles:
                    n, to = TPG * g + t, (g % XR) * TPG + t
                    dve.wait_ge(x_hi, n + 1)
                    scale = r16[:, n:n + 1] if isinstance(n, int) else r16[:, bass.ds(n, 1)]
                    row = at(x2, to)
                    nc.vector.scalar_tensor_tensor(row[:, H:2 * H], at(hc, n)[:, 0:H], scale, row[:, 0:H],
                                                   ALU.mult, ALU.subtract).then_inc(x_lo, 1)

            def attend(g):
                num = isinstance(g, int)
                more, more2, low = not num or g + 1 < NG, not num or g + 2 < NG, not num or g >= 2
                if more:
                    scores(g + 1)
                if more2:
                    normed(g + 2)
                if low:
                    rows_low(g - 2, (0, 1))
                if more:
                    probs(g + 1)
                spreads(g)
                variance(g)
                if more:
                    queries(g + 1)
                if low:
                    rows_low(g - 2, (2, 3))

            normed(0)
            dve.wait_ge(lr_done, 1)
            for n, dst in enumerate((ta, tb)):
                nc.vector.tensor_copy(dst[:, :, H:H + E],
                                      bank[3][0:KZ, n * B * E:(n + 1) * B * E].rearrange(
                                          "p (b e) -> p b e", b=B)).then_inc(tabs_ready, 1)
            invert(1)
            dve.wait_ge(ld_mask, 16)
            scores(0)
            normed(1)
            queries(0)
            probs(0)
            for g in range(PEEL):
                attend(g)
            with dve.Fori(PEEL, NG - 2) as g:
                attend(g)
            attend(NG - 2)
            attend(NG - 1)
            rows_low(NG - 2, range(TPG))
            dve.wait_ge(newton, 13 * NG)

            def et(v):
                return v.unsqueeze(1).to_broadcast([P, E, NT])

            def te(a):
                return a.rearrange("p e t -> p t e")

            steps = [0]

            def step(ins):
                ins.then_inc(rt_chain, 1)
                steps[0] += 1
                return steps[0]

            tt, ts, red = nc.vector.tensor_tensor, nc.vector.tensor_scalar, nc.vector.tensor_reduce
            stt, copy = nc.vector.scalar_tensor_tensor, nc.vector.tensor_copy
            pref = con[:, C_PREF:C_PREF + E].unsqueeze(2).to_broadcast([P, E, NT])
            half_tok = con[:, C_TOK:C_TOK + NT].unsqueeze(1).to_broadcast([P, E, NT])
            raw = hc[:, :, H:H + E].rearrange("p t e -> p e t")
            (lg, ex, c1, oh1, p2, c2, oh2, wt_a, wt_b, sgn, incl, rank, mid, gap) = rt
            (vm, vs, vr, k1, m2_, k2, p2_, den, rden, wa, wb) = rv
            done = step(stt(lg, raw, 1.0 / X_SCALE, et(r16[:, :]), ALU.mult, ALU.mult))
            dve.wait_ge(rt_chain, done)
            done = step(tt(lg, lg, br_s[:, :].unsqueeze(2).to_broadcast([P, E, NT]), ALU.add))
            dve.wait_ge(rt_chain, done)
            done = step(red(vm, te(lg), AX.X, ALU.max))
            dve.wait_ge(rt_chain, done)
            tt(lg, lg, et(vm), ALU.subtract).then_inc(logits_ready, 1)
            dve.wait_ge(logits_ready, 1)
            done = step(stt(c1, lg, 0.0, pref, ALU.is_ge, ALU.mult))
            dve.wait_ge(rt_chain, done)
            done = step(red(k1, te(c1), AX.X, ALU.max))
            dve.wait_ge(rt_chain, done)
            done = step(tt(oh1, c1, et(k1), ALU.is_equal))
            dve.wait_ge(rt_chain, done)
            dve.wait_ge(exps_ready, 1)
            done = step(stt(p2, oh1, -2.0, ex, ALU.mult, ALU.add))
            sum_done = step(red(vs, te(ex), AX.X, ALU.add))
            dve.wait_ge(rt_chain, done)
            m2_done_ = step(red(m2_, te(p2), AX.X, ALU.max))
            dve.wait_ge(rt_chain, sum_done)
            vr_done = step(nc.vector.reciprocal(vr, vs))
            dve.wait_ge(rt_chain, m2_done_)
            done = step(tt(c2, p2, et(m2_), ALU.is_equal))
            dve.wait_ge(rt_chain, vr_done)
            p2_done = step(tt(p2_, m2_, vr, ALU.mult))
            dve.wait_ge(rt_chain, done)
            done = step(tt(c2, c2, pref, ALU.mult))
            dve.wait_ge(rt_chain, p2_done)
            den_done = step(tt(den, vr, p2_, ALU.add))
            dve.wait_ge(rt_chain, done)
            done = step(red(k2, te(c2), AX.X, ALU.max))
            dve.wait_ge(rt_chain, den_done)
            den_done = step(ts(den, den, 1e-9, None, ALU.max))
            dve.wait_ge(rt_chain, done)
            done = step(tt(oh2, c2, et(k2), ALU.is_equal))
            dve.wait_ge(rt_chain, den_done)
            rden_done = step(nc.vector.reciprocal(rden, den))
            dve.wait_ge(rt_chain, done)
            tt(count_b, oh1, oh2, ALU.add).then_inc(counts_ready, 1)
            dve.wait_ge(rt_chain, rden_done)
            step(tt(wa, vr, rden, ALU.mult))
            wb_done = step(tt(wb, p2_, rden, ALU.mult))
            both_done = step(tt(sgn, oh1, oh2, ALU.add))
            dve.wait_ge(rt_chain, wb_done)
            step(tt(wt_a, oh1, et(wa), ALU.mult))
            wt_done = step(tt(wt_b, oh2, et(wb), ALU.mult))
            dve.wait_ge(rt_chain, both_done)
            sgn_done = step(ts(sgn, sgn, 2.0, -1.0, ALU.mult, ALU.add))
            dve.wait_ge(rt_chain, wt_done)
            wt_done = step(tt(wt_a, wt_a, wt_b, ALU.add))
            dve.wait_ge(ranks_done, 1)
            per_tile = bank[0][:, 0:E * NT]
            not_before = bank[0][:, E * NT:2 * E * NT].rearrange("p (e t) -> p e t", e=E)
            incl_done = step(nc.vector.tensor_tensor_scan(incl.rearrange("p e t -> p (e t)"),
                                                          con[:, C_RESET:C_RESET + E * NT], per_tile, 0.0,
                                                          ALU.mult, ALU.add))
            dve.wait_ge(rt_chain, wt_done)
            w_done = step(copy(vals[:, :, 2, :], wt_a))
            dve.wait_ge(rt_chain, incl_done)
            rank_done = step(tt(rank, incl, not_before, ALU.add))
            mid_done = step(stt(mid, incl[:, :, NT - 1:NT].to_broadcast([P, E, NT]), 0.5, half_tok,
                                ALU.mult, ALU.add))
            dve.wait_ge(rt_chain, w_done)
            w_done = step(tt(wt_a, wt_a, vals[:, :, 2, :], ALU.subtract))
            dve.wait_ge(rt_chain, mid_done)
            gap_done = step(tt(gap, rank, mid, ALU.subtract))
            dve.wait_ge(rt_chain, w_done)
            w_done = step(copy(vals[:, :, 3, :], wt_a))
            dve.wait_ge(rt_chain, gap_done)
            gap_done = step(tt(gap, gap, sgn, ALU.mult))
            dve.wait_ge(rt_chain, w_done)
            tt(vals[:, :, 4, :], wt_a, vals[:, :, 3, :], ALU.subtract).then_inc(vals_ready, 1)
            dve.wait_ge(rt_chain, gap_done)
            done = step(tt(posi, mid, gap, ALU.add))
            dve.wait_ge(rt_chain, done)
            low, high = rank.bitcast(I32), gap.bitcast(I32)
            low_done = step(ts(low, posi, P - 1, None, ALU.bitwise_and))
            high_done = step(ts(high, posi, 7, None, ALU.arith_shift_right))
            dve.wait_ge(rt_chain, low_done)
            step(copy(pos_lo[:, :, :], low))
            dve.wait_ge(rt_chain, high_done)
            done = step(copy(pos_hi[:, :, :], high))
            dve.wait_ge(rt_chain, done)
            dve.wait_ge(vals_ready, 3)

            def of(ap, e):
                one = slice(e, e + 1) if isinstance(e, int) else bass.ds(e, 1)
                if len(ap.shape) == 3:
                    return ap[:, one, :].rearrange("p o a -> p (o a)")
                return ap[:, one, :, :].rearrange("p o a b -> p (o a) b")

            def spread(e):
                wait(dve, tab_done, e)
                lo_e, hi_e = of(pos_lo[:, :, :], e), of(pos_hi[:, :, :], e)
                tt(eqs, hi_e.unsqueeze(1).to_broadcast([P, ST, NT]), slot_of[:, :, :],
                   ALU.is_equal).then_inc(eqs_ready, 1)
                dve.wait_ge(eqs_ready, e + 1)
                tt(rhs_t, of(vals[:, :, :, :], e).unsqueeze(2).to_broadcast([P, NV, ST, NT]),
                   eqs.unsqueeze(1).to_broadcast([P, NV, ST, NT]), ALU.mult).then_inc(rhs_ready, 1)
                for c in range(0, NT, TC):
                    tt(oh_lo[:, :, c:c + TC], lane_of[:, :, :],
                       lo_e[:, c:c + TC].unsqueeze(1).to_broadcast([P, P, TC]), ALU.is_equal).then_inc(rhs_ready, 1)

            def table(e):
                dve.wait_ge(tab_done, e + 1)
                nc.vector.tensor_copy(tab.rearrange("p v s -> p (v s)"),
                                      bank[6][:, 0:NV * ST]).then_inc(tab_copied, 1)
                dve.wait_ge(tab_copied, e + 1)
                stt(of(tok_idx[:, :, :], e), tab[:, 1, :], float(P), tab[:, 0, :], ALU.mult, ALU.add
                    ).then_inc(tab_chain, 1)
                tt(tab[:, 2, :], tab[:, 2, :], tab[:, 3, :], ALU.add).then_inc(tab_chain, 1)
                dve.wait_ge(tab_chain, 3 * e + 2)
                tt(tab[:, 2, :], tab[:, 2, :], tab[:, 4, :], ALU.add).then_inc(tab_chain, 1)
                dve.wait_ge(tab_chain, 3 * e + 3)
                ts(of(tok_w[:, :, :], e), tab[:, 2, :], 1.0 / (X_SCALE * W_SCALE), None, ALU.mult
                   ).then_inc(table_ready, 1)

            dve.wait_ge(stage_free, 2 * E)
            spread(0)
            table(0)
            spread(1)
            table(1)
            dve.wait_ge(ld_b2, 16)
            ts(b2s, b2s, X_SCALE * W_SCALE, None, ALU.mult).then_inc(b2_ready, 1)

            def pairs(e, par):
                for f in range(FT):
                    for c in range(2):
                        n = 8 * (2 * e + par) + 2 * f + c
                        dve.wait_ge(gelu_done, n + 1)
                        if f == 0 and c == 0:
                            wait(dve, y_done, HS * (2 * e + par - 1))
                        cols = slice(c * CH, (c + 1) * CH)
                        ts(hT[:, par, 0, f, cols], gel[:, c, :], X_SCALE, None, ALU.mult).then_inc(hi_ready, 1)
                        dve.wait_ge(hi_ready, n + 1)
                        stt(hT[:, par, 1, f, cols], gel[:, c, :], X_SCALE, hT[:, par, 0, f, cols],
                            ALU.mult, ALU.subtract).then_inc(lo_ready, 1)

            def step(i, more, tables):
                pairs(i, 1)
                if tables:
                    spread(i + 2)
                biased(i, 0)
                if more:
                    pairs(i + 1, 0)
                if tables:
                    table(i + 2)
                biased(i, 1)

            def biased(e, par):
                for s in range(HS):
                    dve.wait_ge(y_scaled, HS * (2 * e + par) + s + 1)
                    n = HS * par + s
                    w_ = tok_w[:, e, n:n + 1] if isinstance(e, int) else \
                        tok_w[:, bass.ds(e, 1), n:n + 1].rearrange("p o s -> p (o s)")
                    stt(y[:, par, s, :], at(b2s, e), w_, y[:, par, s, :], ALU.mult, ALU.add).then_inc(y_ready, 1)

            dve.wait_ge(b2_ready, 1)
            pairs(0, 0)
            step(0, True, True)
            with dve.Fori(1, E - 2) as i:
                step(i, True, True)
            step(E - 2, True, False)
            step(E - 1, False, False)

        @block.tensor
        def _(pe):
            mm = nc.tensor.matmul
            pe.wait_ge(wd_ready, 2)
            for c, (first, n) in enumerate(chunks):
                pe.wait_ge(oh_ready, c + 1)
                for f in range(n):
                    for par in range(2):
                        last = mm(dft_bank[c][64 * par:64 * par + 64, f * 2 * NFP:(f + 1) * 2 * NFP],
                                  onehot[:, first + f, :], wd16[:, par, :], start=True, stop=True)
                last.then_inc(dft_done, 1)
            pe.wait_ge(mag_done, 1)
            pe.wait_ge(ld_pw, 32)
            for b in range(B):
                for j in range(NFP):
                    kk = P if j < NFP - 1 else V
                    last = mm(bank[1][V:V + FR, b * DS:(b + 1) * DS], mag[0:kk, j, b * FR:(b + 1) * FR],
                              pw[0:kk, j, :], start=(j == 0), stop=(j == NFP - 1))
            last.then_inc(enc_done, 1)
            pe.wait_ge(ta_centred, 2)
            for kt in range(2):
                for b in range(B):
                    at_ = (kt * B + b) * KZ
                    last = nc.tensor.transpose(bank[4][:, at_:at_ + KZ], ta[:, b, kt * P:(kt + 1) * P],
                                               ident[0:KZ, 0:KZ])
            last.then_inc(tcT_done, 1)
            pe.wait_ge(tcT_ready, 1)
            for b in range(B):
                for kt in range(2):
                    last = mm(bank[5][0:KZ, b * KZ:(b + 1) * KZ], tcT[:, kt, b, :], tcT[:, kt, b, :],
                              start=(kt == 0), stop=(kt == 1))
            last.then_inc(m_done, 1)
            pe.wait_ge(ld_proj, 16 * 7)
            for w_s, bk, done in ((wq_s, bank[6], q_done), (wk_s, bank[7], k_done)):
                for j in range(2):
                    for kt in range(2):
                        last = mm(bk[:, j * B * KZ:(j + 1) * B * KZ], w_s[:, kt, j * P:(j + 1) * P],
                                  tcT[:, kt, :, :].rearrange("p b z -> p (b z)"), start=(kt == 0), stop=(kt == 1))
                last.then_inc(done, 1)

            def mz(g):
                pe.wait_ge(z_ready, 1)
                pe.wait_ge(ld_zc, 16)
                pe.wait_ge(m_ready, 1)
                if g >= 2:
                    pe.wait_ge(zm_ready, 2 * (g - 1))
                bk = (0, 6)[g % 2]
                for hf in range(2):
                    last = mm(bank[bk + hf][0:KZ, 0:HW], mall[:, g // (NG // B), :],
                              zall[:, g, hf * HW:(hf + 1) * HW], start=True, stop=True)
                last.then_inc(mz_done, 1)

            mz(0)
            for b in range(B):
                for kt in range(2):
                    mm(bank[5][0:KZ, b * H:(b + 1) * H], tcT[:, kt, b, :], wv_s[:, kt, :],
                       start=(kt == 0), stop=False)
                last = mm(bank[5][0:KZ, b * H:(b + 1) * H], con[0:1, C_ROW97:C_ROW97 + KZ], bv_s[0:1, :],
                          start=False, stop=True)
            last.then_inc(v_done, 1)
            pe.wait_ge(qk_ready, 2)
            mz(1)
            for b in range(B):
                for j in range(2):
                    last = mm(bank[4][0:KZ, b * KZ:(b + 1) * KZ], qT[:, j, b, :], kT[:, j, b, :],
                              start=(j == 0), stop=(j == 1))
            last.then_inc(b_done, 1)
            half = NG // 2
            for g in range(NG):
                pe.wait_ge(zm_ready, 2 * (g + 1))
                if g == half:
                    pe.wait_ge(sd_ready, 2)
                for hf in range(2):
                    at_ = C_SUM + (g % half) * half
                    last = mm(bank[2 + hf][0:half, 0:HW], con[0:KZ, at_:at_ + half],
                              (zm, zm_odd)[g % 2][:, hf, :], start=(g % half == 0), stop=(g % half == half - 1))
                last.then_inc(zm_used, 1)
                if g + 2 < NG:
                    mz(g + 2)
                if g == 1:
                    pe.wait_ge(tb_centred, 2)
                    for kt in range(2):
                        for b in range(B):
                            at_ = (kt * B + b) * KZ
                            last = nc.tensor.transpose(bank[5][:, at_:at_ + KZ], tb[:, b, kt * P:(kt + 1) * P],
                                                       ident[0:KZ, 0:KZ])
                    last.then_inc(tvT_done, 1)
            pe.wait_ge(tvT_ready, 1)
            pe.wait_ge(sd_ready, 4)
            for n, src in enumerate((tcT, tvT)):
                for b in range(B):
                    at_ = (n * B + b) * E
                    for kt in range(2):
                        last = mm(bank[3][0:KZ, at_:at_ + E], src[:, kt, b, :], wr_s[:, kt, :],
                                  start=(kt == 0), stop=(kt == 1))
            last.then_inc(lr_done, 1)

            def table_times_u(g):
                pe.wait_ge(u_ready, 2 * (g + 1))
                wait(pe, g_ready, g)
                mm(bank[4][0:KZ, :], bcur, u[:, WCTX:WCTX + GRP], start=True, stop=True).then_inc(g_done, 1)

            def scores(g):
                pe.wait_ge(g_ready, g + 1)
                wait(pe, masked, 2 * g)
                for t in range(TPG):
                    last = mm(bank_s[t // 2][:, (t % 2) * KEYS:(t % 2 + 1) * KEYS], gT[:, t * P:(t + 1) * P],
                              u[:, t * P:t * P + KEYS], start=True, stop=True)
                last.then_inc(s_done, 1)
                wait(pe, ut_ready, 2 * g)
                for t in range(TPG):
                    nc.tensor.transpose(bank[5][:, t * KZ:(t + 1) * KZ], u[:, t * P:(t + 1) * P],
                                        ident[0:KZ, 0:KZ])
                nc.tensor.transpose(bank[5][0:2 * WCTX, TPG * KZ:(TPG + 1) * KZ], u[:, GRP:WIN],
                                    ident[0:KZ, 0:KZ]).then_inc(ut_done, 1)

            def turn_probs(g):
                pe.wait_ge(probs_ready, g + 1)
                if isinstance(g, int) and g == 0:
                    pe.wait_ge(tabs_ready, 2)
                wait(pe, prT_ready, 2 * g)
                wait(pe, hc_ready, TPG * g)
                for t in range(TPG):
                    nc.tensor.transpose(bank[3][:, t * P:(t + 1) * P], pr[:, t, 0:P], ident)
                    last = nc.tensor.transpose(bank[7][0:2 * WCTX, EXTRA + t * 32:EXTRA + (t + 1) * 32],
                                               pr[P - 32:P, t, P:KEYS], ident[P - 32:P, P - 32:P])
                last.then_inc(pt_done, 1)

            def mix(g):
                pe.wait_ge(prT_ready, 2 * (g + 1))
                pe.wait_ge(ut_ready, 2 * (g + 1))
                wait(pe, mix_ready, g)
                for t in range(TPG):
                    mm(bank[2][0:KZ, t * P:(t + 1) * P], ut[:, t, :], prT[:, t * P:(t + 1) * P],
                       start=True, stop=False)
                    last = mm(bank[2][0:KZ, (t + 1) * P - 32:(t + 1) * P], ut[0:2 * WCTX, t + 1, :],
                              prE[:, t, :], start=False, stop=True)
                last.then_inc(mix_done, 1)

            def residual(g):
                pe.wait_ge(mix_ready, g + 1)
                pe.wait_ge(zq_ready, g + 1)
                ta_b, tb_b = at(ta, g // (NG // B)), at(tb, g // (NG // B))
                for t in range(TPG):
                    wait(pe, hc_ready, TPG * g + t - 1)
                    mm(bank[6 + t % 2][:, 0:OW], zq[:, t * P:(t + 1) * P], ta_b, start=True, stop=False)
                    mm(bank[6 + t % 2][:, 0:OW], yT[:, t * P:(t + 1) * P], tb_b, start=False,
                       stop=True).then_inc(o_done, 1)

            def attend(g):
                num = isinstance(g, int)
                more, more2 = not num or g + 1 < NG, not num or g + 2 < NG
                mix(g)
                if more:
                    scores(g + 1)
                residual(g)
                if more:
                    turn_probs(g + 1)
                if more2:
                    table_times_u(g + 2)

            table_times_u(0)
            scores(0)
            turn_probs(0)
            table_times_u(1)
            for g in range(PEEL):
                attend(g)
            with pe.Fori(PEEL, NG - 2) as g:
                attend(g)
            attend(NG - 2)
            attend(NG - 1)

            pe.wait_ge(counts_ready, 1)
            pe.wait_ge(misc_ready, 6)
            cb = count_b.rearrange("p e t -> p (e t)")
            mm(bank[0][:, 0:E * NT], ones_b[:, :], cb, start=True, stop=True)
            mm(bank[0][:, E * NT:2 * E * NT], tri_b[:, :], cb, start=True, stop=True).then_inc(ranks_done, 1)

            def table(e):
                wait(pe, tab_copied, e)
                for t in range(NT):
                    if t % TC == 0:
                        pe.wait_ge(rhs_ready, (NT // TC + 1) * e + 2 + t // TC)
                    last = mm(bank[6][:, 0:NV * ST], oh_lo[:, :, t],
                              rhs_t.rearrange("p v s t -> p (v s) t")[:, :, t], start=(t == 0), stop=(t == NT - 1))
                last.then_inc(tab_done, 1)

            pe.wait_ge(vals_ready, 3)
            table(0)
            table(1)

            def rows_T(k, par, tiles=range(HS)):
                for s in tiles:
                    pe.wait_ge(gathered[par][s], 16 * (k // 2 + 1))
                    wait(pe, xt_ready, HS * k + s - 1)
                    tx = bank[(HS * par + s) % 2][:, 0:256].bitcast(F16)
                    for c in range(4):
                        last = nc.tensor.transpose(tx[:, c * P:(c + 1) * P], xg[:, par, s, c * P:(c + 1) * P],
                                                   ident16[:, :])
                    last.then_inc(xt_done, 1)

            def w_cols(w_s, part, e, kt, c0, n):
                if isinstance(e, int):
                    return w_s[:, part, e, kt, c0:c0 + n]
                return w_s[:, part, bass.ds(e, 1), kt, c0:c0 + n].rearrange("p o c -> p (o c)")

            def layer1(e, par):
                k = 2 * e + par
                pe.wait_ge(xt_ready, HS * (k + 1))
                for f in range(FT):
                    for c in range(2):
                        wait(pe, gelu_done, 8 * k + 2 * f + c - 1)
                        for kt in range(2):
                            for wp, xp in ((0, 0), (0, 1), (1, 0)):
                                last = mm(bank[2 + c][:, 0:CH], w_cols(w1s, wp, e, kt, f * P, P),
                                          xT[:, par, 2 * xp + kt, c * CH:(c + 1) * CH],
                                          start=(kt == 0 and wp == 0 and xp == 0), stop=(kt == 1 and wp == 1))
                        last.then_inc(l1_done, 1)

            def layer2(e, par, more):
                k = 2 * e + par
                pe.wait_ge(lo_ready, 8 * (k + 1))
                for s in range(HS):
                    if more:
                        rows_T(k + 2, par, (s,))
                    bk = bank[4 + (HS * par + s) % 2][:, 0:H]
                    wait(pe, y_scaled, HS * k + s - 1)
                    for f in range(FT):
                        for hp, wp in ((0, 0), (0, 1), (1, 0)):
                            last = mm(bk, hT[:, par, hp, f, s * P:(s + 1) * P], w_cols(w2s, wp, e, f, 0, H),
                                      start=(f == 0 and hp == 0 and wp == 0), stop=(f == FT - 1 and hp == 1))
                    last.then_inc(y_done, 1)

            pe.wait_ge(stage_free, 2 * E)
            pe.wait_ge(misc_ready, 6)
            rows_T(0, 0)
            layer1(0, 0)
            rows_T(1, 1)

            def step(i, more, tables):
                layer1(i, 1)
                layer2(i, 0, more)
                if more:
                    layer1(i + 1, 0)
                if tables:
                    table(i + 2)
                layer2(i, 1, more)

            step(0, True, True)
            with pe.Fori(1, E - 2) as i:
                step(i, True, True)
            step(E - 2, True, False)
            step(E - 1, False, False)


def constants():
    con = np.zeros((P, NCONST), np.float32)
    n = np.arange(V)
    dft = np.zeros((V, 2, 2, NFP), np.float64)
    for par in range(2):
        for j in range(NFP):
            f = 2 * j + par
            if f < NF:
                turn = (f * n) % V
                dft[:, par, 0, j] = np.cos(2 * np.pi * turn / V)
                dft[:, par, 1, j] = np.where(turn % (V // 2) == 0, 0.0, -np.sin(2 * np.pi * turn / V))
                dft[:, par, 0, j] = np.where(turn % (V // 2) == V // 4, 0.0, dft[:, par, 0, j])
    con[:, C_DFT:C_DFT + 4 * NFP] = np.tile(dft.reshape(V, -1), (2, 1))
    con[:, C_IOTA:C_IOTA + P] = np.arange(P)
    con[:, C_PART] = np.arange(P)
    con[:, C_ID:C_ID + P] = np.eye(P)
    con[:, C_TRI:C_TRI + P] = np.triu(np.ones((P, P)), 1) - 1.0
    for g in range(NG // 2):
        con[:, C_SUM + g * (NG // 2) + g] = 1.0
    con[0, C_ROW97 + KZ - 1] = 1.0
    con[:, C_TILE:C_TILE + NT] = np.arange(NT)
    con[:, C_TOK:C_TOK + NT] = (np.arange(NT) * P + np.arange(P)[:, None]) / 2
    con[:, C_RESET:C_RESET + E * NT] = np.arange(E * NT) % NT > 0
    con[:, C_PREF:C_PREF + E] = E - np.arange(E)

    t = np.arange(L)
    coord = np.clip((t + 0.5) * (FR / L) - 0.5, 0.0, FR - 1.0)
    i0 = np.floor(coord).astype(np.int64)
    i1 = np.minimum(i0 + 1, FR - 1)
    w = (coord - i0).astype(np.float32)
    z = np.zeros((FR, L), np.float32)
    np.add.at(z, (i0, t), np.float32(1.0) - w)
    np.add.at(z, (i1, t), w)
    frames_of = np.zeros((FR + 1, NG, WIN), np.float32)
    frames_of[FR] = 1.0
    masks = np.full((P, NG // B, TPG, KEYS), -1e30, np.float32)
    for g in range(NG):
        first = (g % (NG // B)) * GRP - WCTX
        for c in range(WIN):
            if 0 <= first + c < L:
                frames_of[:FR, g, c] = z[:, first + c]
    for g in range(NG // B):
        for tile in range(TPG):
            for q in range(P):
                for k in range(q, q + 2 * WCTX + 1):
                    if 0 <= g * GRP + tile * P + k - WCTX < L:
                        masks[q, g, tile, k] = 0.0
    return con, frames_of, masks


def kernel(**inputs):
    import concourse.bacc as bacc
    from concourse.bass_utils import run_bass_kernel_spmd

    a = {k: np.asarray(v) for k, v in inputs.items()}
    x = a["x"].astype(np.int32, copy=False)
    half = V // 2
    padded = np.pad(x, ((0, 0), (half, half)), mode="reflect")
    ids_frames = np.ascontiguousarray(
        np.stack([padded[:, f * V:f * V + V] for f in range(FR)], 1).reshape(B * FR, V).T)
    flat = np.pad(x.reshape(-1), (WCTX, WCTX), mode="edge")
    ids_win = np.stack([flat[g * GRP:g * GRP + WIN] for g in range(NG)])
    pw = np.pad(a["L0_tok_proj_w"].reshape(DS, NF, V), ((0, 0), (0, 2 * NFP - NF), (0, 0)))
    pw = np.ascontiguousarray(pw.reshape(DS, NFP, 2, V).transpose(2, 3, 1, 0).reshape(P, NFP, DS))
    bqk = np.ascontiguousarray(np.stack([a["L0_attn_bq"].reshape(2, P), a["L0_attn_bk"].reshape(2, P)]
                                        ).transpose(2, 0, 1))
    b1 = np.ascontiguousarray(a["L0_ffn_b1"].reshape(E, FT, P).transpose(2, 0, 1))
    con, frames_of, masks = constants()
    arrays = {
        "ids_frames": ids_frames, "ids_win": ids_win, "window": a["L0_tok_window"].reshape(V, 1),
        "emb": a["L0_tok_emb_table"], "proj_w": pw, "proj_b": a["L0_tok_proj_b"],
        "wq": a["L0_attn_Wq"], "wk": a["L0_attn_Wk"], "wv": a["L0_attn_Wv"], "bqk": bqk,
        "bv": a["L0_attn_bv"].reshape(1, H), "wr": a["L0_ffn_router_w"], "br": a["L0_ffn_router_b"],
        "w1": a["L0_ffn_w1"], "b1": b1, "w2": a["L0_ffn_w2"], "b2": a["L0_ffn_b2"],
        "consts": con, "frames_of": frames_of, "masks": masks,
    }
    nc = bacc.Bacc("TRN2", target_bir_lowering=False, num_devices=1)
    aps = [nc.dram_tensor(name, v.shape, mybir.dt.from_np(v.dtype), kind="ExternalInput").ap()
           for name, v in arrays.items()]
    out = nc.dram_tensor("out", (NT, P, H), F32, kind="ExternalOutput").ap()
    build(nc, *aps, out)
    result = run_bass_kernel_spmd(nc, [arrays], core_ids=[0])
    return result.results[0]["out"].reshape(B, L, H)
```
